# Optimizing a Trainium2 kernel written in Bass

```python
import numpy as np
import jax
import jax.numpy as jnp

def _softmax(x, axis=-1):
    return jax.nn.softmax(x, axis=axis)

def _gelu(x):
    return jax.nn.gelu(x, approximate=True)

def _silu(x):
    return jax.nn.silu(x)

def _sigmoid(x):
    return jax.nn.sigmoid(x)

def _layernorm(x, axis=-1, eps=1e-05):
    m = jnp.mean(x, axis=axis, keepdims=True)
    v = jnp.var(x, axis=axis, keepdims=True)
    return (x - m) / jnp.sqrt(v + eps)

def _scatter_add(tgt, idx, src, axis=0):
    return tgt.at[idx].add(src)

def _segment_sum(src, seg, n):
    return jax.ops.segment_sum(src, seg, n)
kernel_name = 'mk_flamingo_gated_d4_seqx_r8_790f2f'

def setup_inputs(seed: int=0):
    np.random.seed(seed)
    _w = jnp.asarray

    def _rec_inputs():
        import jax
        import jax.numpy as jnp
        _rk = jax.random.key(seed)
        x = 7.22e-05 + 1 * jax.random.normal(jax.random.fold_in(_rk, 1), (16, 128, 128), jnp.float32)
        _lenS = 128 - jax.random.randint(jax.random.fold_in(_rk, 7), (16,), 0, max(1, 128 // 4) + 1, jnp.int32)
        _lenS2 = 77 - jax.random.randint(jax.random.fold_in(_rk, 8), (16,), 0, max(1, 77 // 4) + 1, jnp.int32)
        _ctx_1024P = jax.random.normal(jax.random.fold_in(_rk, 11), (16, 16, 128), jnp.float32)
        _ctx_1024c = jax.random.dirichlet(jax.random.fold_in(_rk, 511), 0.3 * jnp.ones((16,), jnp.float32), (16, 77))
        _ctx_1024t = jnp.einsum('bsk,bkd->bsd', _ctx_1024c, _ctx_1024P)
        _ctx_1024t = _ctx_1024t * jax.lax.rsqrt(jnp.mean(jnp.square(_ctx_1024t)) + 1e-12) * 0.953939
        ctx_1024 = 4.13588e-05 + 0.999923 * (_ctx_1024t + 0.3 * jax.random.normal(jax.random.fold_in(_rk, 611), (16, 77, 128), jnp.float32))
        _validS = jnp.arange(128)[None, :] < _lenS[:, None]
        _validS2 = jnp.arange(77)[None, :] < _lenS2[:, None]
        _causal = jnp.tril(jnp.ones((128, 128), dtype=bool))
        mask_BxSxS2_bk1 = jnp.broadcast_to(_validS2[:, None, :], (16, 128, 77))
        _g = jax.random.normal(jax.random.fold_in(_rk, 9001), (2, 4), jnp.float32)
        _g = jnp.sign(_g) * jnp.maximum(jnp.abs(_g), 1.0) + (_g == 0) * 1.0
        g_xattn = _g[0]
        g_ffn = _g[1]
        return (x, ctx_1024, mask_BxSxS2_bk1, g_xattn, g_ffn)
    x, ctx_1024, mask_BxSxS2_bk1, g_xattn, g_ffn = _rec_inputs()

    def _L0_xattn_setup():
        import jax, jax.numpy as jnp
        import numpy as np
        HIDDEN = 128
        NUM_HEADS = 16
        DK = 64
        DV = 64
        NEG_INF = -1000000000.0
        key = jax.random.key(seed)
        ks = jax.random.split(key, 12)
        B, S = (4, 256)
        scale = 0.02
        return {'q_hidden_inputs': jax.random.normal(ks[0], (B, S, HIDDEN), dtype=jnp.float32), 'k_hidden_inputs': jax.random.normal(ks[1], (B, S, HIDDEN), dtype=jnp.float32), 'v_hidden_inputs': jax.random.normal(ks[2], (B, S, HIDDEN), dtype=jnp.float32), 'mask': jax.random.randint(ks[3], (B, S, S), 0, 2) > 0, 'wq': jax.random.normal(ks[4], (NUM_HEADS, HIDDEN, DK), dtype=jnp.float32) * scale, 'bq': jax.random.normal(ks[5], (NUM_HEADS, DK), dtype=jnp.float32) * scale, 'wk': jax.random.normal(ks[6], (NUM_HEADS, HIDDEN, DK), dtype=jnp.float32) * scale, 'bk': jax.random.normal(ks[7], (NUM_HEADS, DK), dtype=jnp.float32) * scale, 'wv': jax.random.normal(ks[8], (NUM_HEADS, HIDDEN, DV), dtype=jnp.float32) * scale, 'bv': jax.random.normal(ks[9], (NUM_HEADS, DV), dtype=jnp.float32) * scale, 'wo': jax.random.normal(ks[10], (NUM_HEADS * DV, HIDDEN), dtype=jnp.float32) * scale, 'bo': jax.random.normal(ks[11], (HIDDEN,), dtype=jnp.float32) * scale}
    _L0_xattn_all = _L0_xattn_setup()
    _L0_xattn_in = {k: v for k, v in _L0_xattn_all.items() if k in ('wq', 'bq', 'wk', 'bk', 'wv', 'bv', 'wo', 'bo')}
    del _L0_xattn_all

    def _L0_ffn_setup():
        import jax, jax.numpy as jnp
        import numpy as np
        key = jax.random.key(seed)
        ks = jax.random.split(key, 4)
        B, T, M, E, F = (4, 256, 128, 8, 512)
        hidden_states = jax.random.normal(ks[0], (B, T, M), dtype=jnp.float32)
        wg = jax.random.normal(ks[1], (M, E), dtype=jnp.float32) * (1.0 / np.sqrt(M))
        w1 = jax.random.normal(ks[2], (E, M, F), dtype=jnp.float32) * (1.0 / np.sqrt(M))
        b1 = jnp.zeros((E, F), dtype=jnp.float32)
        w2 = jax.random.normal(ks[3], (E, F, M), dtype=jnp.float32) * (1.0 / np.sqrt(F))
        b2 = jnp.zeros((E, M), dtype=jnp.float32)
        return {'hidden_states': hidden_states, 'wg': wg, 'w1': w1, 'b1': b1, 'w2': w2, 'b2': b2}
    _L0_ffn_all = _L0_ffn_setup()
    _L0_ffn_in = {k: v for k, v in _L0_ffn_all.items() if k in ('wg', 'w1', 'b1', 'w2', 'b2')}
    del _L0_ffn_all

    def _L1_xattn_setup():
        import jax, jax.numpy as jnp
        import numpy as np
        D1, D2, D3 = (128, 128, 128)
        key = jax.random.key(seed)
        k1, k2, kw, kb = jax.random.split(key, 4)
        x1 = jax.random.normal(k1, (8, 256, D1), dtype=jnp.float32)
        x2 = jax.random.normal(k2, (8, 256, D2), dtype=jnp.float32)
        bound = 1.0 / np.sqrt(D1 + D2)
        W = jax.random.uniform(kw, (D3, D1 + D2), minval=-bound, maxval=bound, dtype=jnp.float32)
        b = jax.random.uniform(kb, (D3,), minval=-bound, maxval=bound, dtype=jnp.float32)
        return {'x1': x1, 'x2': x2, 'W': W, 'b': b}
    _L1_xattn_all = _L1_xattn_setup()
    _L1_xattn_in = {k: v for k, v in _L1_xattn_all.items() if k in ('W', 'b')}
    del _L1_xattn_all

    def _L1_ffn_setup():
        import jax, jax.numpy as jnp
        import numpy as np
        QMAX = 127.0

        def _ste_round(v):
            return v + jax.lax.stop_gradient(jnp.round(v) - v)

        def _act_fake_quant(x, clip_factor):
            scale = jax.nn.sigmoid(clip_factor) * jnp.max(jnp.abs(x)) / QMAX
            return jnp.clip(_ste_round(x / scale), -QMAX - 1.0, QMAX) * scale

        def _weight_fake_quant(w):
            scale = jnp.max(jnp.abs(w), axis=1, keepdims=True) / QMAX
            return jnp.clip(_ste_round(w / scale), -QMAX - 1.0, QMAX) * scale
        key = jax.random.key(seed)
        k1, k2, k3, k4 = jax.random.split(key, 4)
        B, S, H, I = (8, 1024, 128, 352)
        return {'x': jax.random.normal(k1, (B, S, H), dtype=jnp.float32), 'clip_x': jnp.full((1,), 4.0, dtype=jnp.float32), 'clip_down': jnp.full((1,), 4.0, dtype=jnp.float32), 'w_gate': jax.random.normal(k2, (I, H), dtype=jnp.float32) * 0.02, 'w_up': jax.random.normal(k3, (I, H), dtype=jnp.float32) * 0.02, 'w_down': jax.random.normal(k4, (H, I), dtype=jnp.float32) * 0.02}
    _L1_ffn_all = _L1_ffn_setup()
    _L1_ffn_in = {k: v for k, v in _L1_ffn_all.items() if k in ('clip_x', 'clip_down', 'w_gate', 'w_up', 'w_down')}
    del _L1_ffn_all

    def _L2_xattn_setup():
        import jax, jax.numpy as jnp
        import numpy as np
        B, LQ, LK = (4, 256, 256)
        DQ, DK, DO = (128, 128, 128)
        key = jax.random.key(seed)
        ks = jax.random.split(key, 9)
        s = 0.02
        return {'query_input': jax.random.normal(ks[0], (B, LQ, DQ), jnp.float32), 'key_input': jax.random.normal(ks[1], (B, LK, DK), jnp.float32), 'value_input': jax.random.normal(ks[2], (B, LK, DK), jnp.float32), 'Wq': jax.random.normal(ks[3], (DQ, DO), jnp.float32) * s, 'bq': jax.random.normal(ks[4], (DO,), jnp.float32) * s, 'Wk': jax.random.normal(ks[5], (DK, DO), jnp.float32) * s, 'bk': jax.random.normal(ks[6], (DO,), jnp.float32) * s, 'Wv': jax.random.normal(ks[7], (DK, DO), jnp.float32) * s, 'bv': jax.random.normal(ks[8], (DO,), jnp.float32) * s}
    _L2_xattn_all = _L2_xattn_setup()
    _L2_xattn_in = {k: v for k, v in _L2_xattn_all.items() if k in ('Wq', 'bq', 'Wk', 'bk', 'Wv', 'bv')}
    del _L2_xattn_all

    def _L2_ffn_setup():
        import jax, jax.numpy as jnp
        import numpy as np
        BEST_K = 2

        def _expert(xf, w1, w3, w2):
            return jax.nn.silu(xf @ w1) * (xf @ w3) @ w2
        key = jax.random.key(seed)
        ks = jax.random.split(key, 9)
        E, S_sh, D, H = (8, 2, 128, 64)
        B, S = (2, 256)
        w = lambda k, shape: jax.random.normal(k, shape, dtype=jnp.float32) * 0.02
        return {'x': jax.random.normal(ks[0], (B, S, D), dtype=jnp.float32), 'router_w': w(ks[1], (D, E)), 'router_b': jnp.zeros((E,), dtype=jnp.float32), 'routed_w1': w(ks[2], (E, D, H)), 'routed_w3': w(ks[3], (E, D, H)), 'routed_w2': w(ks[4], (E, H, D)), 'shared_w1': w(ks[5], (S_sh, D, H)), 'shared_w3': w(ks[6], (S_sh, D, H)), 'shared_w2': w(ks[7], (S_sh, H, D))}
    _L2_ffn_all = _L2_ffn_setup()
    _L2_ffn_in = {k: v for k, v in _L2_ffn_all.items() if k in ('router_w', 'router_b', 'routed_w1', 'routed_w3', 'routed_w2', 'shared_w1', 'shared_w3', 'shared_w2')}
    del _L2_ffn_all

    def _L3_xattn_setup():
        import jax, jax.numpy as jnp
        import numpy as np
        D, H = (128, 16)
        DH = D // H

        def _split_heads(z):
            b, t, _ = z.shape
            return z.reshape(b, t, H, DH).transpose(0, 2, 1, 3)
        key = jax.random.key(seed)
        ks = jax.random.split(key, 11)
        b, t, ta = (2, 256, 1500)
        s = 1.0 / np.sqrt(D)
        return {'x': jax.random.normal(ks[0], (b, t, D), dtype=jnp.float32), 'xa': jax.random.normal(ks[1], (b, ta, D), dtype=jnp.float32), 'Wqkv': jax.random.normal(ks[2], (D, 3 * D), dtype=jnp.float32) * s, 'bqkv': jax.random.normal(ks[3], (3 * D,), dtype=jnp.float32) * 0.01, 'Wqkv_aux': jax.random.normal(ks[4], (D, 3 * D), dtype=jnp.float32) * s, 'bqkv_aux': jax.random.normal(ks[5], (3 * D,), dtype=jnp.float32) * 0.01, 'Wo': jax.random.normal(ks[6], (D, D), dtype=jnp.float32) * s, 'bo': jax.random.normal(ks[7], (D,), dtype=jnp.float32) * 0.01, 'g': jnp.zeros((H,), dtype=jnp.float32)}
    _L3_xattn_all = _L3_xattn_setup()
    _L3_xattn_in = {k: v for k, v in _L3_xattn_all.items() if k in ('Wqkv', 'bqkv', 'Wqkv_aux', 'bqkv_aux', 'Wo', 'bo', 'g')}
    del _L3_xattn_all

    def _L3_ffn_setup():
        import jax, jax.numpy as jnp
        import numpy as np
        DM = 128
        NEXPERTS = 32
        EXPERTSETS = 4
        EXPERTSIZE = 32
        BATCH, SEQ = (4, 256)
        key = jax.random.key(seed)
        k0, k1, k2, k3 = jax.random.split(key, 4)
        scale = 0.02
        x = jax.random.normal(k0, (BATCH, SEQ, DM), jnp.float32)
        controller = jax.random.normal(k1, (DM, NEXPERTS, EXPERTSETS), jnp.float32) * scale
        f1 = jax.random.normal(k2, (DM, NEXPERTS, EXPERTSETS, EXPERTSIZE), jnp.float32) * scale
        bias = jnp.zeros((NEXPERTS, EXPERTSETS, EXPERTSIZE), jnp.float32)
        f2 = jax.random.normal(k3, (NEXPERTS, EXPERTSETS, EXPERTSIZE, DM), jnp.float32) * scale
        return {'x': x, 'controller': controller, 'f1': f1, 'bias': bias, 'f2': f2}
    _L3_ffn_all = _L3_ffn_setup()
    _L3_ffn_in = {k: v for k, v in _L3_ffn_all.items() if k in ('controller', 'f1', 'bias', 'f2')}
    del _L3_ffn_all
    return {'x': x, 'ctx_1024': ctx_1024, 'mask_BxSxS2_bk1': mask_BxSxS2_bk1, 'g_xattn': g_xattn, 'g_ffn': g_ffn, 'L0_xattn_wq': _L0_xattn_in['wq'], 'L0_xattn_bq': _L0_xattn_in['bq'], 'L0_xattn_wk': _L0_xattn_in['wk'], 'L0_xattn_bk': _L0_xattn_in['bk'], 'L0_xattn_wv': _L0_xattn_in['wv'], 'L0_xattn_bv': _L0_xattn_in['bv'], 'L0_xattn_wo': _L0_xattn_in['wo'], 'L0_xattn_bo': _L0_xattn_in['bo'], 'L0_ffn_wg': _L0_ffn_in['wg'], 'L0_ffn_w1': _L0_ffn_in['w1'], 'L0_ffn_b1': _L0_ffn_in['b1'], 'L0_ffn_w2': _L0_ffn_in['w2'], 'L0_ffn_b2': _L0_ffn_in['b2'], 'L1_xattn_W': _L1_xattn_in['W'], 'L1_xattn_b': _L1_xattn_in['b'], 'L1_ffn_clip_x': _L1_ffn_in['clip_x'], 'L1_ffn_clip_down': _L1_ffn_in['clip_down'], 'L1_ffn_w_gate': _L1_ffn_in['w_gate'], 'L1_ffn_w_up': _L1_ffn_in['w_up'], 'L1_ffn_w_down': _L1_ffn_in['w_down'], 'L2_xattn_Wq': _L2_xattn_in['Wq'], 'L2_xattn_bq': _L2_xattn_in['bq'], 'L2_xattn_Wk': _L2_xattn_in['Wk'], 'L2_xattn_bk': _L2_xattn_in['bk'], 'L2_xattn_Wv': _L2_xattn_in['Wv'], 'L2_xattn_bv': _L2_xattn_in['bv'], 'L2_ffn_router_w': _L2_ffn_in['router_w'], 'L2_ffn_router_b': _L2_ffn_in['router_b'], 'L2_ffn_routed_w1': _L2_ffn_in['routed_w1'], 'L2_ffn_routed_w3': _L2_ffn_in['routed_w3'], 'L2_ffn_routed_w2': _L2_ffn_in['routed_w2'], 'L2_ffn_shared_w1': _L2_ffn_in['shared_w1'], 'L2_ffn_shared_w3': _L2_ffn_in['shared_w3'], 'L2_ffn_shared_w2': _L2_ffn_in['shared_w2'], 'L3_xattn_Wqkv': _L3_xattn_in['Wqkv'], 'L3_xattn_bqkv': _L3_xattn_in['bqkv'], 'L3_xattn_Wqkv_aux': _L3_xattn_in['Wqkv_aux'], 'L3_xattn_bqkv_aux': _L3_xattn_in['bqkv_aux'], 'L3_xattn_Wo': _L3_xattn_in['Wo'], 'L3_xattn_bo': _L3_xattn_in['bo'], 'L3_xattn_g': _L3_xattn_in['g'], 'L3_ffn_controller': _L3_ffn_in['controller'], 'L3_ffn_f1': _L3_ffn_in['f1'], 'L3_ffn_bias': _L3_ffn_in['bias'], 'L3_ffn_f2': _L3_ffn_in['f2']}

def reference(x, ctx_1024, mask_BxSxS2_bk1, g_xattn, g_ffn, L0_xattn_wq, L0_xattn_bq, L0_xattn_wk, L0_xattn_bk, L0_xattn_wv, L0_xattn_bv, L0_xattn_wo, L0_xattn_bo, L0_ffn_wg, L0_ffn_w1, L0_ffn_b1, L0_ffn_w2, L0_ffn_b2, L1_xattn_W, L1_xattn_b, L1_ffn_clip_x, L1_ffn_clip_down, L1_ffn_w_gate, L1_ffn_w_up, L1_ffn_w_down, L2_xattn_Wq, L2_xattn_bq, L2_xattn_Wk, L2_xattn_bk, L2_xattn_Wv, L2_xattn_bv, L2_ffn_router_w, L2_ffn_router_b, L2_ffn_routed_w1, L2_ffn_routed_w3, L2_ffn_routed_w2, L2_ffn_shared_w1, L2_ffn_shared_w3, L2_ffn_shared_w2, L3_xattn_Wqkv, L3_xattn_bqkv, L3_xattn_Wqkv_aux, L3_xattn_bqkv_aux, L3_xattn_Wo, L3_xattn_bo, L3_xattn_g, L3_ffn_controller, L3_ffn_f1, L3_ffn_bias, L3_ffn_f2):
    import jax
    import jax.numpy as jnp

    def _L0_xattn_ref(q_hidden_inputs, k_hidden_inputs, v_hidden_inputs, mask, wq, bq, wk, bk, wv, bv, wo, bo):
        import jax, jax.numpy as jnp
        import numpy as np
        HIDDEN = 128
        NUM_HEADS = 16
        DK = 64
        DV = 64
        NEG_INF = -1000000000.0
        q = jnp.einsum('bsd,hdk->bhsk', q_hidden_inputs, wq) + bq[None, :, None, :]
        k = jnp.einsum('bsd,hdk->bhsk', k_hidden_inputs, wk) + bk[None, :, None, :]
        v = jnp.einsum('bsd,hdv->bhsv', v_hidden_inputs, wv) + bv[None, :, None, :]
        scores = jnp.einsum('bhsk,bhtk->bhst', q, k) / jnp.sqrt(jnp.float32(DK))
        scores = jnp.where(mask[:, None, :, :], scores, NEG_INF)
        attn = jax.nn.softmax(scores, axis=-1)
        out = jnp.einsum('bhst,bhtv->bhsv', attn, v)
        B, H, Sq, Dv = out.shape
        out = jnp.transpose(out, (0, 2, 1, 3)).reshape(B, Sq, H * Dv)
        return out @ wo + bo

    def _L0_ffn_ref(hidden_states, wg, w1, b1, w2, b2):
        import jax, jax.numpy as jnp
        import numpy as np
        B, T, M = hidden_states.shape
        E = wg.shape[1]
        S = B * T
        MIN_CAPACITY = 4
        C = max((S + E - 1) // E, MIN_CAPACITY)
        x = hidden_states.reshape(S, M)
        logits = x @ wg
        gates = jax.nn.softmax(logits, axis=-1)
        idx = jnp.argmax(gates, axis=-1)
        mask1 = jax.nn.one_hot(idx, E, dtype=gates.dtype)
        l_aux = jnp.sum(gates.mean(0) * mask1.mean(0)) * E
        locations1 = jnp.cumsum(mask1, axis=0) - 1.0
        mask1 = mask1 * (locations1 < C)
        gates1_s = jnp.sum(gates * mask1, axis=1)
        loc_s = jnp.sum(locations1 * mask1, axis=1).astype(jnp.int32)
        loc_sc = jax.nn.one_hot(loc_s, C, dtype=gates.dtype)
        combine_weights = jnp.einsum('se,sc->sec', gates1_s[:, None] * mask1, loc_sc)
        dispatch_mask = (combine_weights > 0).astype(x.dtype)
        dispatched = jnp.einsum('sec,sm->ecm', dispatch_mask, x)
        h = jax.nn.gelu(jnp.einsum('ecm,emf->ecf', dispatched, w1) + b1[:, None, :])
        expert_out = jnp.einsum('ecf,efm->ecm', h, w2) + b2[:, None, :]
        out = jnp.einsum('sec,ecm->sm', combine_weights, expert_out)
        return out.reshape(B, T, M)

    def _L1_xattn_ref(x1, x2, W, b):
        import jax, jax.numpy as jnp
        import numpy as np
        D1, D2, D3 = (128, 128, 128)
        d1 = x1.shape[-1]
        W1 = W[:, :d1]
        W2 = W[:, d1:]
        part1 = jnp.einsum('bld,ed->ble', x1, W1)
        part2 = jnp.einsum('bld,ed->be', x2, W2) / x2.shape[1]
        return part1 + part2[:, None, :] + b

    def _L1_ffn_ref(x, clip_x, clip_down, w_gate, w_up, w_down):
        import jax, jax.numpy as jnp
        import numpy as np
        QMAX = 127.0

        def _ste_round(v):
            return v + jax.lax.stop_gradient(jnp.round(v) - v)

        def _act_fake_quant(x, clip_factor):
            scale = jax.nn.sigmoid(clip_factor) * jnp.max(jnp.abs(x)) / QMAX
            return jnp.clip(_ste_round(x / scale), -QMAX - 1.0, QMAX) * scale

        def _weight_fake_quant(w):
            scale = jnp.max(jnp.abs(w), axis=1, keepdims=True) / QMAX
            return jnp.clip(_ste_round(w / scale), -QMAX - 1.0, QMAX) * scale
        xq = _act_fake_quant(x, clip_x[0])
        gate = jnp.einsum('bsh,ih->bsi', xq, _weight_fake_quant(w_gate))
        up = jnp.einsum('bsh,ih->bsi', xq, _weight_fake_quant(w_up))
        h = _act_fake_quant(jax.nn.silu(gate) * up, clip_down[0])
        return jnp.einsum('bsi,hi->bsh', h, _weight_fake_quant(w_down))

    def _L2_xattn_ref(query_input, key_input, value_input, Wq, bq, Wk, bk, Wv, bv):
        import jax, jax.numpy as jnp
        import numpy as np
        B, LQ, LK = (4, 256, 256)
        DQ, DK, DO = (128, 128, 128)
        scale = jnp.asarray(DO, query_input.dtype) ** 0.5
        q = query_input @ Wq + bq
        k = key_input @ Wk + bk
        v = value_input @ Wv + bv
        attn = jnp.einsum('bqd,bkd->bqk', q, k) / scale
        attn = jax.nn.softmax(attn, axis=-1)
        return jnp.einsum('bqk,bkd->bqd', attn, v)

    def _L2_ffn_ref(x, router_w, router_b, routed_w1, routed_w3, routed_w2, shared_w1, shared_w3, shared_w2):
        import jax, jax.numpy as jnp
        import numpy as np
        BEST_K = 2

        def _expert(xf, w1, w3, w2):
            return jax.nn.silu(xf @ w1) * (xf @ w3) @ w2
        B, S, D = x.shape
        T = B * S
        xf = x.reshape(T, D)
        logits = xf @ router_w + router_b
        topk_vals, topk_idx = jax.lax.top_k(logits, BEST_K)
        sparse = jnp.full_like(logits, -jnp.inf)
        sparse = sparse.at[jnp.arange(T)[:, None], topk_idx].set(topk_vals)
        gates = jax.nn.softmax(sparse, axis=-1)
        routed = jax.vmap(_expert, in_axes=(None, 0, 0, 0))(xf, routed_w1, routed_w3, routed_w2)
        routed_out = jnp.einsum('etd,te->td', routed, gates)
        shared_out = jax.vmap(_expert, in_axes=(None, 0, 0, 0))(xf, shared_w1, shared_w3, shared_w2).sum(axis=0)
        return (routed_out + shared_out).reshape(B, S, D)

    def _L3_xattn_ref(x, xa, Wqkv, bqkv, Wqkv_aux, bqkv_aux, Wo, bo, g):
        import jax, jax.numpy as jnp
        import numpy as np
        D, H = (128, 16)
        DH = D // H

        def _split_heads(z):
            b, t, _ = z.shape
            return z.reshape(b, t, H, DH).transpose(0, 2, 1, 3)
        qkv = x @ Wqkv + bqkv
        qkv_a = xa @ Wqkv_aux + bqkv_aux
        q, k, v = (_split_heads(c) for c in jnp.split(qkv, 3, axis=-1))
        qa, ka, va = (_split_heads(c) for c in jnp.split(qkv_a, 3, axis=-1))
        scale = 1.0 / jnp.sqrt(jnp.float32(DH))
        dots = jnp.einsum('bhqd,bhkd->bhqk', q, k) * scale
        dots_aux = jnp.einsum('bhqd,bhkd->bhqk', q, ka) * scale
        p = jax.nn.softmax(dots, axis=-1)
        pa = jax.nn.softmax(dots_aux, axis=-1)
        h_main = jnp.einsum('bhqk,bhkd->bhqd', p, v)
        h_aux = jnp.einsum('bhqk,bhkd->bhqd', pa, va)
        gate = jax.nn.sigmoid(g).reshape(1, H, 1, 1)
        out = h_main * (1.0 - gate) + h_aux * gate
        b, _, t, _ = out.shape
        out = out.transpose(0, 2, 1, 3).reshape(b, t, H * DH)
        return out @ Wo + bo

    def _L3_ffn_ref(x, controller, f1, bias, f2):
        import jax, jax.numpy as jnp
        import numpy as np
        DM = 128
        NEXPERTS = 32
        EXPERTSETS = 4
        EXPERTSIZE = 32
        BATCH, SEQ = (4, 256)
        B, L, d = x.shape
        t = controller.shape[1]
        g = L // t
        grouped = x.reshape(B, g, t, d)
        logits = jnp.einsum('bgtd,des->bgtes', grouped, controller)
        tie = jnp.linspace(0.0, 1e-06, t, dtype=logits.dtype).reshape(t, 1, 1)
        logits = logits + tie
        perm = (logits == jnp.max(logits, axis=-3, keepdims=True)).astype(x.dtype)
        perm = jax.lax.stop_gradient(perm)
        dispatched = jnp.einsum('bgtd,bgtes->bgesd', grouped, perm)
        inner = jax.nn.relu(jnp.einsum('bgesd,desf->bgesf', dispatched, f1) + bias)
        intermediate = jnp.einsum('bgesf,esfd->bgesd', inner, f2)
        out = jnp.einsum('bgesd,bgtes->bgtd', intermediate, perm)
        return out.reshape(B, L, d)
    x = x + jnp.tanh(g_xattn[0]) * _L0_xattn_ref(_layernorm(x, axis=-1), ctx_1024, ctx_1024, mask_BxSxS2_bk1, L0_xattn_wq, L0_xattn_bq, L0_xattn_wk, L0_xattn_bk, L0_xattn_wv, L0_xattn_bv, L0_xattn_wo, L0_xattn_bo)
    x = x + jnp.tanh(g_ffn[0]) * _L0_ffn_ref(_layernorm(x, axis=-1), L0_ffn_wg, L0_ffn_w1, L0_ffn_b1, L0_ffn_w2, L0_ffn_b2)
    x = x + jnp.tanh(g_xattn[1]) * _L1_xattn_ref(_layernorm(x, axis=-1), ctx_1024, L1_xattn_W, L1_xattn_b)
    x = x + jnp.tanh(g_ffn[1]) * _L1_ffn_ref(_layernorm(x, axis=-1), L1_ffn_clip_x, L1_ffn_clip_down, L1_ffn_w_gate, L1_ffn_w_up, L1_ffn_w_down)
    x = x + jnp.tanh(g_xattn[2]) * _L2_xattn_ref(_layernorm(x, axis=-1), ctx_1024, ctx_1024, L2_xattn_Wq, L2_xattn_bq, L2_xattn_Wk, L2_xattn_bk, L2_xattn_Wv, L2_xattn_bv)
    x = x + jnp.tanh(g_ffn[2]) * _L2_ffn_ref(_layernorm(x, axis=-1), L2_ffn_router_w, L2_ffn_router_b, L2_ffn_routed_w1, L2_ffn_routed_w3, L2_ffn_routed_w2, L2_ffn_shared_w1, L2_ffn_shared_w3, L2_ffn_shared_w2)
    x = x + jnp.tanh(g_xattn[3]) * _L3_xattn_ref(_layernorm(x, axis=-1), ctx_1024, L3_xattn_Wqkv, L3_xattn_bqkv, L3_xattn_Wqkv_aux, L3_xattn_bqkv_aux, L3_xattn_Wo, L3_xattn_bo, L3_xattn_g)
    x = x + jnp.tanh(g_ffn[3]) * _L3_ffn_ref(_layernorm(x, axis=-1), L3_ffn_controller, L3_ffn_f1, L3_ffn_bias, L3_ffn_f2)
    return x

_drawn_inputs = setup_inputs


def setup_inputs(seed=0):
    import zlib

    import numpy as np

    out = dict(_drawn_inputs(seed))
    spreads = {'L0_ffn_b1': (0.0, 0.405),
     'L0_ffn_b2': (0.0, 0.283),
     'L2_ffn_router_b': (0.0, 0.8),
     'L3_xattn_g': (0.0, 2.0),
     'L3_ffn_bias': (0.0, 2.0)}
    factors = {'g_ffn': 8.0,
     'L0_xattn_wq': 8.0,
     'L0_xattn_bq': 8.0,
     'L0_xattn_wk': 8.0,
     'L0_xattn_bk': 64.0,
     'L0_xattn_bv': 3.112,
     'L1_ffn_w_gate': 6.301,
     'L1_ffn_w_up': 6.106,
     'L1_ffn_w_down': 6.077,
     'L2_xattn_Wq': 8.0,
     'L2_xattn_bq': 32.6,
     'L2_xattn_Wk': 8.0,
     'L2_xattn_bk': 64.0,
     'L2_xattn_bv': 3.977,
     'L2_ffn_router_w': 8.0,
     'L2_ffn_routed_w1': 8.0,
     'L2_ffn_routed_w3': 8.0,
     'L2_ffn_routed_w2': 8.0,
     'L2_ffn_shared_w1': 8.0,
     'L2_ffn_shared_w3': 8.0,
     'L2_ffn_shared_w2': 8.0,
     'L3_xattn_bqkv': 64.0,
     'L3_xattn_bqkv_aux': 64.0,
     'L3_xattn_bo': 38.545,
     'L3_ffn_controller': 2.742,
     'L3_ffn_f1': 8.0,
     'L3_ffn_f2': 2.683}
    for name, (base, spread) in spreads.items():
        noise = np.random.default_rng([zlib.crc32(name.encode()), seed]).standard_normal(out[name].shape)
        drawn = base * np.exp(spread * noise) if base else spread * noise
        out[name] = jnp.asarray(drawn.astype(out[name].dtype))
    for name, factor in factors.items():
        out[name] = (out[name] * factor).astype(out[name].dtype)
    return out
```

```python
import concourse.bass as bass
import concourse.bacc as bacc
from concourse import mybir
from contextlib import ExitStack

LAST_STAGE = 8

F32 = mybir.dt.float32
BF16 = mybir.dt.bfloat16
U8 = mybir.dt.uint8
I32 = mybir.dt.int32
ALU = mybir.AluOpType
ACT = mybir.ActivationFunctionType
AX = mybir.AxisListType

B, S, D = 16, 128, 128
T = 77
H0, DK0 = 16, 64
E0, F0, C0 = 8, 512, 256
FC0 = F0 // 128
NT = B * S
E2, H2 = 8, 64
H3 = 16
PARTS3 = 48
MAXES3 = PARTS3 + 6
E3, SETS3, F3 = 32, 4, 32
ES3 = E3 * SETS3
G3 = 32
NG3 = B * S // G3
I1 = 352
ROWS1 = [(0, 128), (128, 256), (256, I1)]
QMAX = 127.0
DROW_STEP, XINV_STEP, GUSCALE_STEP, HINV_STEP = 6, 9, 10, 17
MAGIC = 1.5 * 2 ** 23
AREA_A, AREA_B = 15400, 9600
MASKED = -float(2 ** 100)
LN_EPS = 1e-5


def at_least(engine, sem, value):
    if not (isinstance(value, int) and value <= 0):
        engine.wait_ge(sem, value)


def over_tiles(engine, body):
    body(0, 0, 2)
    body(1, 1, 2)
    with engine.Fori(1, B // 2 - 1) as i:
        body(i * 2, 0, 2)
        body(i * 2 + 1, 1, 2)
    body(B - 2, 0, 1)
    body(B - 1, 1, 0)


def build(nc, t):
    ctx = ExitStack()
    with ctx:
        def sb(name, shape, dt=F32):
            return ctx.enter_context(nc.sbuf_tensor(name, shape, dt))

        def sem(name):
            return ctx.enter_context(nc.semaphore(name))

        area = {"A": sb("area_a", [128, AREA_A]), "B": sb("area_b", [128, AREA_B])}

        def carve(which, sizes, p=128, dt=F32):
            at, shape = sizes
            n = 1
            for d in shape:
                n *= d
            words = n if dt == F32 else n // 2
            v = area[which][0:p, at[0]:at[0] + words]
            at[0] += words
            assert at[0] <= (AREA_A if which == "A" else AREA_B), at[0]
            if dt != F32:
                v = v.bitcast(dt)
            names = "abcd"[:len(shape)]
            return v.rearrange(f"p ({' '.join(names)}) -> p {' '.join(names)}", **dict(zip(names, shape))) if len(shape) > 1 else v

        bank = [ctx.enter_context(nc.psum_tensor(f"bank{i}", [128, 512], F32)) for i in range(8)]

        X = sb("X", [128, B, D])
        ident = sb("ident", [128, 128])
        ident_b = sb("ident_b", [128, 128], BF16)
        ones = sb("ones", [128, 128])
        ones_row = ones[0:1, :]
        gates_in = sb("gates_in", [128, 8])
        tg = sb("tg", [128, 8])
        ctxT = sb("ctxT", [128, B, T])
        mask_u8 = sb("mask_u8", [128, B, T], U8)
        mask_bias = sb("mask_bias", [128, B, T], BF16)
        ln_stats = sb("ln_stats", [128, 3, 6])
        ln_mv = sb("ln_mv", [128, 3, 2])
        ln_veps = sb("ln_veps", [128, 3])
        ln_rstd = sb("ln_rstd", [128, 3])
        eps = sb("eps", [128, 1])
        zero = sb("zero", [128, 1])
        scrap = sb("scrap", [128, 6])
        minus_half = sb("minus_half", [128, 1])
        xn = sb("xn", [128, 2, D])
        xnT = sb("xnT", [128, 2, 128])
        ctx_b = sb("ctx_b", [128, 2, T])
        at0, at1, at2, at_moe = [0], [0], [0], [0]
        wq0 = carve("A", (at0, (H0 * DK0,)), 128)
        wk0 = carve("A", (at0, (H0 * DK0,)), 128)
        wv0 = carve("A", (at0, (H0 * DK0,)), 128)
        wo0 = carve("A", (at0, (8, D,)), 128)
        bq0 = sb("bq0", [128, 8])
        bk0 = sb("bk0", [128, 8])
        bv0 = carve("A", (at0, (H0, DK0,)), T)
        bo0 = sb("bo0", [1, D])
        qT = carve("A", (at0, (8, 128,)), 128)
        kT = carve("A", (at0, (H0, T,)), 128)
        v0 = carve("A", (at0, (2, H0, DK0 + 1,)), T)
        e0 = carve("A", (at0, (H0, T,)), 128)
        mx0 = sb("mx0", [128, H0])
        eT0 = carve("A", (at0, (H0, 128,)), T)
        rs0 = sb("rs0", [128, H0])
        o0 = carve("A", (at0, (H0, DK0,)), 128)
        oT0 = carve("A", (at0, (8, 128,)), 128)

        XN = sb("XN", [128, B, D])
        wg0 = sb("wg0", [128, E0])
        r0 = {k: sb(f"r0_{k}", [128, B, E0]) for k in ("exp", "gate", "rank", "keep", "at", "gkeep")}
        r0s = {k: sb(f"r0_{k}", [128, B]) for k in ("max", "sum", "rsum", "gmax", "rmax", "slot", "kept", "gsel", "weight", "alt", "alt2")}
        first0 = sb("first0", [128, B, E0], BF16)
        scatter_at = sb("scatter_at", [128, B], I32)
        gather_at = sb("gather_at", [128, B], I32)
        rank_w = sb("rank_w", [128, E0])
        slot_base = sb("slot_base", [128, E0])
        spare_slot = sb("spare_slot", [128, B])
        tri_b = sb("tri_b", [128, 128], BF16)
        ones_b = sb("ones_b", [128, 128], BF16)
        w1e = carve("B", (at_moe, (2, F0,)), 128)
        w2e = carve("B", (at_moe, (2, FC0, D,)), 128)
        b1e = sb("b1e", [128, 2, FC0])
        b2e = sb("b2e", [1, 2, D])
        xe = carve("B", (at_moe, (2, 2, D,)), 128)
        xeT = carve("B", (at_moe, (2, 2 * 128,)), 128)
        hT0 = carve("B", (at_moe, (2, FC0, 2 * 128,)), 128)
        ye = carve("B", (at_moe, (2, 2, D,)), 128)

        w1x = sb("w1x", [128, D])
        w2x = sb("w2x", [128, D])
        bx = sb("bx", [1, D])
        ctx_mean = sb("ctx_mean", [128, B])
        ctx_sum = sb("ctx_sum", [128, B])
        mix_row = sb("mix_row", [1, B * D])
        absmax1 = sb("absmax1", [128, B])
        clips = sb("clips", [128, 2])
        clip_tanh = sb("clip_tanh", [128, 2])
        clip_sig = sb("clip_sig", [128, 2])
        minus_magic = sb("minus_magic", [128, 1])
        wgu1 = sb("wgu1", [128, 2, 3, D])
        wd1 = sb("wd1", [128, I1])
        wmax1 = sb("wmax1", [128, 7])
        wscale1 = sb("wscale1", [128, 7])
        winv1 = sb("winv1", [128, 7])
        wguT1 = sb("wguT1", [128, 2, I1], BF16)
        wdT1 = sb("wdT1", [128, 3, D], BF16)
        dscale1 = sb("dscale1", [128, D])
        drow1 = sb("drow1", [128, D])
        col1 = {k: sb(f"col1_{k}", [128, 1]) for k in ("xmax", "xscale", "xinv", "hmax", "hscale", "hinv", "out")}
        cell1 = sb("cell1", [1, 2])
        guscale1 = sb("guscale1", [128, 2, 3])
        xq1 = sb("xq1", [128, 4, D])
        xqT1 = sb("xqT1", [128, 2, 512], BF16)
        silu1 = carve("A", (at1, (3, 512,)), 128)
        h1 = carve("A", (at1, (3, NT)), 128)
        hq1 = carve("A", (at1, (3, NT,)), 128, BF16)
        hmax1 = sb("hmax1", [128, 12])
        tmp512 = sb("tmp512", [128, 2, 512])

        g_stats = sb("g_stats", [128, 2, 4, 6])
        g_mv = sb("g_mv", [128, 2, 4, 2])
        g_veps = sb("g_veps", [128, 2, 4])
        g_rstd = sb("g_rstd", [128, 2, 4])
        xn4 = sb("xn4", [128, 2, 4, D])
        xnT4 = sb("xnT4", [128, 2, 512])
        wqkv2 = sb("wqkv2", [128, 3, D])
        bqk2 = sb("bqk2", [128, 2])
        bv2 = sb("bv2", [T, D])
        kT2 = carve("A", (at2, (B, T,)), 128)
        v2 = carve("A", (at2, (B, D,)), T)
        qT2 = carve("A", (at2, (512,)), 128)
        e2 = sb("e2", [128, 4, T])
        eT2 = carve("A", (at2, (512,)), T)
        s2 = {k: sb(f"s2_{k}", [128, 4]) for k in ("max", "sum", "rsum", "out")}
        rw2 = sb("rw2", [128, E2])
        rb2 = sb("rb2", [1, E2])
        at_w2 = [13000]
        w13_2 = carve("A", (at_w2, (2, 5, 128)), 128)
        w2_2 = carve("A", (at_w2, (5, D)), 128)
        pair_sel = sb("pair_sel", [E2, 4, 128])
        r2 = {k: sb(f"r2_{k}", [128, 4, E2]) for k in ("rank", "rank2", "first", "second", "rest", "a", "b", "gate")}
        r2s = {k: sb(f"r2s_{k}", [128, 4]) for k in ("m1", "r1", "m2", "r2", "d", "e", "den", "g1", "g2")}
        gT2 = sb("gT2", [E2, 512])
        th2 = carve("A", (at2, (2, 512,)), 128)
        u2 = carve("A", (at2, (2, 512,)), 128)
        h2 = carve("A", (at2, (5, 512,)), 128)

        at3 = [0]
        em3 = carve("B", (at3, (H3, 128)), 128)
        ea3 = carve("B", (at3, (H3, 128)), T)
        sq3 = carve("B", (at3, (2, H3, 64)), 128, BF16)
        sk3 = carve("B", (at3, (H3, 64)), 128, BF16)
        sa3 = carve("B", (at3, (H3, 64)), T, BF16)
        qT3 = carve("B", (at3, (8, 128)), 128, BF16)
        qmT3 = carve("B", (at3, (8, 128)), 128, BF16)
        kT3 = carve("B", (at3, (8, 128)), 128, BF16)
        kaT3 = carve("B", (at3, (8, T + 1)), 128, BF16)
        wqkv3 = sb("wqkv3", [128, 3 * D])
        wkva3 = sb("wkva3", [128, 2 * D])
        bqkv3 = sb("bqkv3", [128, 3 * D])
        bkva3 = sb("bkva3", [T, 2 * D])
        wo3 = sb("wo3", [128, D])
        bo3 = sb("bo3", [1, D])
        g3 = sb("g3", [128, H3])
        g3_tanh = sb("g3_tanh", [128, H3])
        gate3 = sb("gate3", [128, 2, H3])
        qk3 = sb("qk3", [128, 2, H3, 8])
        ka3 = sb("ka3", [T, H3, 8])
        v3 = sb("v3", [128, 2, H3, 9])
        va3 = sb("va3", [T, 2, H3, 9])
        left3 = [sb(f"left3_{i}", [128, H3, 8]) for i in range(3)]
        mx3 = sb("mx3", [128, 2, H3])
        mleft3 = sb("mleft3", [128, 2, H3])
        rs3 = sb("rs3", [128, 2, H3])
        rg3 = sb("rg3", [128, 2, H3])
        ov3 = sb("ov3", [128, 2, H3, 8])
        o3 = sb("o3", [128, D])
        oT3 = sb("oT3", [128, 128])

        at4, at5 = [0], [0]
        d3 = carve("A", (at4, (NG3, ES3)), 128)
        f1_3 = carve("A", (at4, (ES3, F3)), 128)
        in3 = carve("A", (at4, (E3, NG3)), 128)
        out3 = carve("B", (at5, (NG3, ES3)), 128)
        perm3 = XN[:, :, :].rearrange("p b d -> p (b d)")
        f2_3 = sb("f2_3", [128, E3, D])
        ctrl3 = sb("ctrl3", [128, ES3])
        tie3 = sb("tie3", [128, G3])
        bias3 = sb("bias3", [128, E3])
        gmax3 = sb("gmax3", [128, 16])
        pt3 = carve("B", (at5, (2, 4, ES3)), 128)
        rows3 = carve("A", (at4, (2, 4, D)), 128)

        x_loaded = sem("x_loaded")
        const_loaded = sem("const_loaded")
        ctx_loaded = sem("ctx_loaded")
        mask_loaded = sem("mask_loaded")
        wqkv0_loaded = sem("wqkv0_loaded")
        wo0_loaded = sem("wo0_loaded")
        out_stored = sem("out_stored")
        pool_ready = sem("pool_ready")
        tg_ready = sem("tg_ready")
        stats_done = sem("stats_done")
        var_done = sem("var_done")
        veps_done = sem("veps_done")
        rstd_done = sem("rstd_done")
        xn_done = sem("xn_done")
        xnT_in_psum = sem("xnT_in_psum")
        xnT_done = sem("xnT_done")
        ctx_b_done = sem("ctx_b_done")
        x_updated = sem("x_updated")
        proj_in_psum = sem("proj_in_psum")
        proj_done = sem("proj_done")
        scores_in_psum = sem("scores_in_psum")
        max_done = sem("max_done")
        shifted_done = sem("shifted_done")
        exp_done = sem("exp_done")
        turn_in_psum = sem("turn_in_psum")
        turn_done = sem("turn_done")
        av_in_psum = sem("av_in_psum")
        sums_done = sem("sums_done")
        av_done = sem("av_done")
        wo_in_psum = sem("wo_in_psum")
        route0_loaded = sem("route0_loaded")
        xn_kept = sem("xn_kept")
        logits_in_psum = sem("logits_in_psum")
        route_step = sem("route_step")
        route_exp = sem("route_exp")
        first_done = sem("first_done")
        rank_in_psum = sem("rank_in_psum")
        places_done = sem("places_done")
        slots_zeroed = sem("slots_zeroed")
        zero_ready = sem("zero_ready")
        scattered = sem("scattered")
        expert_loaded = [sem(f"expert_loaded{i}") for i in range(2)]
        xeT_in_psum = sem("xeT_in_psum")
        xeT_done = sem("xeT_done")
        h_in_psum = sem("h_in_psum")
        h_done = sem("h_done")
        y_in_psum = sem("y_in_psum")
        y_done = sem("y_done")
        y_stored = [sem(f"y_stored{i}") for i in range(2)]
        gathered = [sem(f"gathered{i}") for i in range(4)]
        mix_loaded = sem("mix_loaded")
        ctx_mean_done = sem("ctx_mean_done")
        mix_row_in_psum = sem("mix_row_in_psum")
        mix_row_done = sem("mix_row_done")
        mix_in_psum = sem("mix_in_psum")
        absmax_done = sem("absmax_done")
        norm1_done = sem("norm1_done")
        ffn1_loaded = sem("ffn1_loaded")
        quant_step = sem("quant_step")
        clip_tanh_done = sem("clip_tanh_done")
        w_rounded = sem("w_rounded")
        wT_in_psum = sem("wT_in_psum")
        wT_done = sem("wT_done")
        drow_in_psum = sem("drow_in_psum")
        colmax_done = sem("colmax_done")
        maxrow_in_psum = sem("maxrow_in_psum")
        cell_done = sem("cell_done")
        max_in_psum = sem("max_in_psum")
        xq_done = sem("xq_done")
        xqT_in_psum = sem("xqT_in_psum")
        xqT_done = sem("xqT_done")
        gu_in_psum = sem("gu_in_psum")
        silu_done = sem("silu_done")
        h1_done = sem("h1_done")
        hq_rounded = sem("hq_rounded")
        hq_done = sem("hq_done")
        down_in_psum = sem("down_in_psum")
        g_stats_done = sem("g_stats_done")
        moe3_loaded = sem("moe3_loaded")
        f1_loaded = sem("f1_loaded")
        l3_in_psum = sem("l3_in_psum")
        tie3_step = sem("tie3_step")
        perm3_done = sem("perm3_done")
        pt3_in_psum = sem("pt3_in_psum")
        pt3_done = sem("pt3_done")
        d3_in_psum = sem("d3_in_psum")
        d3_act_done = sem("d3_act_done")
        d3_dve_done = sem("d3_dve_done")
        in3_in_psum = sem("in3_in_psum")
        in3_biased = sem("in3_biased")
        in3_done = sem("in3_done")
        f3_in_psum = sem("f3_in_psum")
        out3_act_done = sem("out3_act_done")
        out3_dve_done = sem("out3_dve_done")
        rows3_in_psum = sem("rows3_in_psum")
        rows3_done = sem("rows3_done")
        comb3_in_psum = sem("comb3_in_psum")
        attn3_loaded = sem("attn3_loaded")
        qkv3_in_psum = sem("qkv3_in_psum")
        kva3_in_psum = sem("kva3_in_psum")
        proj3_done = sem("proj3_done")
        split3_step = sem("split3_step")
        split3_done = sem("split3_done")
        stack3_zeroed = sem("stack3_zeroed")
        stack3_ready = sem("stack3_ready")
        t3_in_psum = sem("t3_in_psum")
        t3_done = sem("t3_done")
        s3_in_psum = sem("s3_in_psum")
        max3_done = sem("max3_done")
        maxsplit3_step = sem("maxsplit3_step")
        maxcols3_done = sem("maxcols3_done")
        sT3_in_psum = sem("sT3_in_psum")
        exp3_done = sem("exp3_done")
        av3_in_psum = sem("av3_in_psum")
        o3_step = sem("o3_step")
        o3_done = sem("o3_done")
        wo3_in_psum = sem("wo3_in_psum")
        g3_tanh_done = sem("g3_tanh_done")
        g3_step = sem("g3_step")
        g_var_done = sem("g_var_done")
        g_veps_done = sem("g_veps_done")
        g_rstd_done = sem("g_rstd_done")
        g_xn_done = sem("g_xn_done")
        g_xnT_in_psum = sem("g_xnT_in_psum")
        g_xnT_done = sem("g_xnT_done")
        attn2_loaded = sem("attn2_loaded")
        kv2_in_psum = sem("kv2_in_psum")
        k2_done = sem("k2_done")
        v2_done = sem("v2_done")
        q2_in_psum = sem("q2_in_psum")
        q2_done = sem("q2_done")
        s2_in_psum = sem("s2_in_psum")
        shift2_done = sem("shift2_done")
        exp2_done = sem("exp2_done")
        eT2_in_psum = sem("eT2_in_psum")
        eT2_done = sem("eT2_done")
        av2_in_psum = sem("av2_in_psum")
        a2_step = sem("a2_step")
        moe2_loaded = sem("moe2_loaded")
        logits2_in_psum = sem("logits2_in_psum")
        route2_step = sem("route2_step")
        gap2_done = sem("gap2_done")
        gap2_exp = sem("gap2_exp")
        gates2_done = sem("gates2_done")
        gT2_in_psum = sem("gT2_in_psum")
        gT2_done = sem("gT2_done")
        ab2_in_psum = sem("ab2_in_psum")
        g2_in_psum = sem("g2_in_psum")
        tanh2_done = sem("tanh2_done")
        mul2_step = sem("mul2_step")
        h2_done = sem("h2_done")
        out2_in_psum = sem("out2_in_psum")

        block = ctx.enter_context(nc.Block())

        def slot(b):
            return X[:, bass.ds(b, 1), :].rearrange("p a d -> p (a d)")

        def vector_ln_stats(dve, b, n, u, updates=0):
            if not (isinstance(updates, int) and updates == 0):
                dve.wait_ge(x_updated, updates)
            if not isinstance(updates, int):
                dve.memset(scrap[:, 3 + u:4 + u], 0.0)
            dve.bn_stats(ln_stats[:, u, :], slot(b)).then_inc(stats_done, 1)
            dve.wait_ge(stats_done, n + 1)
            dve.memset(scrap[:, u:u + 1], 0.0)
            dve.bn_aggr(ln_mv[:, u, :], ln_stats[:, u, :]).then_inc(var_done, 1)

        def gpsimd_ln_rstd(pool, n, u):
            pool.wait_ge(var_done, n + 1)
            pool.tensor_tensor(ln_veps[:, u:u + 1], ln_mv[:, u, 1:2], eps[:, :], ALU.add).then_inc(veps_done, 1)
            pool.wait_ge(veps_done, n + 1)
            pool.tensor_tensor(ln_rstd[:, u:u + 1], ln_veps[:, u:u + 1], minus_half[:, :], ALU.pow).then_inc(rstd_done, 1)

        def vector_ln_apply(dve, b, n, u, kept=None, q=None):
            dve.wait_ge(rstd_done, (n if q is None else q) + 1)
            at_least(dve, xnT_in_psum, n - 1)
            if kept is not None:
                at_least(dve, *kept)
            dve.tensor_scalar(xn[:, u, :], slot(b), ln_mv[:, u, 0:1], ln_rstd[:, u:u + 1],
                              ALU.subtract, ALU.mult).then_inc(xn_done, 1)

        def tensor_xnT(pe, n, u, psum):
            pe.wait_ge(xn_done, n + 1)
            at_least(pe, xnT_done, n - 1)
            pe.transpose(psum[:, 0:128], xn[:, u, :], ident[:, :]).then_inc(xnT_in_psum, 1)

        def scalar_xnT(act, n, u, psum):
            act.wait_ge(xnT_in_psum, n + 1)
            act.activation(xnT[:, u, :], psum[:, 0:128], ACT.Copy).then_inc(xnT_done, 1)

        P0 = [bank[0], bank[1]]
        S0 = [bank[2], bank[3], bank[4]]
        T0 = [bank[5], bank[6]]
        HEADS0 = [(0, 6), (6, 12), (12, 16)]
        WO = bank[7][:, 0:128]

        def tensor_attn0(pe):
            def project(b, u):
                for j in range(6):
                    if j == 0:
                        pe.wait_ge(xnT_done, b + 1)
                    if j == 4:
                        pe.wait_ge(ctx_b_done, b + 1)
                    at_least(pe, proj_done, 8 * b + [0, 0, 1, 2, 4, 6][j])
                    dst = P0[j % 2]
                    half = j % 2
                    if j < 4:
                        w, rhs, n = (wq0, xnT[:, u, :], 128) if j < 2 else (wk0, ctxT[:, bass.ds(b, 1), :].rearrange("p a t -> p (a t)"), T)
                        for c in range(4):
                            m = pe.matmul(dst[:, c * n:(c + 1) * n], w[:, (4 * half + c) * 128:(4 * half + c + 1) * 128],
                                          rhs, start=True, stop=True)
                    else:
                        m = pe.matmul(dst[0:T, :], ctx_b[:, u, :], wv0[:, half * 512:(half + 1) * 512], start=True, stop=True)
                    m.then_inc(proj_in_psum, 1)

            def scores(b):
                pe.wait_ge(proj_done, 8 * b + 6)
                for c, (lo, hi) in enumerate(HEADS0):
                    at_least(pe, av_done, 3 * b - 3 + c + 1)
                    n = hi - lo
                    pe.matmul(S0[c][:, 0:n * T], ident_b[:, :],
                              mask_bias[:, bass.ds(b, 1), :].to_broadcast([128, n, T]), start=True, stop=False)
                    for h in range(lo, hi, 2):
                        m = pe.matmul(S0[c][:, (h - lo) * T:(h - lo + 2) * T], qT[:, h // 2, :],
                                      kT[:, h:h + 2, :].rearrange("p a t -> p (a t)"), start=False, stop=(h == hi - 2))
                    m.then_inc(scores_in_psum, 1)

            def attend(b, u, more):
                for j in range(4):
                    pe.wait_ge(exp_done, 3 * b + (4 * j + 3) // 6 + 1)
                    at_least(pe, turn_done, 6 * b + max(j - 1, 0))
                    if j == 1 and more >= 1:
                        pe.wait_ge(xnT_done, b + 2)
                    for h in range(4 * j, 4 * j + 4):
                        m = pe.transpose(T0[(u + j) % 2][0:T, (h % 4) * 128:(h % 4 + 1) * 128], e0[:, h, :], ident[:, :])
                    m.then_inc(turn_in_psum, 1)
                for c, (lo, hi) in enumerate(HEADS0):
                    for h in range(lo, hi):
                        if h % 4 == 0 or h == lo:
                            pe.wait_ge(turn_done, 6 * b + h // 4 + 1)
                        m = pe.matmul(S0[c][:, (h - lo) * 65:(h - lo + 1) * 65], eT0[:, h, :], v0[:, u, h, :], start=True, stop=True)
                    m.then_inc(av_in_psum, 1)
                for j in range(2):
                    pe.wait_ge(av_done, 3 * b + 2 + j)
                    pe.wait_ge(turn_done, 6 * b + 4 + j - 1)
                    for c in range(4 * j, 4 * j + 4):
                        m = pe.transpose(T0[(u + j) % 2][:, (c % 4) * 128:(c % 4 + 1) * 128],
                                         o0[:, 2 * c:2 * c + 2, :].rearrange("p a d -> p (a d)"), ident[:, :])
                    m.then_inc(turn_in_psum, 1)

            def output(b):
                at_least(pe, x_updated, b)
                pe.wait_ge(turn_done, 6 * b + 6)
                for c in range(8):
                    pe.matmul(WO, oT0[:, c, :], wo0[:, c, :], start=(c == 0), stop=False)
                pe.matmul(WO, ones_row[:, :], bo0[:, :], start=False, stop=True).then_inc(wo_in_psum, 1)

            pe.wait_ge(const_loaded, 4 * 16)
            pe.wait_ge(pool_ready, 3)
            pe.wait_ge(ctx_loaded, 16)
            tensor_xnT(pe, 0, 0, T0[0])
            pe.wait_ge(wqkv0_loaded, 6 * 16)
            project(0, 0)
            scores(0)
            tensor_xnT(pe, 1, 1, T0[1])
            pe.wait_ge(wo0_loaded, 2 * 16)

            def body(b, u, more):
                if more >= 1:
                    project(b + 1, 1 - u)
                attend(b, u, more)
                if more >= 1:
                    scores(b + 1)
                output(b)
                if more >= 2:
                    pe.wait_ge(turn_done, 6 * b + 5)
                    tensor_xnT(pe, b + 2, u, T0[u])
            over_tiles(pe, body)

        def vector_attn0(dve):
            def projected(b, u):
                for j in range(6):
                    dve.wait_ge(proj_in_psum, 6 * b + j + 1)
                    half = j % 2
                    c = slice(4 * half, 4 * half + 4)
                    if j < 2:
                        dve.tensor_tensor(qT[:, c, :], P0[half][:, 0:512].rearrange("p (c n) -> p c n", n=128),
                                          bq0[:, c].unsqueeze(2).to_broadcast([128, 4, 128]), ALU.add).then_inc(proj_done, 1)
                    elif j < 4:
                        for r in range(2):
                            p = slice(64 * r, 64 * r + 64)
                            dve.tensor_tensor(kT[p, 8 * half + r:8 * half + 8:2, :],
                                              P0[half][p, 0:4 * T].rearrange("p (c n) -> p c n", n=T),
                                              bk0[p, c].unsqueeze(2).to_broadcast([64, 4, T]), ALU.add).then_inc(proj_done, 1)
                    else:
                        h = slice(8 * half, 8 * half + 8)
                        dve.tensor_tensor(v0[:, u, h, 0:DK0], P0[half][0:T, :].rearrange("p (h d) -> p h d", d=DK0),
                                          bv0[:, h, :], ALU.add).then_inc(proj_done, 1)

            def softmax(b):
                for c, (lo, hi) in enumerate(HEADS0):
                    n = hi - lo
                    sc = S0[c][:, 0:n * T].rearrange("p (h t) -> p h t", t=T)
                    dve.wait_ge(scores_in_psum, 3 * b + c + 1)
                    dve.tensor_reduce(mx0[:, lo:hi], sc, AX.X, ALU.max).then_inc(max_done, 1)
                    dve.wait_ge(max_done, 3 * b + c + 1)
                    dve.tensor_tensor(e0[:, lo:hi, :], sc, mx0[:, lo:hi].unsqueeze(2).to_broadcast([128, n, T]),
                                      ALU.subtract).then_inc(shifted_done, 1)

            def normalise(b):
                for c, (lo, hi) in enumerate(HEADS0):
                    n = hi - lo
                    av = S0[c][:, 0:n * 65].rearrange("p (h d) -> p h d", d=65)
                    dve.wait_ge(av_in_psum, 3 * b + c + 1)
                    dve.reciprocal(rs0[:, lo:hi], av[:, :, 64]).then_inc(sums_done, 1)
                    dve.wait_ge(sums_done, 3 * b + c + 1)
                    dve.tensor_tensor(o0[:, lo:hi, :], av[:, :, 0:64], rs0[:, lo:hi].unsqueeze(2).to_broadcast([128, n, 64]),
                                      ALU.mult).then_inc(av_done, 1)

            def update(b):
                dve.wait_ge(wo_in_psum, b + 1)
                dve.scalar_tensor_tensor(slot(b), WO, tg[:, 0:1], slot(b), ALU.mult, ALU.add).then_inc(x_updated, 1)

            dve.wait_ge(x_loaded, 16)
            dve.wait_ge(pool_ready, 3)
            vector_ln_stats(dve, 0, 0, 0)
            vector_ln_apply(dve, 0, 0, 0)
            vector_ln_stats(dve, 1, 1, 1)
            vector_ln_apply(dve, 1, 1, 1)
            dve.wait_ge(wqkv0_loaded, 6 * 16)
            dve.wait_ge(tg_ready, 1)
            projected(0, 0)
            softmax(0)

            def body(b, u, more):
                if more >= 2:
                    vector_ln_stats(dve, b + 2, b + 2, u)
                if more >= 1:
                    projected(b + 1, 1 - u)
                if more >= 2:
                    vector_ln_apply(dve, b + 2, b + 2, u)
                normalise(b)
                if more >= 1:
                    softmax(b + 1)
                update(b)
            over_tiles(dve, body)

        def scalar_attn0(act):
            def exps(b):
                for c, (lo, hi) in enumerate(HEADS0):
                    act.wait_ge(shifted_done, 3 * b + c + 1)
                    act.activation(e0[:, lo:hi, :], e0[:, lo:hi, :], ACT.Exp, scale=DK0 ** -0.5).then_inc(exp_done, 1)

            scalar_xnT(act, 0, 0, T0[0])
            exps(0)
            scalar_xnT(act, 1, 1, T0[1])

            def body(b, u, more):
                for j in range(4):
                    act.wait_ge(turn_in_psum, 6 * b + j + 1)
                    act.activation(eT0[:, 4 * j:4 * j + 4, :], T0[(u + j) % 2][0:T, :].rearrange("p (h q) -> p h q", q=128),
                                   ACT.Copy).then_inc(turn_done, 1)
                for j in range(2):
                    act.wait_ge(turn_in_psum, 6 * b + 4 + j + 1)
                    act.activation(oT0[:, 4 * j:4 * j + 4, :], T0[(u + j) % 2][:, :].rearrange("p (h q) -> p h q", q=128),
                                   ACT.Copy).then_inc(turn_done, 1)
                if more >= 1:
                    exps(b + 1)
                if more >= 2:
                    scalar_xnT(act, b + 2, u, T0[u])
            over_tiles(act, body)

        def gpsimd_attn0(pool):
            def context(b, u):
                at_least(pool, proj_in_psum, 6 * b - 6)
                pool.tensor_copy(ctx_b[:, u, :], ctxT[:, bass.ds(b, 1), :].rearrange("p a t -> p (a t)")).then_inc(ctx_b_done, 1)

            gpsimd_ln_rstd(pool, 0, 0)
            gpsimd_ln_rstd(pool, 1, 1)
            pool.wait_ge(ctx_loaded, 16)
            context(0, 0)
            context(1, 1)

            def body(b, u, more):
                if more >= 2:
                    gpsimd_ln_rstd(pool, b + 2, u)
                    context(b + 2, u)
            over_tiles(pool, body)

        LOGITS0 = bank[4]
        RANK0 = bank[7]
        H_BANKS = [bank[0:2], bank[2:4]]
        XE_BANK = [bank[4], bank[5]]
        Y_BANK = [bank[6], bank[7]]

        def over_experts(engine, body):
            body(0, 0, True)
            body(1, 1, True)
            with engine.Fori(1, E0 // 2 - 1) as i:
                body(i * 2, 0, True)
                body(i * 2 + 1, 1, True)
            body(E0 - 2, 0, True)
            body(E0 - 1, 1, False)

        def tensor_moe0(pe):
            pe.wait_ge(route0_loaded, 6 * 16)
            tensor_xnT(pe, 16, 0, T0[0])

            def tile(b, u, more):
                if more >= 1:
                    tensor_xnT(pe, b + 17, 1 - u, T0[1 - u])
                pe.wait_ge(xnT_done, b + 17)
                pe.matmul(LOGITS0[:, bass.ds(b * E0, E0)], xnT[:, u, :], wg0[:, :], start=True, stop=True).then_inc(logits_in_psum, 1)
            over_tiles(pe, tile)
            pe.wait_ge(first_done, 1)
            pe.matmul(RANK0[:, 0:B * E0], tri_b[:, :], first0[:, :, :].rearrange("p b e -> p (b e)"), start=True, stop=False)
            for k in range(1, B):
                m = pe.matmul(RANK0[:, k * E0:B * E0], ones_b[:, :], first0[:, 0:B - k, :].rearrange("p b e -> p (b e)"),
                              start=False, stop=(k == B - 1))
            m.then_inc(rank_in_psum, 1)

            def turn(e, v):
                pe.wait_ge(expert_loaded[v], 80 * (e // 2 + 1) if isinstance(e, int) else (e - v) * 40 + 80)
                at_least(pe, xeT_done, e - 1)
                for j in range(2):
                    m = pe.transpose(XE_BANK[v][:, j * 128:(j + 1) * 128], xe[:, v, j, :], ident[:, :])
                m.then_inc(xeT_in_psum, 1)

            def hidden(e, v):
                pe.wait_ge(xeT_done, e + 1)
                at_least(pe, h_done, 4 * e - 4)
                for c in range(FC0):
                    m = pe.matmul(H_BANKS[v][c // 2][:, (c % 2) * 256:(c % 2 + 1) * 256], w1e[:, v, c * 128:(c + 1) * 128],
                                  xeT[:, v, :], start=True, stop=True)
                    if c % 2:
                        m.then_inc(h_in_psum, 1)

            def rows_out(e, v):
                at_least(pe, y_done, e - 1)
                pe.wait_ge(h_done, 4 * e + 4)
                for j in range(2):
                    for c in range(FC0):
                        pe.matmul(Y_BANK[v][:, j * 128:(j + 1) * 128], hT0[:, v, c, j * 128:(j + 1) * 128], w2e[:, v, c, :],
                                  start=(c == 0), stop=False)
                    m = pe.matmul(Y_BANK[v][:, j * 128:(j + 1) * 128], ones_row[:, :], b2e[:, v, :], start=False, stop=True)
                m.then_inc(y_in_psum, 1)

            turn(0, 0)
            hidden(0, 0)

            def expert(e, v, more):
                if more:
                    turn(e + 1, 1 - v)
                    hidden(e + 1, 1 - v)
                rows_out(e, v)
            over_experts(pe, expert)

        def vector_moe0(dve):
            vector_ln_stats(dve, 0, 16, 0, 1)

            def tile(b, u, more):
                if more >= 1:
                    vector_ln_stats(dve, b + 1, b + 17, 1 - u, b + 2)
                vector_ln_apply(dve, b, b + 16, u, (xn_kept, b - 1))
            over_tiles(dve, tile)

            steps = [0]

            def link(ins):
                steps[0] += 1
                ins.then_inc(route_step, 1)
                dve.wait_ge(route_step, steps[0])

            def wide(a):
                return a[:, :].unsqueeze(2).to_broadcast([128, B, E0])

            def per_expert(a):
                return a[:, :].unsqueeze(1).to_broadcast([128, B, E0])

            lg = LOGITS0[:, 0:B * E0].rearrange("p (b e) -> p b e", e=E0)
            rank = RANK0[:, 0:B * E0].rearrange("p (b e) -> p b e", e=E0)
            dve.wait_ge(logits_in_psum, B)
            dve.wait_ge(route0_loaded, 6 * 16)
            link(dve.tensor_reduce(r0s["max"][:, :], lg, AX.X, ALU.max))
            dve.tensor_tensor(r0["exp"][:, :, :], lg, wide(r0s["max"]), ALU.subtract).then_inc(route_exp, 1)
            dve.wait_ge(route_exp, 2)
            link(dve.tensor_reduce(r0s["sum"][:, :], r0["exp"][:, :, :], AX.X, ALU.add))
            link(dve.reciprocal(r0s["rsum"][:, :], r0s["sum"][:, :]))
            link(dve.tensor_tensor(r0["gate"][:, :, :], r0["exp"][:, :, :], wide(r0s["rsum"]), ALU.mult))
            link(dve.tensor_reduce(r0s["gmax"][:, :], r0["gate"][:, :, :], AX.X, ALU.max))
            link(dve.tensor_tensor(r0["rank"][:, :, :], r0["gate"][:, :, :], wide(r0s["gmax"]), ALU.is_equal))
            link(dve.tensor_tensor(r0["at"][:, :, :], r0["rank"][:, :, :], per_expert(rank_w), ALU.mult))
            link(dve.tensor_reduce(r0s["rmax"][:, :], r0["at"][:, :, :], AX.X, ALU.max))
            dve.tensor_tensor(first0[:, :, :], r0["at"][:, :, :], wide(r0s["rmax"]), ALU.is_equal).then_inc(first_done, 1)
            dve.wait_ge(rank_in_psum, 1)
            link(dve.scalar_tensor_tensor(r0["keep"][:, :, :].rearrange("p b e -> p (b e)"), RANK0[:, 0:B * E0], float(C0),
                                          first0[:, :, :].rearrange("p b e -> p (b e)"), ALU.is_le, ALU.mult))
            link(dve.tensor_tensor(r0["rank"][:, :, :], rank, per_expert(slot_base), ALU.add))
            link(dve.tensor_tensor(r0["at"][:, :, :], r0["rank"][:, :, :], r0["keep"][:, :, :], ALU.mult))
            link(dve.tensor_reduce(r0s["slot"][:, :], r0["at"][:, :, :], AX.X, ALU.add))
            link(dve.tensor_reduce(r0s["kept"][:, :], r0["keep"][:, :, :], AX.X, ALU.add))
            link(dve.tensor_tensor(r0s["alt"][:, :], spare_slot[:, :], r0s["kept"][:, :], ALU.mult))
            link(dve.tensor_tensor(r0s["alt2"][:, :], spare_slot[:, :], r0s["alt"][:, :], ALU.subtract))
            dve.tensor_tensor(scatter_at[:, :], r0s["slot"][:, :], r0s["alt2"][:, :], ALU.add).then_inc(places_done, 1)
            dve.tensor_copy(gather_at[:, :], r0s["slot"][:, :]).then_inc(places_done, 1)
            link(dve.tensor_tensor(r0["gkeep"][:, :, :], r0["gate"][:, :, :], r0["keep"][:, :, :], ALU.mult))
            link(dve.tensor_reduce(r0s["gsel"][:, :], r0["gkeep"][:, :, :], AX.X, ALU.add))
            link(dve.tensor_scalar(r0s["weight"][:, :], r0s["gsel"][:, :], tg[:, 4:5], None, ALU.mult))

            def expert(e, v, more):
                dve.wait_ge(y_in_psum, e + 1)
                if not isinstance(e, int):
                    dve.wait_ge(y_stored[v], (e - v) * 8)
                elif e >= 2:
                    dve.wait_ge(y_stored[v], 16 * (e // 2))
                dve.tensor_copy(ye[:, v, :, :], Y_BANK[v][:, 0:256].rearrange("p (j d) -> p j d", d=D)).then_inc(y_done, 1)
            over_experts(dve, expert)

            for b in range(B):
                if b % 4 == 0:
                    dve.wait_ge(gathered[b // 4], 64)
                dve.scalar_tensor_tensor(X[:, b, :], XN[:, b, :], r0s["weight"][:, b:b + 1], X[:, b, :],
                                         ALU.mult, ALU.add).then_inc(x_updated, 1)

        def scalar_moe0(act):
            def tile(b, u, more):
                scalar_xnT(act, b + 16, u, T0[u])
            over_tiles(act, tile)
            act.wait_ge(route_exp, 1)
            act.activation(r0["exp"][:, :, :], r0["exp"][:, :, :], ACT.Exp).then_inc(route_exp, 1)

            def turn(e, v):
                act.wait_ge(xeT_in_psum, e + 1)
                act.activation(xeT[:, v, :], XE_BANK[v][:, 0:256], ACT.Copy).then_inc(xeT_done, 1)

            turn(0, 0)

            def expert(e, v, more):
                if more:
                    turn(e + 1, 1 - v)
                for c in range(FC0):
                    act.wait_ge(h_in_psum, 2 * e + c // 2 + 1)
                    act.activation(hT0[:, v, c, :], H_BANKS[v][c // 2][:, (c % 2) * 256:(c % 2 + 1) * 256],
                                   ACT.Gelu_apprx_tanh, bias=b1e[:, v, c:c + 1]).then_inc(h_done, 1)
            over_experts(act, expert)

        def gpsimd_moe0(pool):
            gpsimd_ln_rstd(pool, 16, 0)

            def tile(b, u, more):
                if more >= 1:
                    gpsimd_ln_rstd(pool, b + 17, 1 - u)
                pool.wait_ge(xn_done, b + 17)
                pool.tensor_copy(XN[:, bass.ds(b, 1), :].rearrange("p a d -> p (a d)"), xn[:, u, :]).then_inc(xn_kept, 1)
            over_tiles(pool, tile)
            pool.wait_ge(xn_kept, B)
            pool.wait_ge(places_done, 2)
            pool.wait_ge(slots_zeroed, 16)
            for b in range(B):
                pool.indirect_dma_start(out=t["x_slots"], out_offset=bass.IndirectOffsetOnAxis(ap=scatter_at[:, b:b + 1], axis=0),
                                        in_=XN[:, b, :], in_offset=None).then_inc(scattered, 16)
            pool.wait_ge(y_stored[0], E0 // 2 * 16)
            pool.wait_ge(y_stored[1], E0 // 2 * 16)
            for b in range(B):
                pool.indirect_dma_start(out=XN[:, b, :], out_offset=None, in_=t["y_slots"],
                                        in_offset=bass.IndirectOffsetOnAxis(ap=gather_at[:, b:b + 1], axis=0)).then_inc(gathered[b // 4], 16)

        def sync_moe0(sp):
            sp.wait_ge(scattered, B * 16)

            def load(e, v):
                def one(name, pattern=None, **kw):
                    a = t[name][bass.ds(e, 1)]
                    return a.rearrange(pattern, **kw)
                sp.dma_start(xe[:, v, :, :], t["x_slots"][bass.ds(e * C0, C0), :].rearrange("(j p) d -> p j d", p=128)).then_inc(expert_loaded[v], 16)
                sp.dma_start(w1e[:, v, :], one("w1_0", "a p f -> p (a f)")).then_inc(expert_loaded[v], 16)
                sp.dma_start(w2e[:, v, :, :], one("w2_0", "a (c p) d -> p (a c) d", p=128)).then_inc(expert_loaded[v], 16)
                sp.dma_start(b1e[:, v, :], one("b1_0", "a p c -> p (a c)")).then_inc(expert_loaded[v], 16)
                sp.dma_start(b2e[:, v, :], one("b2_0", "a x d -> a (x d)")).then_inc(expert_loaded[v], 16)
            load(0, 0)

            def expert(e, v, more):
                if more:
                    at_least(sp, y_in_psum, e)
                    load(e + 1, 1 - v)
                sp.wait_ge(y_done, e + 1)
                sp.dma_start(t["y_slots"][bass.ds(e * C0, C0), :].rearrange("(j p) d -> p j d", p=128), ye[:, v, :, :]).then_inc(y_stored[v], 16)
            over_experts(sp, expert)

        MIX = [bank[4], bank[7]]

        def tensor_mix1(pe):
            pe.wait_ge(mix_loaded, 3 * 16)
            pe.wait_ge(ctx_mean_done, 1)
            for b in range(B):
                dst = bank[b // 4][0:1, (b % 4) * D:(b % 4 + 1) * D]
                pe.matmul(dst, ctx_mean[:, b:b + 1], w2x[:, :], start=True, stop=False)
                m = pe.matmul(dst, ones_row[:, 0:1], bx[:, :], start=False, stop=True)
                if b % 4 == 3:
                    m.then_inc(mix_row_in_psum, 1)
            tensor_xnT(pe, 32, 0, T0[0])
            pe.wait_ge(mix_row_done, 4)

            def tile(b, u, more):
                if more >= 1:
                    tensor_xnT(pe, b + 33, 1 - u, T0[1 - u])
                pe.wait_ge(xnT_done, b + 33)
                at_least(pe, x_updated, 2 * B + b - 1)
                pe.matmul(MIX[u][:, 0:D], xnT[:, u, :], w1x[:, :], start=True, stop=False)
                pe.matmul(MIX[u][:, 0:D], ones_row[:, :], mix_row[:, bass.ds(b * D, D)], start=False, stop=True).then_inc(mix_in_psum, 1)
            over_tiles(pe, tile)

        def vector_mix1(dve):
            dve.tensor_reduce(ctx_sum[:, :], ctxT[:, :, :], AX.X, ALU.add).then_inc(quant_step, 1)
            dve.wait_ge(quant_step, 1)
            dve.tensor_scalar(ctx_mean[:, :], ctx_sum[:, :], 1.0 / T, None, ALU.mult).then_inc(ctx_mean_done, 1)
            for g in range(4):
                dve.wait_ge(mix_row_in_psum, g + 1)
                dve.tensor_copy(mix_row[:, g * 512:(g + 1) * 512], bank[g][0:1, :]).then_inc(mix_row_done, 1)
            vector_ln_stats(dve, 0, 32, 0, 2 * B)
            vector_ln_apply(dve, 0, 32, 0)

            def tile(b, u, more):
                last = more == 0
                if not last:
                    vector_ln_stats(dve, b + 1, 2 * b + 33, 1 - u)
                    vector_ln_apply(dve, b + 1, b + 33, 1 - u, None, 2 * b + 33)
                dve.wait_ge(mix_in_psum, b + 1)
                dve.scalar_tensor_tensor(slot(b), MIX[u][:, 0:D], tg[:, 1:2], slot(b), ALU.mult, ALU.add).then_inc(x_updated, 1)
                q = 2 * b + (33 if last else 34)
                vector_ln_stats(dve, b, q, 2, 2 * B + b + 1)
                dve.wait_ge(rstd_done, q + 1)
                dve.tensor_scalar(XN[:, bass.ds(b, 1), :].rearrange("p a d -> p (a d)"), slot(b), ln_mv[:, 2, 0:1], ln_rstd[:, 2:3],
                                  ALU.subtract, ALU.mult).then_inc(norm1_done, 1)
                dve.wait_ge(norm1_done, b + 1)
                dve.tensor_reduce(absmax1[:, bass.ds(b, 1)], XN[:, bass.ds(b, 1), :].rearrange("p a d -> p (a d)"), AX.X, ALU.max,
                                  apply_absolute_value=True).then_inc(absmax_done, 1)
            over_tiles(dve, tile)

        def scalar_mix1(act):
            def tile(b, u, more):
                scalar_xnT(act, b + 32, u, T0[u])
            over_tiles(act, tile)

        def gpsimd_mix1(pool):
            gpsimd_ln_rstd(pool, 32, 0)

            def tile(b, u, more):
                if more:
                    gpsimd_ln_rstd(pool, 2 * b + 33, 1 - u)
                gpsimd_ln_rstd(pool, 2 * b + (34 if more else 33), 2)
            over_tiles(pool, tile)

        GATE_BANK = [bank[0], bank[2], bank[4]]
        UP_BANK = [bank[1], bank[3], bank[7]]
        XQ_BANK = [bank[5], bank[6]]
        DOWN_BANK = [bank[0], bank[2], bank[1], bank[3]]

        def tensor_ffn1(pe):
            for k in range(7):
                pe.wait_ge(w_rounded, k + 1)
                at_least(pe, wT_done, k - 1)
                if k < 6:
                    lo, hi = ROWS1[k % 3]
                    pe.transpose(XQ_BANK[k % 2][:, 0:hi - lo], wgu1[0:hi - lo, k // 3, k % 3, :], ident[0:hi - lo, 0:hi - lo]).then_inc(wT_in_psum, 1)
                else:
                    for c, (lo, hi) in enumerate(ROWS1):
                        m = pe.transpose(XQ_BANK[0][0:hi - lo, c * D:(c + 1) * D], wd1[:, lo:hi], ident[:, :])
                    m.then_inc(wT_in_psum, 1)
            pe.wait_ge(drow_in_psum, 1)
            pe.matmul(bank[0][:, 0:D], ones[:, :], dscale1[:, :], start=True, stop=True).then_inc(drow_in_psum, 1)

            def spread_max(k, col):
                pe.wait_ge(colmax_done, k + 1)
                pe.transpose(bank[0][0:1, 128:256], col[:, :], ident[:, :]).then_inc(maxrow_in_psum, 1)
                pe.wait_ge(cell_done, k + 1)
                pe.matmul(bank[0][:, 256:257], ones_row[:, :], cell1[:, k:k + 1], start=True, stop=True).then_inc(max_in_psum, 1)

            pe.wait_ge(quant_step, DROW_STEP)
            spread_max(0, col1["xmax"])

            def turn(g):
                pe.wait_ge(xq_done, g + 1)
                if g == 0:
                    pe.wait_ge(wT_done, 7)
                at_least(pe, xqT_done, g - 1)
                for j in range(4):
                    m = pe.transpose(XQ_BANK[g % 2][:, j * 128:(j + 1) * 128], xq1[:, j, :], ident[:, :])
                m.then_inc(xqT_in_psum, 1)

            turn(0)
            for g in range(4):
                pe.wait_ge(xqT_done, g + 1)
                for c, (lo, hi) in enumerate(ROWS1):
                    if g == 0 and c == 0:
                        pe.wait_ge(quant_step, XINV_STEP)
                    at_least(pe, silu_done, 3 * (g - 1) + c + 1)
                    at_least(pe, h1_done, 3 * (g - 1) + c + 1)
                    pe.matmul(GATE_BANK[c][0:hi - lo, :], wguT1[:, 0, lo:hi], xqT1[:, g % 2, :], start=True, stop=True)
                    pe.matmul(UP_BANK[c][0:hi - lo, :], wguT1[:, 1, lo:hi], xqT1[:, g % 2, :], start=True, stop=True).then_inc(gu_in_psum, 1)
                if g < 3:
                    turn(g + 1)
            pe.wait_ge(silu_done, 12)
            spread_max(1, col1["hmax"])
            for g in range(4):
                at_least(pe, h1_done, 12)
                pe.wait_ge(hq_done, 3)
                if g == 0:
                    pe.wait_ge(quant_step, HINV_STEP)
                for j in range(4):
                    for c, (lo, hi) in enumerate(ROWS1):
                        tok = (4 * g + j) * 128
                        m = pe.matmul(DOWN_BANK[g][:, j * D:(j + 1) * D], hq1[0:hi - lo, c, tok:tok + 128], wdT1[0:hi - lo, c, :],
                                      start=(c == 0), stop=(c == 2))
                m.then_inc(down_in_psum, 1)

        def vector_ffn1(dve):
            steps = [1]

            def link(ins):
                steps[0] += 1
                ins.then_inc(quant_step, 1)
                dve.wait_ge(quant_step, steps[0])

            dve.wait_ge(ffn1_loaded, 5 * 16)
            dve.memset(wmax1[:, :], 1.0)
            link(dve.memset(hmax1[:, :], 0.0))
            for k in range(6):
                lo, hi = ROWS1[k % 3]
                dve.tensor_reduce(wmax1[0:hi - lo, k:k + 1], wgu1[0:hi - lo, k // 3, k % 3, :], AX.X, ALU.max, apply_absolute_value=True)
            link(dve.tensor_reduce(wmax1[:, 6:7], wd1[:, :], AX.X, ALU.max, apply_absolute_value=True))
            link(dve.tensor_scalar(wscale1[:, :], wmax1[:, :], 1.0 / QMAX, None, ALU.mult))
            link(dve.reciprocal(winv1[:, :], wscale1[:, :]))
            for k in range(6):
                lo, hi = ROWS1[k % 3]
                w = wgu1[0:hi - lo, k // 3, k % 3, :]
                dve.tensor_scalar(w, w, winv1[0:hi - lo, k:k + 1], MAGIC, ALU.mult, ALU.add).then_inc(w_rounded, 1)
            dve.tensor_scalar(wd1[:, :], wd1[:, :], winv1[:, 6:7], MAGIC, ALU.mult, ALU.add).then_inc(w_rounded, 1)
            dve.tensor_scalar(dscale1[:, :], ident[:, :], wscale1[:, 6:7], None, ALU.mult).then_inc(drow_in_psum, 1)
            dve.wait_ge(drow_in_psum, 2)
            link(dve.tensor_copy(drow1[:, :], bank[0][:, 0:D]))
            assert steps[0] == DROW_STEP
            dve.wait_ge(clip_tanh_done, 1)
            link(dve.tensor_scalar(clip_sig[:, :], clip_tanh[:, :], 0.5, 0.5, ALU.mult, ALU.add))

            def scale_of(k, columns, colmax, scale, inv):
                dve.tensor_reduce(colmax[:, :], columns, AX.X, ALU.max).then_inc(colmax_done, 1)
                dve.wait_ge(maxrow_in_psum, k + 1)
                dve.tensor_reduce(cell1[:, k:k + 1], bank[0][0:1, 128:256], AX.X, ALU.max).then_inc(cell_done, 1)
                dve.wait_ge(max_in_psum, k + 1)
                link(dve.tensor_scalar(scale[:, :], bank[0][:, 256:257], clip_sig[:, k:k + 1], 1.0 / QMAX, ALU.mult, ALU.mult))
                link(dve.reciprocal(inv[:, :], scale[:, :]))

            dve.wait_ge(absmax_done, B)
            scale_of(0, absmax1[:, :], col1["xmax"], col1["xscale"], col1["xinv"])
            assert steps[0] == XINV_STEP
            link(dve.tensor_scalar(guscale1[:, :, :].rearrange("p a c -> p (a c)"), wscale1[:, 0:6], col1["xscale"][:, :], None, ALU.mult))

            def quantise(g):
                at_least(dve, xqT_in_psum, g)
                x4 = XN[:, 4 * g:4 * g + 4, :]
                link(dve.tensor_scalar(x4, x4, col1["xinv"][:, :], QMAX, ALU.mult, ALU.min))
                dve.tensor_scalar(xq1[:, :, :], x4, -QMAX - 1.0, MAGIC, ALU.max, ALU.add).then_inc(xq_done, 1)

            quantise(0)
            for g in range(4):
                if g < 3:
                    quantise(g + 1)
                for c, (lo, hi) in enumerate(ROWS1):
                    h = h1[0:hi - lo, c, g * 512:(g + 1) * 512]
                    dve.wait_ge(silu_done, 3 * g + c + 1)
                    dve.scalar_tensor_tensor(h, UP_BANK[c][0:hi - lo, :], guscale1[0:hi - lo, 1, c:c + 1], silu1[0:hi - lo, c, :],
                                             ALU.mult, ALU.mult).then_inc(h1_done, 1)
                    dve.wait_ge(h1_done, 3 * g + c + 1)
                    m = dve.tensor_reduce(hmax1[0:hi - lo, 3 * g + c:3 * g + c + 1], h, AX.X, ALU.max, apply_absolute_value=True)
            link(m)
            scale_of(1, hmax1[:, :], col1["hmax"], col1["hscale"], col1["hinv"])
            assert steps[0] == HINV_STEP
            for c, (lo, hi) in enumerate(ROWS1):
                h = h1[0:hi - lo, c, :]
                link(dve.tensor_scalar(h, h, col1["hinv"][0:hi - lo, :], QMAX, ALU.mult, ALU.min))
                dve.tensor_scalar(h, h, -QMAX - 1.0, MAGIC, ALU.max, ALU.add).then_inc(hq_rounded, 1)
            link(dve.tensor_tensor(col1["out"][:, :], col1["hscale"][:, :], tg[:, 5:6], ALU.mult))
            for g in range(4):
                dve.wait_ge(down_in_psum, g + 1)
                out = tmp512[:, g % 2, :].rearrange("p (j d) -> p j d", d=D)
                link(dve.scalar_tensor_tensor(out, DOWN_BANK[g][:, :].rearrange("p (j d) -> p j d", d=D), col1["out"][:, :],
                                              drow1[:, :].unsqueeze(1).to_broadcast([128, 4, D]), ALU.mult, ALU.mult))
                dve.tensor_tensor(X[:, 4 * g:4 * g + 4, :], out, X[:, 4 * g:4 * g + 4, :], ALU.add).then_inc(x_updated, 4)

        def scalar_ffn1(act):
            for k in range(7):
                act.wait_ge(wT_in_psum, k + 1)
                if k < 6:
                    lo, hi = ROWS1[k % 3]
                    m = act.activation(wguT1[:, k // 3, lo:hi], XQ_BANK[k % 2][:, 0:hi - lo], ACT.Identity, bias=minus_magic[:, :])
                else:
                    for c, (lo, hi) in enumerate(ROWS1):
                        m = act.activation(wdT1[0:hi - lo, c, :], XQ_BANK[0][0:hi - lo, c * D:(c + 1) * D], ACT.Identity,
                                           bias=minus_magic[0:hi - lo, :])
                m.then_inc(wT_done, 1)

            def turn(g):
                act.wait_ge(xqT_in_psum, g + 1)
                act.activation(xqT1[:, g % 2, :], XQ_BANK[g % 2][:, :], ACT.Identity, bias=minus_magic[:, :]).then_inc(xqT_done, 1)

            turn(0)
            for g in range(4):
                for c, (lo, hi) in enumerate(ROWS1):
                    act.wait_ge(gu_in_psum, 3 * g + c + 1)
                    at_least(act, h1_done, 3 * (g - 1) + c + 1)
                    if g == 0 and c == 0:
                        act.wait_ge(quant_step, GUSCALE_STEP)
                    act.activation(silu1[0:hi - lo, c, :], GATE_BANK[c][0:hi - lo, :], ACT.Silu,
                                   scale=guscale1[0:hi - lo, 0, c:c + 1]).then_inc(silu_done, 1)
                if g < 3:
                    turn(g + 1)
            for c, (lo, hi) in enumerate(ROWS1):
                act.wait_ge(hq_rounded, c + 1)
                act.activation(hq1[0:hi - lo, c, :], h1[0:hi - lo, c, :], ACT.Identity, bias=minus_magic[0:hi - lo, :]).then_inc(hq_done, 1)

        XT4 = [bank[5], bank[6]]

        def vector_g_stats(dve, g, k, updates):
            dve.wait_ge(x_updated, updates)
            for j in range(4):
                dve.bn_stats(g_stats[:, k % 2, j, :], X[:, 4 * g + j, :]).then_inc(g_stats_done, 1)
            dve.wait_ge(g_stats_done, 4 * (k + 1))
            for j in range(4):
                dve.bn_aggr(g_mv[:, k % 2, j, :], g_stats[:, k % 2, j, :]).then_inc(g_var_done, 1)

        def gpsimd_g_rstd(pool, k):
            u = k % 2
            pool.wait_ge(g_var_done, 4 * (k + 1))
            pool.tensor_tensor(g_veps[:, u, :], g_mv[:, u, :, 1], eps[:, :].to_broadcast([128, 4]), ALU.add).then_inc(g_veps_done, 1)
            pool.wait_ge(g_veps_done, k + 1)
            pool.tensor_tensor(g_rstd[:, u, :], g_veps[:, u, :], minus_half[:, :].to_broadcast([128, 4]), ALU.pow).then_inc(g_rstd_done, 1)

        def vector_g_apply(dve, g, k, used=0):
            dve.wait_ge(g_rstd_done, k + 1)
            at_least(dve, d3_in_psum, used)
            at_least(dve, g_xnT_in_psum, k - 1)
            for j in range(4):
                dve.tensor_scalar(xn4[:, k % 2, j, :], X[:, 4 * g + j, :], g_mv[:, k % 2, j, 0:1], g_rstd[:, k % 2, j:j + 1],
                                  ALU.subtract, ALU.mult).then_inc(g_xn_done, 1)

        def tensor_g_xnT(pe, k, psum):
            pe.wait_ge(g_xn_done, 4 * (k + 1))
            at_least(pe, g_xnT_done, k)
            for j in range(4):
                m = pe.transpose(psum[:, j * 128:(j + 1) * 128], xn4[:, k % 2, j, :], ident[:, :])
            m.then_inc(g_xnT_in_psum, 1)

        def scalar_g_xnT(act, k, psum):
            act.wait_ge(g_xnT_in_psum, k + 1)
            act.activation(xnT4[:, k % 2, :], psum[:, :], ACT.Copy).then_inc(g_xnT_done, 1)

        KV2 = [bank[0], bank[1], bank[2], bank[3], bank[4], bank[7], bank[6]]
        Q2, S2, ET2, AV2 = bank[0], bank[1], bank[2], bank[3]
        KB2 = [(0, 6), (6, 12), (12, 16)]

        def tensor_attn2(pe):
            pe.wait_ge(attn2_loaded, 4 * 16)
            pe.wait_ge(x_updated, 4 * B)
            for n, (lo, hi) in enumerate(KB2):
                pe.matmul(KV2[n][:, 0:(hi - lo) * T], wqkv2[:, 1, :], ctxT[:, lo:hi, :].rearrange("p b t -> p (b t)"),
                          start=True, stop=True).then_inc(kv2_in_psum, 1)
            for n in range(4):
                for j in range(4):
                    m = pe.matmul(KV2[3 + n][0:T, j * D:(j + 1) * D], ctxT[:, 4 * n + j, :], wqkv2[:, 2, :], start=True, stop=True)
                m.then_inc(kv2_in_psum, 1)
            tensor_g_xnT(pe, 0, XT4[0])
            pe.wait_ge(v2_done, 4)
            pe.wait_ge(k2_done, 3)
            for g in range(4):
                pe.wait_ge(g_xnT_done, g + 1)
                at_least(pe, q2_done, g)
                pe.matmul(Q2[:, :], wqkv2[:, 0, :], xnT4[:, g % 2, :], start=True, stop=True).then_inc(q2_in_psum, 1)
                pe.wait_ge(q2_done, g + 1)
                at_least(pe, shift2_done, g)
                for j in range(4):
                    m = pe.matmul(S2[:, j * T:(j + 1) * T], qT2[:, j * 128:(j + 1) * 128], kT2[:, 4 * g + j, :], start=True, stop=True)
                m.then_inc(s2_in_psum, 1)
                if g < 3:
                    tensor_g_xnT(pe, g + 1, XT4[(g + 1) % 2])
                pe.wait_ge(exp2_done, g + 1)
                at_least(pe, eT2_done, g)
                for j in range(4):
                    m = pe.transpose(ET2[0:T, j * 128:(j + 1) * 128], e2[:, j, :], ident[:, :])
                m.then_inc(eT2_in_psum, 1)
                pe.wait_ge(eT2_done, g + 1)
                at_least(pe, x_updated, 4 * B + 4 * g)
                for j in range(4):
                    m = pe.matmul(AV2[:, j * D:(j + 1) * D], eT2[:, j * 128:(j + 1) * 128], v2[:, 4 * g + j, :], start=True, stop=True)
                m.then_inc(av2_in_psum, 1)

        def vector_attn2(dve):
            steps = [0]

            def link(ins):
                steps[0] += 1
                ins.then_inc(a2_step, 1)
                dve.wait_ge(a2_step, steps[0])

            vector_g_stats(dve, 0, 0, 4 * B)
            for n in range(4):
                dve.wait_ge(kv2_in_psum, 4 + n)
                dve.tensor_tensor(v2[:, 4 * n:4 * n + 4, :], KV2[3 + n][0:T, :].rearrange("p (j d) -> p j d", d=D),
                                  bv2[:, :].unsqueeze(1).to_broadcast([T, 4, D]), ALU.add).then_inc(v2_done, 1)
            vector_g_apply(dve, 0, 0)

            def softmax(g):
                sc = S2[:, 0:4 * T].rearrange("p (j t) -> p j t", t=T)
                dve.wait_ge(s2_in_psum, g + 1)
                link(dve.tensor_reduce(s2["max"][:, :], sc, AX.X, ALU.max))
                dve.tensor_tensor(e2[:, :, :], sc, s2["max"][:, :].unsqueeze(2).to_broadcast([128, 4, T]), ALU.subtract).then_inc(shift2_done, 1)
                if g < 3:
                    vector_g_apply(dve, g + 1, g + 1)
                dve.wait_ge(exp2_done, g + 1)
                link(dve.tensor_reduce(s2["sum"][:, :], e2[:, :, :], AX.X, ALU.add))
                link(dve.reciprocal(s2["rsum"][:, :], s2["sum"][:, :]))
                link(dve.tensor_scalar(s2["out"][:, :], s2["rsum"][:, :], tg[:, 2:3], None, ALU.mult))

            for g in range(4):
                if g < 3:
                    vector_g_stats(dve, g + 1, g + 1, 4 * B)
                softmax(g)
                dve.wait_ge(av2_in_psum, g + 1)
                out = tmp512[:, g % 2, :].rearrange("p (j d) -> p j d", d=D)
                link(dve.tensor_tensor(out, AV2[:, :].rearrange("p (j d) -> p j d", d=D),
                                       s2["out"][:, :].unsqueeze(2).to_broadcast([128, 4, D]), ALU.mult))
                dve.tensor_tensor(X[:, 4 * g:4 * g + 4, :], out, X[:, 4 * g:4 * g + 4, :], ALU.add).then_inc(x_updated, 4)

        def scalar_attn2(act):
            for n, (lo, hi) in enumerate(KB2):
                act.wait_ge(kv2_in_psum, n + 1)
                act.activation(kT2[:, lo:hi, :].rearrange("p b t -> p (b t)"), KV2[n][:, 0:(hi - lo) * T], ACT.Identity,
                               bias=bqk2[:, 1:2]).then_inc(k2_done, 1)
            scalar_g_xnT(act, 0, XT4[0])
            for g in range(4):
                act.wait_ge(q2_in_psum, g + 1)
                act.activation(qT2[:, :], Q2[:, :], ACT.Identity, bias=bqk2[:, 0:1]).then_inc(q2_done, 1)
                act.wait_ge(shift2_done, g + 1)
                act.activation(e2[:, :, :], e2[:, :, :], ACT.Exp, scale=D ** -0.5).then_inc(exp2_done, 1)
                if g < 3:
                    scalar_g_xnT(act, g + 1, XT4[(g + 1) % 2])
                act.wait_ge(eT2_in_psum, g + 1)
                act.activation(eT2[:, :], ET2[0:T, :], ACT.Copy).then_inc(eT2_done, 1)

        def gpsimd_attn2(pool):
            for k in range(4):
                gpsimd_g_rstd(pool, k)

        SETS2 = [(bank[0], bank[1], bank[2]), (bank[3], bank[4], bank[7])]
        MISC2 = bank[6]
        PAIRS2 = [4, 0, 1, 2, 3]

        def tensor_moe2(pe):
            pe.wait_ge(moe2_loaded, 5 * 16)
            tensor_g_xnT(pe, 4, bank[5])
            for g in range(4):
                x4 = xnT4[:, g % 2, :]

                def up(i):
                    n = 5 * g + i
                    at_least(pe, h2_done, n - 1)
                    for a in range(2):
                        m = pe.matmul(SETS2[n % 2][a][:, :], w13_2[:, a, PAIRS2[i], :], x4, start=True, stop=True)
                    m.then_inc(ab2_in_psum, 1)

                pe.wait_ge(g_xnT_done, g + 5)
                pe.wait_ge(x_updated, 5 * B + 4 * g)
                for j in range(4):
                    dst = MISC2[:, j * E2:(j + 1) * E2]
                    pe.matmul(dst, x4[:, j * 128:(j + 1) * 128], rw2[:, :], start=True, stop=False)
                    m = pe.matmul(dst, ones_row[:, :], rb2[:, :], start=False, stop=True)
                m.then_inc(logits2_in_psum, 1)
                up(0)
                up(1)
                if g < 3:
                    tensor_g_xnT(pe, g + 5, bank[5])
                pe.wait_ge(gates2_done, g + 1)
                for j in range(4):
                    m = pe.transpose(MISC2[0:E2, j * 128:(j + 1) * 128], r2["gate"][:, j, :], ident[:, :])
                m.then_inc(gT2_in_psum, 1)
                pe.wait_ge(gT2_done, g + 1)
                for i in range(1, 5):
                    pe.matmul(SETS2[(5 * g + i) % 2][2][:, :], pair_sel[:, PAIRS2[i], :], gT2[:, :], start=True, stop=True).then_inc(g2_in_psum, 1)
                    if i < 4:
                        up(i + 1)
                pe.wait_ge(h2_done, 5 * g + 5)
                for j in range(4):
                    for p in range(5):
                        m = pe.matmul(MISC2[:, j * D:(j + 1) * D], h2[:, p, j * 128:(j + 1) * 128], w2_2[:, p, :],
                                      start=(p == 0), stop=(p == 4))
                m.then_inc(out2_in_psum, 1)

        def vector_moe2(dve):
            steps = [0, 0]

            def link(ins):
                steps[0] += 1
                ins.then_inc(route2_step, 1)
                dve.wait_ge(route2_step, steps[0])

            def link2(ins):
                steps[1] += 1
                ins.then_inc(mul2_step, 1)
                dve.wait_ge(mul2_step, steps[1])

            def wide(a):
                return r2s[a][:, :].unsqueeze(2).to_broadcast([128, 4, E2])

            ranks = rank_w[:, :].unsqueeze(1).to_broadcast([128, 4, E2])
            lg = MISC2[:, 0:4 * E2].rearrange("p (j e) -> p j e", e=E2)

            def best(src, m, r, tmp, onehot):
                link(dve.tensor_reduce(r2s[m][:, :], src, AX.X, ALU.max))
                link(dve.tensor_tensor(r2[tmp][:, :, :], src, wide(m), ALU.is_equal))
                link(dve.tensor_tensor(r2["a"][:, :, :], r2[tmp][:, :, :], ranks, ALU.mult))
                link(dve.tensor_reduce(r2s[r][:, :], r2["a"][:, :, :], AX.X, ALU.max))
                link(dve.tensor_tensor(r2[onehot][:, :, :], r2["a"][:, :, :], wide(r), ALU.is_equal))

            def route(g):
                dve.wait_ge(logits2_in_psum, g + 1)
                best(lg, "m1", "r1", "rank", "first")
                link(dve.scalar_tensor_tensor(r2["rest"][:, :, :].rearrange("p j e -> p (j e)"), r2["first"][:, :, :].rearrange("p j e -> p (j e)"),
                                              MASKED, MISC2[:, 0:4 * E2], ALU.mult, ALU.add))
                best(r2["rest"][:, :, :], "m2", "r2", "rank2", "second")
                dve.tensor_tensor(r2s["d"][:, :], r2s["m2"][:, :], r2s["m1"][:, :], ALU.subtract).then_inc(gap2_done, 1)
                dve.wait_ge(gap2_exp, g + 1)
                link(dve.tensor_scalar(r2s["den"][:, :], r2s["e"][:, :], 1.0, None, ALU.add))
                link(dve.reciprocal(r2s["g1"][:, :], r2s["den"][:, :]))
                link(dve.tensor_tensor(r2s["g2"][:, :], r2s["e"][:, :], r2s["g1"][:, :], ALU.mult))
                dve.tensor_tensor(r2["a"][:, :, :], r2["first"][:, :, :], wide("g1"), ALU.mult)
                link(dve.tensor_tensor(r2["b"][:, :, :], r2["second"][:, :, :], wide("g2"), ALU.mult))
                dve.tensor_tensor(r2["gate"][:, :, :], r2["a"][:, :, :], r2["b"][:, :, :], ALU.add).then_inc(gates2_done, 1)

            def activate(g, i):
                n = 5 * g + i
                a, b, gate = SETS2[n % 2]
                u = u2[:, n % 2, :]
                p = PAIRS2[i]
                dve.wait_ge(tanh2_done, n + 1)
                link2(dve.scalar_tensor_tensor(u, th2[:, n % 2, :], 1.0, a[:, :], ALU.add, ALU.mult))
                if i == 0:
                    at_least(dve, out2_in_psum, g)
                    dve.scalar_tensor_tensor(h2[:, p, :], u, 0.5, b[:, :], ALU.mult, ALU.mult).then_inc(h2_done, 1)
                else:
                    link2(dve.tensor_tensor(u, u, b[:, :], ALU.mult))
                    dve.wait_ge(g2_in_psum, 4 * g + i)
                    dve.tensor_tensor(h2[:, p, :], u, gate[:, :], ALU.mult).then_inc(h2_done, 1)

            vector_g_stats(dve, 0, 4, 5 * B)
            vector_g_apply(dve, 0, 4)
            for g in range(4):
                if g < 3:
                    vector_g_stats(dve, g + 1, g + 5, 5 * B)
                route(g)
                if g < 3:
                    vector_g_apply(dve, g + 1, g + 5)
                for i in range(5):
                    activate(g, i)
                dve.wait_ge(out2_in_psum, g + 1)
                x4 = X[:, 4 * g:4 * g + 4, :].rearrange("p j d -> p (j d)")
                dve.scalar_tensor_tensor(x4, MISC2[:, :], tg[:, 6:7], x4, ALU.mult, ALU.add).then_inc(x_updated, 4)

        def scalar_moe2(act):
            def tanh(g, i):
                n = 5 * g + i
                act.wait_ge(ab2_in_psum, n + 1)
                act.activation(th2[:, n % 2, :], SETS2[n % 2][0][:, :], ACT.Tanh, scale=0.5).then_inc(tanh2_done, 1)

            scalar_g_xnT(act, 4, bank[5])
            for g in range(4):
                act.wait_ge(gap2_done, g + 1)
                act.activation(r2s["e"][:, :], r2s["d"][:, :], ACT.Exp).then_inc(gap2_exp, 1)
                tanh(g, 0)
                tanh(g, 1)
                if g < 3:
                    scalar_g_xnT(act, g + 5, bank[5])
                act.wait_ge(gT2_in_psum, g + 1)
                act.activation(gT2[:, :], MISC2[0:E2, :], ACT.Copy).then_inc(gT2_done, 1)
                for i in range(2, 5):
                    tanh(g, i)

        def gpsimd_moe2(pool):
            for k in range(4, 8):
                gpsimd_g_rstd(pool, k)

        RING3 = bank[0:4]
        QKV3, MISC3 = bank[4], bank[7]
        CHUNKS3 = [(half, aux, odd) for half in range(2) for aux in range(2) for odd in range(2)]

        def heads3(half, odd):
            return slice(8 * half + odd, 8 * half + 8, 2)

        def tensor_attn3(pe):
            def project(b, u):
                pe.wait_ge(xnT_done, 48 + b + 1)
                at_least(pe, proj3_done, 4 * b - 2)
                pe.matmul(QKV3[:, 0:3 * D], xnT[:, u, :], wqkv3[:, :], start=True, stop=True).then_inc(qkv3_in_psum, 1)
                pe.wait_ge(ctx_b_done, B + b + 1)
                pe.wait_ge(x_updated, 6 * B + b - 1) if not (isinstance(b, int) and b == 0) else None
                pe.matmul(MISC3[0:T, 0:2 * D], ctx_b[:, u, :], wkva3[:, :], start=True, stop=True).then_inc(kva3_in_psum, 1)

            def turn_stacks(b, u, after):
                for n, (src, p, w) in enumerate(((sq3[:, u], 128, 128), (sk3, 128, 128), (sa3, T, T + 1))):
                    sem_, count = after[n]
                    at_least(pe, sem_, count)
                    pe.wait_ge(split3_done, 3 * b + n + 1)
                    dst = T0[n % 2][:, :].bitcast(BF16)
                    for c in range(8):
                        m = pe.transpose(dst[:, c * w:c * w + p], src[:, 2 * c:2 * c + 2, :].rearrange("p a d -> p (a d)"),
                                         ident_b[0:p, 0:p])
                    m.then_inc(t3_in_psum, 1)

            def scores(b, transposed):
                for j, (half, aux, odd) in enumerate(CHUNKS3):
                    p, n = 64 * odd, (T if aux else 128)
                    k = kaT3 if aux else kT3
                    if not transposed:
                        at_least(pe, *((exp3_done, 8 * b - 3 + j) if j < 4 else (max3_done, 8 * b + j - 3)))
                    else:
                        pe.wait_ge(*((max3_done, 8 * b + 5 + j) if j < 4 else (exp3_done, 8 * b + j - 3)))
                    for i in range(4):
                        c = 4 * half + i
                        if not transposed:
                            m = pe.matmul(RING3[j % 4][:, i * n:(i + 1) * n], qT3[p:p + PARTS3, c, :], k[p:p + PARTS3, c, 0:n],
                                          start=True, stop=True)
                        else:
                            m = pe.matmul(RING3[j % 4][0:n, i * 128:(i + 1) * 128], k[p:p + MAXES3, c, 0:n], qmT3[p:p + MAXES3, c, :],
                                          start=True, stop=True)
                    m.then_inc(sT3_in_psum if transposed else s3_in_psum, 1)

            pe.wait_ge(attn3_loaded, 7 * 16)
            pe.wait_ge(x_updated, 6 * B)
            tensor_xnT(pe, 48, 0, T0[0])
            tensor_xnT(pe, 49, 1, T0[1])
            project(0, 0)
            turn_stacks(0, 0, ((xnT_done, 49), (xnT_done, 50), (t3_done, 1)))

            def tile(b, u, more):
                pe.wait_ge(t3_done, 5 * b + 3)
                scores(b, False)
                if more >= 1:
                    project(b + 1, 1 - u)
                pe.wait_ge(maxcols3_done, b + 1)
                for c in range(8):
                    m = pe.transpose(T0[0][:, :].bitcast(BF16)[:, c * 128:(c + 1) * 128],
                                     sq3[:, u, 2 * c:2 * c + 2, :].rearrange("p a d -> p (a d)"), ident_b[:, :])
                m.then_inc(t3_in_psum, 1)
                pe.wait_ge(t3_done, 5 * b + 4)
                scores(b, True)
                if more >= 2:
                    tensor_xnT(pe, b + 50, u, T0[1])
                if more >= 1:
                    turn_stacks(b + 1, 1 - u, ((t3_done, 5 * b + 4), (xnT_done, b + 51 if more >= 2 else 0), (t3_done, 5 * b + 5)))
                if more >= 1:
                    pe.wait_ge(proj3_done, 4 * b + 8)
                for j, (half, aux, odd) in enumerate(CHUNKS3):
                    pe.wait_ge(exp3_done, 8 * b + j + 1)
                    for h in range(8 * half + odd, 8 * half + 8, 2):
                        at = (16 * aux + h) * 9
                        e, v = (ea3, va3) if aux else (em3, v3)
                        m = pe.matmul(MISC3[:, at:at + 9], e[:, h, :], v[:, u, h, :], start=True, stop=True)
                m.then_inc(av3_in_psum, 1)
                pe.wait_ge(o3_done, b + 1)
                if more >= 1:
                    pe.wait_ge(t3_done, 5 * b + 6)
                pe.transpose(T0[1][:, 0:128], o3[:, :], ident[:, :]).then_inc(t3_in_psum, 1)
                pe.wait_ge(t3_done, 5 * b + (8 if more >= 1 else 5))
                pe.matmul(MISC3[:, 0:D], oT3[:, :], wo3[:, :], start=True, stop=False)
                pe.matmul(MISC3[:, 0:D], ones_row[:, :], bo3[:, :], start=False, stop=True).then_inc(wo3_in_psum, 1)
            over_tiles(pe, tile)

        def vector_attn3(dve):
            def projected(b, u):
                dve.wait_ge(qkv3_in_psum, b + 1)
                at_least(dve, split3_done, 3 * b)
                dve.tensor_tensor(qk3[:, :, :, :].rearrange("p a h d -> p (a h d)"), QKV3[:, 0:2 * D], bqkv3[:, 0:2 * D], ALU.add).then_inc(proj3_done, 1)
                dve.tensor_tensor(v3[:, u, :, 0:8], QKV3[:, 2 * D:3 * D].rearrange("p (h d) -> p h d", d=8),
                                  bqkv3[:, 2 * D:3 * D].rearrange("p (h d) -> p h d", d=8), ALU.add).then_inc(proj3_done, 1)
                dve.wait_ge(kva3_in_psum, b + 1)
                dve.tensor_tensor(ka3[:, :, :].rearrange("p h d -> p (h d)"), MISC3[0:T, 0:D], bkva3[:, 0:D], ALU.add).then_inc(proj3_done, 1)
                dve.tensor_tensor(va3[:, u, :, 0:8], MISC3[0:T, D:2 * D].rearrange("p (h d) -> p h d", d=8),
                                  bkva3[:, D:2 * D].rearrange("p (h d) -> p h d", d=8), ALU.add).then_inc(proj3_done, 1)

            vector_ln_stats(dve, 0, 64, 0, 6 * B)
            vector_ln_apply(dve, 0, 48, 0, None, 64)
            vector_ln_stats(dve, 1, 65, 1, 6 * B)
            vector_ln_apply(dve, 1, 49, 1, None, 65)
            dve.wait_ge(g3_tanh_done, 1)
            dve.tensor_scalar(gate3[:, 1, :], g3_tanh[:, :], 0.5, 0.5, ALU.mult, ALU.add).then_inc(g3_step, 1)
            dve.wait_ge(g3_step, 1)
            dve.tensor_scalar(gate3[:, 0, :], gate3[:, 1, :], -1.0, 1.0, ALU.mult, ALU.add).then_inc(g3_step, 1)
            dve.wait_ge(stack3_ready, 1)
            projected(0, 0)

            def tile(b, u, more):
                for j, (half, aux, odd) in enumerate(CHUNKS3):
                    n = T if aux else 128
                    dve.wait_ge(s3_in_psum, 8 * b + j + 1)
                    dve.tensor_reduce(mx3[:, aux, heads3(half, odd)], RING3[j % 4][:, 0:4 * n].rearrange("p (h k) -> p h k", k=n),
                                      AX.X, ALU.max, negate=True).then_inc(max3_done, 1)
                cols = sq3[:, u, :, PARTS3:MAXES3].rearrange("p h (a c) -> p h a c", c=3)
                m = mx3[:, :, :].rearrange("p a h -> p h a")
                left = mleft3[:, :, :].rearrange("p a h -> p h a")
                dve.wait_ge(max3_done, 8 * b + 8)
                dve.tensor_copy(cols[:, :, :, 0], m).then_inc(maxsplit3_step, 1)
                dve.wait_ge(maxsplit3_step, 3 * b + 1)
                dve.tensor_tensor(left, m, cols[:, :, :, 0], ALU.subtract).then_inc(maxsplit3_step, 1)
                dve.wait_ge(maxsplit3_step, 3 * b + 2)
                dve.tensor_copy(cols[:, :, :, 1], left).then_inc(maxsplit3_step, 1)
                dve.wait_ge(maxsplit3_step, 3 * b + 3)
                dve.tensor_tensor(cols[:, :, :, 2], left, cols[:, :, :, 1], ALU.subtract).then_inc(maxcols3_done, 1)
                if more >= 1:
                    projected(b + 1, 1 - u)
                if more >= 2:
                    vector_ln_stats(dve, b + 2, b + 66, u)
                    vector_ln_apply(dve, b + 2, b + 50, u, None, b + 66)
                av = MISC3[:, 0:32 * 9].rearrange("p (a h d) -> p a h d", a=2, d=9)
                dve.wait_ge(av3_in_psum, b + 1)
                dve.reciprocal(rs3[:, :, :], av[:, :, :, 8]).then_inc(o3_step, 1)
                dve.wait_ge(o3_step, 3 * b + 1)
                dve.tensor_tensor(rg3[:, :, :], rs3[:, :, :], gate3[:, :, :], ALU.mult).then_inc(o3_step, 1)
                dve.wait_ge(o3_step, 3 * b + 2)
                dve.tensor_tensor(ov3[:, :, :, :].rearrange("p a h d -> p (a h) d"), MISC3[:, 0:32 * 9].rearrange("p (h d) -> p h d", d=9)[:, :, 0:8],
                                  rg3[:, :, :].rearrange("p a h -> p (a h)").unsqueeze(2).to_broadcast([128, 32, 8]), ALU.mult).then_inc(o3_step, 1)
                dve.wait_ge(o3_step, 3 * b + 3)
                dve.tensor_tensor(o3[:, :], ov3[:, 0, :, :].rearrange("p h d -> p (h d)"), ov3[:, 1, :, :].rearrange("p h d -> p (h d)"),
                                  ALU.add).then_inc(o3_done, 1)
                dve.wait_ge(wo3_in_psum, b + 1)
                dve.scalar_tensor_tensor(slot(b), MISC3[:, 0:D], tg[:, 3:4], slot(b), ALU.mult, ALU.add).then_inc(x_updated, 1)
            over_tiles(dve, tile)

        def scalar_attn3(act):
            def stacks(b, count):
                for n, (dst, w) in enumerate(((qT3, 128), (kT3, 128), (kaT3, T + 1))):
                    act.wait_ge(t3_in_psum, count + n)
                    src = T0[n % 2][:, :].bitcast(BF16)[:, 0:8 * w].rearrange("p (c k) -> p c k", k=w)
                    k = min(w, 128) if n < 2 else T
                    act.activation(dst[:, :, 0:k], src[:, :, 0:k], ACT.Copy).then_inc(t3_done, 1)

            scalar_xnT(act, 48, 0, T0[0])
            scalar_xnT(act, 49, 1, T0[1])
            stacks(0, 1)

            def tile(b, u, more):
                act.wait_ge(t3_in_psum, 5 * b + 4)
                act.activation(qmT3[:, :, :].rearrange("p c k -> p (c k)"), T0[0][:, :].bitcast(BF16)[:, :], ACT.Copy).then_inc(t3_done, 1)
                for j, (half, aux, odd) in enumerate(CHUNKS3):
                    n = T if aux else 128
                    act.wait_ge(sT3_in_psum, 8 * b + j + 1)
                    act.activation((ea3 if aux else em3)[:, heads3(half, odd), :], RING3[j % 4][0:n, :].rearrange("p (h q) -> p h q", q=128),
                                   ACT.Exp, scale=8 ** -0.5).then_inc(exp3_done, 1)
                if more >= 2:
                    scalar_xnT(act, b + 50, u, T0[1])
                if more >= 1:
                    stacks(b + 1, 5 * b + 5)
                act.wait_ge(t3_in_psum, 5 * b + (8 if more >= 1 else 5))
                act.activation(oT3[:, :], T0[1][:, 0:128], ACT.Copy).then_inc(t3_done, 1)
            over_tiles(act, tile)

        def gpsimd_attn3(pool):
            pool.wait_ge(x_updated, 2 * B)
            pool.memset(sq3[:, :, :, :], 0.0)
            pool.memset(sk3[:, :, :], 0.0)
            pool.memset(sa3[:, :, :], 0.0)
            pool.memset(v3[:, :, :, 8:9], 1.0)
            pool.memset(va3[:, :, :, 8:9], 1.0).then_inc(stack3_zeroed, 1)
            pool.wait_ge(stack3_zeroed, 1)
            pool.memset(sk3[:, :, PARTS3:PARTS3 + 3], 1.0)
            pool.memset(sa3[:, :, PARTS3 + 3:MAXES3], 1.0).then_inc(stack3_ready, 1)
            pool.wait_ge(stack3_ready, 1)

            def context(b, u):
                at_least(pool, kva3_in_psum, b - 1)
                pool.tensor_copy(ctx_b[:, u, :], ctxT[:, bass.ds(b, 1), :].rearrange("p a t -> p (a t)")).then_inc(ctx_b_done, 1)

            def part(stack, n, slots):
                first, step, count = slots
                v = stack[:, :, 0:PARTS3].rearrange("p h (s d) -> p h s d", d=8)
                return v[:, :, first:first + step * (count - 1) + 1:step, :]

            def split(b, u):
                Q_AT = ((0, 1, 3), (3, 1, 2), (5, 1, 1))
                K_AT = ((0, 3, 2), (1, 3, 2), (2, 1, 1))
                work = ((qk3[:, 0], sq3[:, u], 128, Q_AT), (qk3[:, 1], sk3, 128, K_AT), (ka3[:, :, :], sa3, T, K_AT))
                pool.wait_ge(proj3_done, 4 * b + 3)
                for n, (x, stack, p, at) in enumerate(work):
                    left = left3[n][0:p, :, :]

                    def spread(src, slots):
                        return src.unsqueeze(2).to_broadcast([p, H3, slots[2], 8])

                    def nothing(slots):
                        return zero[0:p, :].unsqueeze(2).unsqueeze(3).to_broadcast([p, H3, slots[2], 8])
                    if n:
                        pool.tensor_copy(part(stack, n, (5, 1, 1))[:, :, 0, :], x)
                    pool.tensor_tensor(part(stack, n, at[0]), spread(x, at[0]), nothing(at[0]), ALU.add).then_inc(split3_step, 1)
                    pool.wait_ge(split3_step, 9 * b + 3 * n + 1)
                    pool.tensor_tensor(left, x, stack[:, :, 0:8], ALU.subtract).then_inc(split3_step, 1)
                    pool.wait_ge(split3_step, 9 * b + 3 * n + 2)
                    pool.tensor_tensor(part(stack, n, at[1]), spread(left, at[1]), nothing(at[1]), ALU.add).then_inc(split3_step, 1)
                    pool.wait_ge(split3_step, 9 * b + 3 * n + 3)
                    pool.tensor_tensor(part(stack, n, at[2])[:, :, 0, :], left, part(stack, n, at[1])[:, :, 0, :], ALU.subtract).then_inc(split3_done, 1)

            gpsimd_ln_rstd(pool, 64, 0)
            gpsimd_ln_rstd(pool, 65, 1)
            context(0, 0)
            context(1, 1)
            split(0, 0)

            def tile(b, u, more):
                if more >= 1:
                    split(b + 1, 1 - u)
                if more >= 2:
                    gpsimd_ln_rstd(pool, b + 66, u)
                    context(b + 2, u)
            over_tiles(pool, tile)

        D_BANK = bank[0:4]
        LOGITS3, PT_BANK = bank[6], bank[4]
        IN_BANK = bank[4:8]
        F_BANK = [bank[0:4], bank[4:8]]
        ROWS_BANK, COMB_BANK = bank[0:2], bank[2:4]

        def tensor_moe3(pe):
            pe.wait_ge(moe3_loaded, 4 * 16)
            pe.wait_ge(x_updated, 7 * B)
            tensor_g_xnT(pe, 8, bank[5])
            for g in range(4):
                pe.wait_ge(g_xnT_done, g + 9)
                pe.matmul(LOGITS3[:, :], ctrl3[:, :], xnT4[:, g % 2, :], start=True, stop=True).then_inc(l3_in_psum, 1)
                pe.wait_ge(perm3_done, g + 1)
                at_least(pe, pt3_done, g)
                for j in range(4):
                    tok = (4 * g + j) * 128
                    m = pe.transpose(PT_BANK[:, j * 128:(j + 1) * 128], perm3[:, tok:tok + 128], ident[:, :])
                m.then_inc(pt3_in_psum, 1)
                if g < 3:
                    tensor_g_xnT(pe, g + 9, bank[5])
                pe.wait_ge(pt3_done, g + 1)
                at_least(pe, d3_act_done, 2 * g)
                at_least(pe, d3_dve_done, 2 * g)
                for j in range(4):
                    for r in range(4):
                        p = slice(G3 * r, G3 * r + G3)
                        m = pe.matmul(D_BANK[r][:, j * 128:(j + 1) * 128], xn4[p, g % 2, j, :], pt3[p, g % 2, j, :], start=True, stop=True)
                m.then_inc(d3_in_psum, 1)
            pe.wait_ge(f1_loaded, 16)
            pe.wait_ge(d3_act_done, 8)
            pe.wait_ge(d3_dve_done, 8)
            for e in range(E3):
                for s_ in range(SETS3):
                    m = pe.matmul(IN_BANK[e // 8][F3 * s_:F3 * s_ + F3, (e % 8) * NG3:(e % 8 + 1) * NG3], f1_3[:, SETS3 * e + s_, :],
                                  d3[:, :, SETS3 * e + s_], start=True, stop=True)
                if e % 8 == 7:
                    m.then_inc(in3_in_psum, 1)
            for r in range(4):
                pe.wait_ge(in3_done, r + 1 if r % 2 == 0 else 4)
                if r >= 2:
                    pe.wait_ge(out3_act_done, 2 * (r - 1))
                    pe.wait_ge(out3_dve_done, 2 * (r - 1))
                for e in range(8 * r, 8 * r + 8):
                    for s_ in range(SETS3):
                        p = slice(F3 * s_, F3 * s_ + F3)
                        m = pe.matmul(F_BANK[r % 2][s_][:, (e % 8) * NG3:(e % 8 + 1) * NG3], f2_3[p, e, :], in3[p, e, :], start=True, stop=True)
                m.then_inc(f3_in_psum, 1)
            pe.wait_ge(out3_act_done, 8)
            pe.wait_ge(out3_dve_done, 8)

            def rows(b):
                at_least(pe, rows3_done, b - 1)
                for r in range(4):
                    m = pe.transpose(ROWS_BANK[b % 2][:, r * 128:(r + 1) * 128], out3[:, 4 * b + r, :], ident[:, :])
                m.then_inc(rows3_in_psum, 1)

            rows(0)
            for b in range(B):
                if b + 1 < B:
                    rows(b + 1)
                pe.wait_ge(rows3_done, b + 1)
                at_least(pe, x_updated, 7 * B + b - 1)
                for r in range(4):
                    tok = 128 * b + G3 * r
                    m = pe.matmul(COMB_BANK[b % 2][G3 * r:G3 * r + G3, 0:D], perm3[:, tok:tok + G3], rows3[:, b % 2, r, :], start=True, stop=True)
                m.then_inc(comb3_in_psum, 1)

        def d3_view(g, r):
            return d3[:, 16 * g + r:16 * g + 13 + r:4, :]

        def out3_view(r, s_):
            at = 8 * SETS3 * r + s_
            return out3[:, :, at:at + 7 * SETS3 + 1:SETS3].rearrange("p g e -> p e g")

        def vector_moe3(dve):
            steps = [0]

            def link(ins):
                steps[0] += 1
                ins.then_inc(tie3_step, 1)
                dve.wait_ge(tie3_step, steps[0])

            vector_g_stats(dve, 0, 8, 7 * B)
            vector_g_apply(dve, 0, 8)
            dve.wait_ge(moe3_loaded, 4 * 16)
            for g in range(4):
                if g < 3:
                    vector_g_stats(dve, g + 1, g + 9, 7 * B)
                dve.wait_ge(l3_in_psum, g + 1)
                lt = tmp512[:, g % 2, :].rearrange("p (g t) -> p g t", t=G3)
                link(dve.tensor_tensor(lt, LOGITS3[:, :].rearrange("p (g t) -> p g t", t=G3), tie3[:, :].unsqueeze(1).to_broadcast([128, 16, G3]), ALU.add))
                link(dve.tensor_reduce(gmax3[:, :], lt, AX.X, ALU.max))
                dve.tensor_tensor(perm3[:, g * 512:(g + 1) * 512].rearrange("p (g t) -> p g t", t=G3), lt,
                                  gmax3[:, :].unsqueeze(2).to_broadcast([128, 16, G3]), ALU.is_equal).then_inc(perm3_done, 1)
                if g < 3:
                    vector_g_apply(dve, g + 1, g + 9, g)
                dve.wait_ge(d3_in_psum, g + 1)
                for r in (2, 3):
                    dve.tensor_copy(d3_view(g, r), D_BANK[r][:, :].rearrange("p (j e) -> p j e", e=ES3)).then_inc(d3_dve_done, 1)
            for r in range(4):
                dve.wait_ge(in3_in_psum, r + 1)
                dve.tensor_tensor(in3[:, 8 * r:8 * r + 8, :], IN_BANK[r][:, :].rearrange("p (e g) -> p e g", g=NG3),
                                  bias3[:, 8 * r:8 * r + 8].unsqueeze(2).to_broadcast([128, 8, NG3]), ALU.add).then_inc(in3_biased, 1)
            for r in range(4):
                dve.wait_ge(f3_in_psum, r + 1)
                for s_ in (2, 3):
                    dve.tensor_copy(out3_view(r, s_), F_BANK[r % 2][s_][:, :].rearrange("p (e g) -> p e g", g=NG3)).then_inc(out3_dve_done, 1)
            for b in range(B):
                dve.wait_ge(comb3_in_psum, b + 1)
                dve.scalar_tensor_tensor(X[:, b, :], COMB_BANK[b % 2][:, 0:D], tg[:, 7:8], X[:, b, :], ALU.mult, ALU.add).then_inc(x_updated, 1)

        def scalar_moe3(act):
            scalar_g_xnT(act, 8, bank[5])
            for g in range(4):
                act.wait_ge(pt3_in_psum, g + 1)
                act.activation(pt3[:, g % 2, :, :].rearrange("p j e -> p (j e)"), PT_BANK[:, :], ACT.Copy).then_inc(pt3_done, 1)
                if g < 3:
                    scalar_g_xnT(act, g + 9, bank[5])
                act.wait_ge(d3_in_psum, g + 1)
                for r in (0, 1):
                    act.activation(d3_view(g, r), D_BANK[r][:, :].rearrange("p (j e) -> p j e", e=ES3), ACT.Copy).then_inc(d3_act_done, 1)
            for r in range(4):
                act.wait_ge(in3_biased, r + 1)
                v = in3[:, 8 * r:8 * r + 8, :]
                act.activation(v, v, ACT.Relu).then_inc(in3_done, 1)
            for r in range(4):
                act.wait_ge(f3_in_psum, r + 1)
                for s_ in (0, 1):
                    act.activation(out3_view(r, s_), F_BANK[r % 2][s_][:, :].rearrange("p (e g) -> p e g", g=NG3), ACT.Copy).then_inc(out3_act_done, 1)
            for b in range(B):
                act.wait_ge(rows3_in_psum, b + 1)
                at_least(act, comb3_in_psum, b - 1)
                act.activation(rows3[:, b % 2, :, :].rearrange("p r d -> p (r d)"), ROWS_BANK[b % 2][:, :], ACT.Copy).then_inc(rows3_done, 1)

        def gpsimd_moe3(pool):
            for k in range(8, 12):
                gpsimd_g_rstd(pool, k)

        @block.sync
        def _(sp):
            sp.dma_start(X[:, :, :], t["x"]).then_inc(x_loaded, 16)
            sp.dma_start(ident[:, :], t["ident"]).then_inc(const_loaded, 16)
            sp.dma_start(ident_b[:, :], t["ident_b"]).then_inc(const_loaded, 16)
            sp.dma_start(gates_in[:, :], t["gates"]).then_inc(const_loaded, 16)
            sp.dma_start(ones[:, :], t["ones"]).then_inc(const_loaded, 16)
            sp.dma_start(ctxT[:, :, :], t["ctxT"]).then_inc(ctx_loaded, 16)
            sp.dma_start(wq0[:, :], t["wq0"]).then_inc(wqkv0_loaded, 16)
            sp.dma_start(bq0[:, :], t["bq0"]).then_inc(wqkv0_loaded, 16)
            sp.dma_start(bk0[:, :], t["bk0"]).then_inc(wqkv0_loaded, 16)
            sp.dma_start(wk0[:, :], t["wk0"]).then_inc(wqkv0_loaded, 16)
            sp.dma_start(wv0[:, :], t["wv0"]).then_inc(wqkv0_loaded, 16)
            sp.dma_start(bv0[:, :, :], t["bv0"]).then_inc(wqkv0_loaded, 16)
            sp.dma_start(wo0[:, :, :], t["wo0"]).then_inc(wo0_loaded, 16)
            sp.dma_start(bo0[:, :], t["bo0"]).then_inc(wo0_loaded, 16)
            for name, dst in (("wg0", wg0), ("rank_w", rank_w), ("slot_base", slot_base), ("spare_slot", spare_slot),
                              ("tri_b", tri_b), ("ones_b", ones_b)):
                sp.dma_start(dst[:, :], t[name]).then_inc(route0_loaded, 16)
            sp.wait_ge(zero_ready, 1)
            sp.dma_start(t["x_slots"][0:NT, :].rearrange("(t p) d -> p t d", p=128), XN[:, :, :]).then_inc(slots_zeroed, 16)
            for dst, name in ((w1x, "w1x"), (w2x, "w2x"), (bx, "bx")):
                sp.dma_start(dst[:, :], t[name]).then_inc(mix_loaded, 16)
            for g in range(2):
                sp.dma_start(wgu1[:, g, 0:2, :], t["wgu1"][g, 0:256, :].rearrange("(c p) d -> p c d", p=128)).then_inc(ffn1_loaded, 16)
            sp.dma_start(wgu1[0:I1 - 256, :, 2, :], t["wgu1"][:, 256:I1, :].rearrange("g p d -> p g d")).then_inc(ffn1_loaded, 16)
            sp.dma_start(wd1[:, :], t["wd1"]).then_inc(ffn1_loaded, 16)
            sp.dma_start(clips[:, :], t["clips"]).then_inc(ffn1_loaded, 16)
            for dst, name in ((wqkv2[:, :, :], "wqkv2"), (bqk2[:, 0:1], "bq2"), (bqk2[:, 1:2], "bk2"), (bv2[:, :], "bv2")):
                sp.dma_start(dst, t[name]).then_inc(attn2_loaded, 16)
            for dst, name in ((rw2[:, :], "rw2"), (rb2[:, :], "rb2"), (pair_sel[:, :, :], "pair_sel")):
                sp.dma_start(dst, t[name]).then_inc(moe2_loaded, 16)
            for dst, name in ((wqkv3, "wqkv3"), (wkva3, "wkva3"), (bqkv3, "bqkv3"), (bkva3, "bkva3"), (wo3, "wo3"), (bo3, "bo3"), (g3, "g3")):
                sp.dma_start(dst[:, :], t[name]).then_inc(attn3_loaded, 16)
            for dst, name in ((f2_3[:, :, :], "f2_3"), (ctrl3[:, :], "ctrl3"), (tie3[:, :], "tie3"), (bias3[:, :], "bias3")):
                sp.dma_start(dst, t[name]).then_inc(moe3_loaded, 16)
            sp.wait_ge(x_updated, B)
            for dst, name in ((w13_2[:, :, :, :], "w13_2"), (w2_2[:, :, :], "w2_2")):
                sp.dma_start(dst, t[name]).then_inc(moe2_loaded, 16)
            if LAST_STAGE >= 2:
                sync_moe0(sp)
            if LAST_STAGE >= 8:
                sp.wait_ge(x_updated, 6 * B)
                sp.dma_start(f1_3, t["f1_3"]).then_inc(f1_loaded, 16)
            sp.wait_ge(x_updated, 16 * LAST_STAGE)
            sp.dma_start(t["out"], X[:, :, :]).then_inc(out_stored, 16)
            sp.wait_ge(out_stored, 16)

        @block.gpsimd
        def _(pool):
            pool.memset(XN[:, :, :], 0.0).then_inc(zero_ready, 1)
            pool.memset(minus_half[:, :], -0.5)
            pool.memset(zero[:, :], 0.0)
            pool.memset(minus_magic[:, :], -MAGIC)
            pool.memset(eps[:, :], LN_EPS).then_inc(pool_ready, 1)
            pool.memset(kT[:, :, :], 0.0)
            pool.memset(v0[:, :, :, DK0:DK0 + 1], 1.0).then_inc(pool_ready, 1)
            pool.wait_ge(mask_loaded, 16)
            pool.tensor_scalar(mask_bias[:, :, :], mask_u8[:, :, :], -MASKED, MASKED, ALU.mult, ALU.add).then_inc(pool_ready, 1)
            gpsimd_attn0(pool)
            pool.wait_ge(slots_zeroed, 16)
            if LAST_STAGE >= 2:
                gpsimd_moe0(pool)
            if LAST_STAGE >= 3:
                gpsimd_mix1(pool)
            if LAST_STAGE >= 5:
                gpsimd_attn2(pool)
            if LAST_STAGE >= 6:
                gpsimd_moe2(pool)
            if LAST_STAGE >= 7:
                gpsimd_attn3(pool)
            if LAST_STAGE >= 8:
                gpsimd_moe3(pool)

        @block.scalar
        def _(act):
            act.dma_start(mask_u8[:, :, :], t["mask"]).then_inc(mask_loaded, 16)
            act.wait_ge(const_loaded, 4 * 16)
            act.activation(tg[:, :], gates_in[:, :], ACT.Tanh).then_inc(tg_ready, 1)
            act.wait_ge(ffn1_loaded, 5 * 16)
            act.activation(clip_tanh[:, :], clips[:, :], ACT.Tanh, scale=0.5).then_inc(clip_tanh_done, 1)
            act.wait_ge(attn3_loaded, 7 * 16)
            act.activation(g3_tanh[:, :], g3[:, :], ACT.Tanh, scale=0.5).then_inc(g3_tanh_done, 1)
            scalar_attn0(act)
            if LAST_STAGE >= 2:
                scalar_moe0(act)
            if LAST_STAGE >= 3:
                scalar_mix1(act)
            if LAST_STAGE >= 4:
                scalar_ffn1(act)
            if LAST_STAGE >= 5:
                scalar_attn2(act)
            if LAST_STAGE >= 6:
                scalar_moe2(act)
            if LAST_STAGE >= 7:
                scalar_attn3(act)
            if LAST_STAGE >= 8:
                scalar_moe3(act)

        @block.vector
        def _(dve):
            vector_attn0(dve)
            if LAST_STAGE >= 2:
                vector_moe0(dve)
            if LAST_STAGE >= 3:
                vector_mix1(dve)
            if LAST_STAGE >= 4:
                vector_ffn1(dve)
            if LAST_STAGE >= 5:
                vector_attn2(dve)
            if LAST_STAGE >= 6:
                vector_moe2(dve)
            if LAST_STAGE >= 7:
                vector_attn3(dve)
            if LAST_STAGE >= 8:
                vector_moe3(dve)

        @block.tensor
        def _(pe):
            tensor_attn0(pe)
            if LAST_STAGE >= 2:
                tensor_moe0(pe)
            if LAST_STAGE >= 3:
                tensor_mix1(pe)
            if LAST_STAGE >= 4:
                tensor_ffn1(pe)
            if LAST_STAGE >= 5:
                tensor_attn2(pe)
            if LAST_STAGE >= 6:
                tensor_moe2(pe)
            if LAST_STAGE >= 7:
                tensor_attn3(pe)
            if LAST_STAGE >= 8:
                tensor_moe3(pe)


def kernel(**inputs):
    import numpy as np
    from concourse.bass_utils import run_bass_kernel_spmd

    a = {k: np.asarray(v) for k, v in inputs.items()}

    def rows(v, n):
        v = np.asarray(v)
        return np.broadcast_to(v.reshape(1, -1), (n, v.size))

    def pairs(routed, shared):
        both = np.concatenate([routed, shared])
        return both.reshape(5, 2, *both.shape[1:])

    ins = {
        "x": a["x"].transpose(1, 0, 2),
        "ctxT": a["ctx_1024"].transpose(2, 0, 1),
        "mask": a["mask_BxSxS2_bk1"].transpose(1, 0, 2),
        "ident": np.eye(128, dtype=np.float32),
        "ident_b": np.eye(128, dtype=mybir.dt.np(BF16)),
        "ones": np.ones((128, 128), np.float32),
        "gates": rows(np.concatenate([a["g_xattn"], a["g_ffn"]]), 128),
        "wq0": a["L0_xattn_wq"].transpose(1, 0, 2).reshape(128, 1024),
        "wk0": a["L0_xattn_wk"].transpose(1, 0, 2).reshape(128, 1024),
        "wv0": a["L0_xattn_wv"].transpose(1, 0, 2).reshape(128, 1024),
        "wo0": a["L0_xattn_wo"].reshape(8, 128, 128).transpose(1, 0, 2),
        "bq0": a["L0_xattn_bq"].reshape(8, 128).T,
        "bk0": a["L0_xattn_bk"].reshape(8, 128).T,
        "bv0": rows(a["L0_xattn_bv"], T).reshape(T, H0, DK0),
        "bo0": a["L0_xattn_bo"].reshape(1, 128),
        "wg0": a["L0_ffn_wg"],
        "w1x": a["L1_xattn_W"][:, :D].T,
        "w2x": a["L1_xattn_W"][:, D:].T,
        "bx": a["L1_xattn_b"].reshape(1, D),
        "wgu1": np.stack([a["L1_ffn_w_gate"], a["L1_ffn_w_up"]]),
        "wd1": a["L1_ffn_w_down"],
        "wqkv2": np.stack([a["L2_xattn_Wq"], a["L2_xattn_Wk"], a["L2_xattn_Wv"]]).transpose(1, 0, 2),
        "bq2": a["L2_xattn_bq"].reshape(D, 1),
        "bk2": a["L2_xattn_bk"].reshape(D, 1),
        "bv2": rows(a["L2_xattn_bv"], T),
        "rw2": a["L2_ffn_router_w"],
        "rb2": a["L2_ffn_router_b"].reshape(1, E2),
        "w13_2": np.stack([pairs(a[f"L2_ffn_routed_{w}"], a[f"L2_ffn_shared_{w}"]).transpose(2, 0, 1, 3).reshape(D, 5, 128)
                           for w in ("w1", "w3")], axis=1),
        "w2_2": pairs(a["L2_ffn_routed_w2"], a["L2_ffn_shared_w2"]).reshape(5, 128, D).transpose(1, 0, 2),
        "pair_sel": 0.5 * np.kron(np.eye(E2, dtype=np.float32), np.ones((1, H2), np.float32)).reshape(E2, 4, 128),
        "wqkv3": a["L3_xattn_Wqkv"],
        "wkva3": a["L3_xattn_Wqkv_aux"][:, D:],
        "bqkv3": rows(a["L3_xattn_bqkv"], 128),
        "bkva3": rows(a["L3_xattn_bqkv_aux"][D:], T),
        "wo3": a["L3_xattn_Wo"],
        "bo3": a["L3_xattn_bo"].reshape(1, D),
        "g3": rows(a["L3_xattn_g"], 128),
        "f1_3": a["L3_ffn_f1"].reshape(D, ES3, F3),
        "f2_3": a["L3_ffn_f2"].transpose(1, 2, 0, 3).reshape(SETS3 * F3, E3, D),
        "ctrl3": a["L3_ffn_controller"].reshape(D, ES3),
        "tie3": rows(np.linspace(0.0, 1e-06, G3, dtype=np.float32), 128),
        "bias3": a["L3_ffn_bias"].transpose(1, 2, 0).reshape(SETS3 * F3, E3),
        "clips": rows(np.concatenate([a["L1_ffn_clip_x"], a["L1_ffn_clip_down"]]), 128),
        "rank_w": rows(np.arange(E0, 0, -1, dtype=np.float32), 128),
        "slot_base": rows(np.arange(E0, dtype=np.float32) * C0 - 1, 128),
        "spare_slot": NT + np.arange(NT, dtype=np.float32).reshape(B, 128).T,
        "tri_b": np.triu(np.ones((128, 128))).astype(mybir.dt.np(BF16)),
        "ones_b": np.ones((128, 128)).astype(mybir.dt.np(BF16)),
        "w1_0": a["L0_ffn_w1"],
        "w2_0": a["L0_ffn_w2"],
        "b1_0": a["L0_ffn_b1"].reshape(E0, FC0, 128).transpose(0, 2, 1),
        "b2_0": a["L0_ffn_b2"].reshape(E0, 1, D),
    }
    ins = {k: np.ascontiguousarray(v) for k, v in ins.items()}
    nc = bacc.Bacc("TRN2", target_bir_lowering=False, num_devices=1)
    t = {k: nc.dram_tensor(f"in_{k}", v.shape, mybir.dt.from_np(v.dtype), kind="ExternalInput").ap() for k, v in ins.items()}
    t["out"] = nc.dram_tensor("out", (S, B, D), F32, kind="ExternalOutput").ap()
    t["x_slots"] = nc.dram_tensor("x_slots", (2 * NT, D), F32, kind="Internal").ap()
    t["y_slots"] = nc.dram_tensor("y_slots", (NT, D), F32, kind="Internal").ap()
    build(nc, t)
    r = run_bass_kernel_spmd(nc, [{f"in_{k}": v for k, v in ins.items()}], core_ids=[0])
    return np.ascontiguousarray(r.results[0]["out"].transpose(1, 0, 2))
```

```python
import concourse.bass as bass
import concourse.bacc as bacc
from concourse import mybir
from contextlib import ExitStack

LAST_STAGE = 8

F32 = mybir.dt.float32
BF16 = mybir.dt.bfloat16
U8 = mybir.dt.uint8
I32 = mybir.dt.int32
ALU = mybir.AluOpType
ACT = mybir.ActivationFunctionType
AX = mybir.AxisListType

B, S, D = 16, 128, 128
T = 77
H0, DK0 = 16, 64
E0, F0, C0 = 8, 512, 256
FC0 = F0 // 128
NT = B * S
E2, H2 = 8, 64
H3 = 16
PARTS3 = 48
MAXES3 = PARTS3 + 6
E3, SETS3, F3 = 32, 4, 32
ES3 = E3 * SETS3
G3 = 32
NG3 = B * S // G3
I1 = 352
ROWS1 = [(0, 128), (128, 256), (256, I1)]
QMAX = 127.0
DROW_STEP, XINV_STEP, GUSCALE_STEP, HINV_STEP = 6, 9, 10, 17
MAGIC = 1.5 * 2 ** 23
AREA_A, AREA_B = 15400, 9600
MASKED = -float(2 ** 100)
LN_EPS = 1e-5


def at_least(engine, sem, value):
    if not (isinstance(value, int) and value <= 0):
        engine.wait_ge(sem, value)


def over_tiles(engine, body, tail=1):
    body(0, 0, 2 * tail)
    body(1, 1, 2 * tail)
    with engine.Fori(1, B // 2 - tail) as i:
        body(i * 2, 0, 2 * tail)
        body(i * 2 + 1, 1, 2 * tail)
    for b in range(B - 2 * tail, B):
        body(b, b % 2, B - 1 - b)


def build(nc, t):
    ctx = ExitStack()
    with ctx:
        def sb(name, shape, dt=F32):
            return ctx.enter_context(nc.sbuf_tensor(name, shape, dt))

        def sem(name):
            return ctx.enter_context(nc.semaphore(name))

        area = {"A": sb("area_a", [128, AREA_A]), "B": sb("area_b", [128, AREA_B])}

        def carve(which, sizes, p=128, dt=F32):
            at, shape = sizes
            n = 1
            for d in shape:
                n *= d
            words = n if dt == F32 else n // 2
            v = area[which][0:p, at[0]:at[0] + words]
            at[0] += words
            assert at[0] <= (AREA_A if which == "A" else AREA_B), at[0]
            if dt != F32:
                v = v.bitcast(dt)
            names = "abcd"[:len(shape)]
            return v.rearrange(f"p ({' '.join(names)}) -> p {' '.join(names)}", **dict(zip(names, shape))) if len(shape) > 1 else v

        bank = [ctx.enter_context(nc.psum_tensor(f"bank{i}", [128, 512], F32)) for i in range(8)]

        X = sb("X", [128, B, D])
        ident = sb("ident", [128, 128])
        ident_b = sb("ident_b", [128, 128], BF16)
        ones = sb("ones", [128, 128])
        ones_row = ones[0:1, :]
        gates_in = sb("gates_in", [128, 8])
        tg = sb("tg", [128, 8])
        ctxT = sb("ctxT", [128, B, T])
        mask_u8 = sb("mask_u8", [128, B, T], U8)
        mask_bias = sb("mask_bias", [128, B, T], BF16)
        ln_stats = sb("ln_stats", [128, 3, 6])
        ln_mv = sb("ln_mv", [128, 3, 2])
        ln_veps = sb("ln_veps", [128, 3])
        ln_rstd = sb("ln_rstd", [128, 3])
        eps = sb("eps", [128, 1])
        zero = sb("zero", [128, 1])
        scrap = sb("scrap", [128, 6])
        minus_half = sb("minus_half", [128, 1])
        xn = sb("xn", [128, 2, D])
        xnT = sb("xnT", [128, 2, 128])
        ctx_b = sb("ctx_b", [128, 2, T])
        at0, at1, at2, at_moe = [0], [0], [0], [0]
        wq0 = carve("A", (at0, (H0 * DK0,)), 128)
        wk0 = carve("A", (at0, (H0 * DK0,)), 128)
        wv0 = carve("A", (at0, (H0 * DK0,)), 128)
        wo0 = carve("A", (at0, (8, D,)), 128)
        bq0 = sb("bq0", [128, 8])
        bk0 = sb("bk0", [128, 8])
        bv0 = carve("A", (at0, (H0, DK0,)), T)
        bo0 = sb("bo0", [1, D])
        qT = carve("A", (at0, (8, 128,)), 128)
        kT = carve("A", (at0, (H0, T,)), 128)
        v0 = carve("A", (at0, (2, H0, DK0,)), T)
        e0 = carve("A", (at0, (H0, T,)), 128)
        mx0 = sb("mx0", [128, H0])
        eT0 = carve("A", (at0, (H0, 128,)), T)
        sum0 = sb("sum0", [128, H0])
        rs0 = sb("rs0", [128, H0])
        oT0 = carve("A", (at0, (8, 128,)), 128)

        XN = sb("XN", [128, B, D])
        wg0 = sb("wg0", [128, E0])
        r0 = {k: sb(f"r0_{k}", [128, B, E0]) for k in ("exp", "gate", "rank", "keep", "at", "gkeep")}
        r0s = {k: sb(f"r0_{k}", [128, B]) for k in ("max", "sum", "rsum", "gmax", "rmax", "slot", "kept", "gsel", "weight", "alt", "alt2")}
        first0 = sb("first0", [128, B, E0], BF16)
        scatter_at = sb("scatter_at", [128, B], I32)
        gather_at = sb("gather_at", [128, B], I32)
        rank_w = sb("rank_w", [128, E0])
        slot_base = sb("slot_base", [128, E0])
        spare_slot = sb("spare_slot", [128, B])
        tri_b = sb("tri_b", [128, 128], BF16)
        ones_b = sb("ones_b", [128, 128], BF16)
        w1e = carve("B", (at_moe, (2, F0,)), 128)
        w2e = carve("B", (at_moe, (2, FC0, D,)), 128)
        b1e = sb("b1e", [128, 2, FC0])
        b2e = sb("b2e", [1, 2, D])
        xe = carve("B", (at_moe, (2, 2, D,)), 128)
        xeT = carve("B", (at_moe, (2, 2 * 128,)), 128)
        hT0 = carve("B", (at_moe, (2, FC0, 2 * 128,)), 128)
        ye = carve("B", (at_moe, (2, 2, D,)), 128)

        w1x = sb("w1x", [128, D])
        w2x = sb("w2x", [128, D])
        bx = sb("bx", [1, D])
        ctx_mean = sb("ctx_mean", [128, B])
        ctx_sum = sb("ctx_sum", [128, B])
        mix_row = sb("mix_row", [1, B * D])
        absmax1 = sb("absmax1", [128, B])
        clips = sb("clips", [128, 2])
        clip_tanh = sb("clip_tanh", [128, 2])
        clip_sig = sb("clip_sig", [128, 2])
        minus_magic = sb("minus_magic", [128, 1])
        wgu1 = sb("wgu1", [128, 2, 3, D])
        wd1 = sb("wd1", [128, I1])
        wmax1 = sb("wmax1", [128, 7])
        wscale1 = sb("wscale1", [128, 7])
        winv1 = sb("winv1", [128, 7])
        wguT1 = sb("wguT1", [128, 2, I1], BF16)
        wdT1 = sb("wdT1", [128, 3, D], BF16)
        dscale1 = sb("dscale1", [128, D])
        drow1 = sb("drow1", [128, D])
        col1 = {k: sb(f"col1_{k}", [128, 1]) for k in ("xmax", "xscale", "xinv", "hmax", "hscale", "hinv", "out")}
        cell1 = sb("cell1", [1, 2])
        guscale1 = sb("guscale1", [128, 2, 3])
        xq1 = sb("xq1", [128, 4, D])
        xqT1 = sb("xqT1", [128, 2, 512], BF16)
        silu1 = carve("A", (at1, (3, 512,)), 128)
        h1 = carve("A", (at1, (3, NT)), 128)
        hq1 = carve("A", (at1, (3, NT,)), 128, BF16)
        hmax1 = sb("hmax1", [128, 12])
        tmp512 = sb("tmp512", [128, 2, 512])

        g_stats = sb("g_stats", [128, 2, 4, 6])
        g_mv = sb("g_mv", [128, 2, 4, 2])
        g_veps = sb("g_veps", [128, 2, 4])
        g_rstd = sb("g_rstd", [128, 2, 4])
        xn4 = sb("xn4", [128, 2, 4, D])
        xnT4 = sb("xnT4", [128, 2, 512])
        wqkv2 = sb("wqkv2", [128, 3, D])
        bqk2 = sb("bqk2", [128, 2])
        bv2 = sb("bv2", [T, D])
        kT2 = carve("A", (at2, (B, T,)), 128)
        v2 = carve("A", (at2, (B, D,)), T)
        qT2 = carve("A", (at2, (512,)), 128)
        e2 = sb("e2", [128, 4, T])
        eT2 = carve("A", (at2, (512,)), T)
        s2 = {k: sb(f"s2_{k}", [128, 4]) for k in ("max", "sum", "rsum", "out")}
        rw2 = sb("rw2", [128, E2])
        rb2 = sb("rb2", [1, E2])
        at_w2 = [13000]
        w13_2 = carve("A", (at_w2, (2, 5, 128)), 128)
        w2_2 = carve("A", (at_w2, (5, D)), 128)
        pair_sel = sb("pair_sel", [E2, 4, 128])
        r2 = {k: sb(f"r2_{k}", [128, 4, E2]) for k in ("rank", "rank2", "first", "second", "rest", "a", "b", "gate")}
        r2s = {k: sb(f"r2s_{k}", [128, 4]) for k in ("m1", "r1", "m2", "r2", "d", "e", "den", "g1", "g2")}
        gT2 = sb("gT2", [E2, 512])
        th2 = carve("A", (at2, (2, 512,)), 128)
        u2 = carve("A", (at2, (2, 512,)), 128)
        h2 = carve("A", (at2, (5, 512,)), 128)

        at3 = [0]
        em3 = carve("B", (at3, (H3, 128)), 128)
        ea3 = carve("B", (at3, (H3, 128)), T)
        sq3 = carve("B", (at3, (2, H3, 64)), 128, BF16)
        sk3 = carve("B", (at3, (H3, 64)), 128, BF16)
        sa3 = carve("B", (at3, (H3, 64)), T, BF16)
        qT3 = carve("B", (at3, (8, 128)), 128, BF16)
        qmT3 = carve("B", (at3, (8, 128)), 128, BF16)
        at3a = [0]
        kT3 = carve("A", (at3a, (2, 8, 128)), 128, BF16)
        kaT3 = carve("A", (at3a, (2, 8, T + 1)), 128, BF16)
        wqkv3 = sb("wqkv3", [128, 3 * D])
        wkva3 = sb("wkva3", [128, 2 * D])
        bqkv3 = sb("bqkv3", [128, 3 * D])
        bkva3 = sb("bkva3", [T, 2 * D])
        wo3 = sb("wo3", [128, D])
        bo3 = sb("bo3", [1, D])
        g3 = sb("g3", [128, H3])
        g3_tanh = sb("g3_tanh", [128, H3])
        gate3 = sb("gate3", [128, 2, H3])
        qk3 = sb("qk3", [128, 2, H3, 8])
        ka3 = sb("ka3", [T, H3, 8])
        v3 = carve("A", (at3a, (2, H3, 32)), 128)
        va3 = carve("A", (at3a, (2, H3, 32)), T)
        ovT3 = carve("A", (at3a, (2, 4, 128)), 128)
        left3 = [sb(f"left3_{i}", [128, H3, 8]) for i in range(3)]
        mx3 = sb("mx3", [128, 2, H3])
        mleft3 = sb("mleft3", [128, 2, H3])
        rs3 = sb("rs3", [128, 2, H3])
        rg3 = sb("rg3", [128, 2, H3])
        ov3 = sb("ov3", [128, 2, H3, 8])
        o3 = sb("o3", [128, D])
        oT3 = sb("oT3", [128, 128])

        at4, at5 = [0], [0]
        d3 = carve("A", (at4, (NG3, ES3)), 128)
        f1_3 = carve("A", (at4, (ES3, F3)), 128)
        in3 = carve("A", (at4, (E3, NG3)), 128)
        out3 = carve("B", (at5, (NG3, ES3)), 128)
        perm3 = XN[:, :, :].rearrange("p b d -> p (b d)")
        f2_3 = sb("f2_3", [128, E3, D])
        ctrl3 = sb("ctrl3", [128, ES3])
        tie3 = sb("tie3", [128, G3])
        bias3 = sb("bias3", [128, E3])
        gmax3 = sb("gmax3", [128, 16])
        pt3 = carve("B", (at5, (2, 4, ES3)), 128)
        rows3 = carve("A", (at4, (2, 4, D)), 128)

        x_loaded = sem("x_loaded")
        const_loaded = sem("const_loaded")
        ctx_loaded = sem("ctx_loaded")
        mask_loaded = sem("mask_loaded")
        wqkv0_loaded = sem("wqkv0_loaded")
        wo0_loaded = sem("wo0_loaded")
        out_stored = sem("out_stored")
        pool_ready = sem("pool_ready")
        tg_ready = sem("tg_ready")
        stats_done = sem("stats_done")
        var_done = sem("var_done")
        veps_done = sem("veps_done")
        rstd_done = sem("rstd_done")
        xn_done = sem("xn_done")
        xnT_in_psum = sem("xnT_in_psum")
        xnT_done = sem("xnT_done")
        ctx_b_done = sem("ctx_b_done")
        x_updated = sem("x_updated")
        proj_in_psum = sem("proj_in_psum")
        proj_done = sem("proj_done")
        scores_in_psum = sem("scores_in_psum")
        max_done = sem("max_done")
        shifted_done = sem("shifted_done")
        exp_done = sem("exp_done")
        turn_in_psum = sem("turn_in_psum")
        turn_done = sem("turn_done")
        av_in_psum = sem("av_in_psum")
        sums_done = sem("sums_done")
        probs_done = sem("probs_done")
        av_done = sem("av_done")
        wo_in_psum = sem("wo_in_psum")
        route0_loaded = sem("route0_loaded")
        xn_kept = sem("xn_kept")
        logits_in_psum = sem("logits_in_psum")
        route_step = sem("route_step")
        route_exp = sem("route_exp")
        first_done = sem("first_done")
        rank_in_psum = sem("rank_in_psum")
        places_done = sem("places_done")
        slots_zeroed = sem("slots_zeroed")
        scattered = sem("scattered")
        expert_loaded = [sem(f"expert_loaded{i}") for i in range(2)]
        xeT_in_psum = sem("xeT_in_psum")
        xeT_done = sem("xeT_done")
        h_in_psum = sem("h_in_psum")
        h_done = sem("h_done")
        y_in_psum = sem("y_in_psum")
        y_done = sem("y_done")
        y_stored = [sem(f"y_stored{i}") for i in range(2)]
        gathered = [sem(f"gathered{i}") for i in range(4)]
        mix_loaded = sem("mix_loaded")
        ctx_mean_done = sem("ctx_mean_done")
        mix_row_in_psum = sem("mix_row_in_psum")
        mix_row_done = sem("mix_row_done")
        mix_in_psum = sem("mix_in_psum")
        absmax_done = sem("absmax_done")
        norm1_done = sem("norm1_done")
        ffn1_loaded = sem("ffn1_loaded")
        quant_step = sem("quant_step")
        clip_tanh_done = sem("clip_tanh_done")
        w_rounded = sem("w_rounded")
        wT_in_psum = sem("wT_in_psum")
        wT_done = sem("wT_done")
        drow_in_psum = sem("drow_in_psum")
        colmax_done = sem("colmax_done")
        maxrow_in_psum = sem("maxrow_in_psum")
        cell_done = sem("cell_done")
        max_in_psum = sem("max_in_psum")
        xq_done = sem("xq_done")
        xqT_in_psum = sem("xqT_in_psum")
        xqT_done = sem("xqT_done")
        gu_in_psum = sem("gu_in_psum")
        silu_done = sem("silu_done")
        h1_done = sem("h1_done")
        hq_rounded = sem("hq_rounded")
        hq_done = sem("hq_done")
        down_in_psum = sem("down_in_psum")
        g_stats_done = sem("g_stats_done")
        moe3_loaded = sem("moe3_loaded")
        f1_loaded = sem("f1_loaded")
        l3_in_psum = sem("l3_in_psum")
        tie3_step = sem("tie3_step")
        perm3_done = sem("perm3_done")
        pt3_in_psum = sem("pt3_in_psum")
        pt3_done = sem("pt3_done")
        d3_in_psum = sem("d3_in_psum")
        d3_act_done = sem("d3_act_done")
        d3_dve_done = sem("d3_dve_done")
        in3_in_psum = sem("in3_in_psum")
        in3_biased = sem("in3_biased")
        in3_done = sem("in3_done")
        f3_in_psum = sem("f3_in_psum")
        out3_act_done = sem("out3_act_done")
        out3_dve_done = sem("out3_dve_done")
        rows3_in_psum = sem("rows3_in_psum")
        rows3_done = sem("rows3_done")
        comb3_in_psum = sem("comb3_in_psum")
        attn3_loaded = sem("attn3_loaded")
        qkv3_in_psum = sem("qkv3_in_psum")
        proj3_done = sem("proj3_done")
        v3_done = sem("v3_done")
        split3_step = sem("split3_step")
        split3_done = sem("split3_done")
        stack3_ready = sem("stack3_ready")
        t3_in_psum = sem("t3_in_psum")
        t3_done = sem("t3_done")
        s3_in_psum = sem("s3_in_psum")
        max3_done = sem("max3_done")
        maxsplit3_step = sem("maxsplit3_step")
        maxcols3_done = sem("maxcols3_done")
        sT3_in_psum = sem("sT3_in_psum")
        exp3_done = sem("exp3_done")
        av3_in_psum = sem("av3_in_psum")
        ovT3_done = sem("ovT3_done")
        o3_step = sem("o3_step")
        o3_done = sem("o3_done")
        wo3_in_psum = sem("wo3_in_psum")
        g3_tanh_done = sem("g3_tanh_done")
        g_var_done = sem("g_var_done")
        g_veps_done = sem("g_veps_done")
        g_rstd_done = sem("g_rstd_done")
        g_xn_done = sem("g_xn_done")
        g_xnT_in_psum = sem("g_xnT_in_psum")
        g_xnT_done = sem("g_xnT_done")
        attn2_loaded = sem("attn2_loaded")
        kv2_in_psum = sem("kv2_in_psum")
        k2_done = sem("k2_done")
        v2_done = sem("v2_done")
        q2_in_psum = sem("q2_in_psum")
        q2_done = sem("q2_done")
        s2_in_psum = sem("s2_in_psum")
        shift2_done = sem("shift2_done")
        exp2_done = sem("exp2_done")
        eT2_in_psum = sem("eT2_in_psum")
        eT2_done = sem("eT2_done")
        av2_in_psum = sem("av2_in_psum")
        a2_step = sem("a2_step")
        moe2_loaded = sem("moe2_loaded")
        logits2_in_psum = sem("logits2_in_psum")
        route2_step = sem("route2_step")
        gap2_done = sem("gap2_done")
        gap2_exp = sem("gap2_exp")
        gates2_done = sem("gates2_done")
        gT2_in_psum = sem("gT2_in_psum")
        gT2_done = sem("gT2_done")
        ab2_in_psum = sem("ab2_in_psum")
        g2_in_psum = sem("g2_in_psum")
        tanh2_done = sem("tanh2_done")
        mul2_step = sem("mul2_step")
        h2_done = sem("h2_done")
        out2_in_psum = sem("out2_in_psum")

        block = ctx.enter_context(nc.Block())

        def slot(b):
            return X[:, bass.ds(b, 1), :].rearrange("p a d -> p (a d)")

        def vector_ln_stats(dve, b, n, u, updates=0):
            if not (isinstance(updates, int) and updates == 0):
                dve.wait_ge(x_updated, updates)
            if not isinstance(updates, int):
                dve.memset(scrap[:, 3 + u:4 + u], 0.0)
            dve.bn_stats(ln_stats[:, u, :], slot(b)).then_inc(stats_done, 1)
            dve.wait_ge(stats_done, n + 1)
            dve.memset(scrap[:, u:u + 1], 0.0)
            dve.bn_aggr(ln_mv[:, u, :], ln_stats[:, u, :]).then_inc(var_done, 1)

        def gpsimd_ln_rstd(pool, n, u):
            pool.wait_ge(var_done, n + 1)
            pool.tensor_tensor(ln_veps[:, u:u + 1], ln_mv[:, u, 1:2], eps[:, :], ALU.add).then_inc(veps_done, 1)
            pool.wait_ge(veps_done, n + 1)
            pool.tensor_tensor(ln_rstd[:, u:u + 1], ln_veps[:, u:u + 1], minus_half[:, :], ALU.pow).then_inc(rstd_done, 1)

        def vector_ln_apply(dve, b, n, u, kept=None):
            dve.wait_ge(rstd_done, n + 1)
            at_least(dve, xnT_in_psum, n - 1)
            if kept is not None:
                at_least(dve, *kept)
            dve.tensor_scalar(xn[:, u, :], slot(b), ln_mv[:, u, 0:1], ln_rstd[:, u:u + 1],
                              ALU.subtract, ALU.mult).then_inc(xn_done, 1)

        def tensor_xnT(pe, n, u, psum):
            pe.wait_ge(xn_done, n + 1)
            at_least(pe, xnT_done, n - 1)
            pe.transpose(psum[:, 0:128], xn[:, u, :], ident[:, :]).then_inc(xnT_in_psum, 1)

        def scalar_xnT(act, n, u, psum):
            act.wait_ge(xnT_in_psum, n + 1)
            act.activation(xnT[:, u, :], psum[:, 0:128], ACT.Copy).then_inc(xnT_done, 1)

        P0 = [bank[0], bank[1]]
        S0 = [bank[2], bank[3], bank[4]]
        T0 = [bank[5], bank[6]]
        HEADS0 = [(0, 6), (6, 12), (12, 16)]
        WO = bank[7][:, 0:128]

        def tensor_attn0(pe):
            def project(b, u):
                for j in range(6):
                    if j == 0:
                        pe.wait_ge(xnT_done, b + 1)
                    if j == 4:
                        pe.wait_ge(ctx_b_done, b + 1)
                    if j < 2:
                        at_least(pe, av_done, 2 * b - 3 + j)
                    else:
                        pe.wait_ge(proj_done, 8 * b + [1, 2, 4, 6][j - 2])
                    dst = P0[j % 2]
                    half = j % 2
                    if j < 4:
                        w, rhs, n = (wq0, xnT[:, u, :], 128) if j < 2 else (wk0, ctxT[:, bass.ds(b, 1), :].rearrange("p a t -> p (a t)"), T)
                        for c in range(4):
                            m = pe.matmul(dst[:, c * n:(c + 1) * n], w[:, (4 * half + c) * 128:(4 * half + c + 1) * 128],
                                          rhs, start=True, stop=True)
                    else:
                        m = pe.matmul(dst[0:T, :], ctx_b[:, u, :], wv0[:, half * 512:(half + 1) * 512], start=True, stop=True)
                    m.then_inc(proj_in_psum, 1)

            def scores(b):
                pe.wait_ge(proj_done, 8 * b + 6)
                for c, (lo, hi) in enumerate(HEADS0):
                    at_least(pe, shifted_done, 3 * b - 2 + c)
                    n = hi - lo
                    pe.matmul(S0[c][:, 0:n * T], ident_b[:, :],
                              mask_bias[:, bass.ds(b, 1), :].to_broadcast([128, n, T]), start=True, stop=False)
                    for h in range(lo, hi, 2):
                        m = pe.matmul(S0[c][:, (h - lo) * T:(h - lo + 2) * T], qT[:, h // 2, :],
                                      kT[:, h:h + 2, :].rearrange("p a t -> p (a t)"), start=False, stop=(h == hi - 2))
                    m.then_inc(scores_in_psum, 1)

            def turn(b, u, j, more):
                pe.wait_ge(probs_done, 3 * b + (4 * j + 3) // 6 + 1)
                at_least(pe, turn_done, 4 * b + max(j - 1, 0))
                if j == 1 and more >= 1:
                    pe.wait_ge(xnT_done, b + 2)
                for h in range(4 * j, 4 * j + 4):
                    m = pe.transpose(T0[(u + j) % 2][0:T, (h % 4) * 128:(h % 4 + 1) * 128], e0[:, h, :], ident[:, :])
                m.then_inc(turn_in_psum, 1)

            def attend(b, u, j, more):
                pe.wait_ge(turn_done, 4 * b + j + 1)
                if more >= 1 and j % 2 == 0:
                    pe.wait_ge(proj_done, 8 * b + 15 + j // 2)
                for h in range(4 * j, 4 * j + 4):
                    c, p = h // 2, 64 * (h % 2)
                    m = pe.matmul(P0[c // 4][p:p + 64, (c % 4) * 128:(c % 4 + 1) * 128], v0[:, u, h, :], eT0[:, h, :], start=True, stop=True)
                if j % 2 == 1:
                    m.then_inc(av_in_psum, 1)

            def output(b):
                at_least(pe, x_updated, b)
                pe.wait_ge(av_done, 2 * b + 2)
                for c in range(8):
                    pe.matmul(WO, oT0[:, c, :], wo0[:, c, :], start=(c == 0), stop=False)
                pe.matmul(WO, ones_row[:, :], bo0[:, :], start=False, stop=True).then_inc(wo_in_psum, 1)

            pe.wait_ge(const_loaded, 4 * 16)
            pe.wait_ge(pool_ready, 3)
            pe.wait_ge(ctx_loaded, 16)
            tensor_xnT(pe, 0, 0, T0[0])
            pe.wait_ge(wqkv0_loaded, 6 * 16)
            project(0, 0)
            scores(0)
            tensor_xnT(pe, 1, 1, T0[1])
            pe.wait_ge(wo0_loaded, 2 * 16)

            def body(b, u, more):
                if more >= 1:
                    project(b + 1, 1 - u)
                turn(b, u, 0, more)
                turn(b, u, 1, more)
                turn(b, u, 2, more)
                attend(b, u, 0, more)
                turn(b, u, 3, more)
                for j in range(1, 4):
                    attend(b, u, j, more)
                if more >= 2:
                    tensor_xnT(pe, b + 2, u, T0[u])
                if more >= 1:
                    scores(b + 1)
                output(b)
            over_tiles(pe, body)

        def vector_attn0(dve):
            def projected(b, u, parts):
                for j in parts:
                    dve.wait_ge(proj_in_psum, 6 * b + j + 1)
                    half = j % 2
                    c = slice(4 * half, 4 * half + 4)
                    if j < 2:
                        dve.tensor_tensor(qT[:, c, :], P0[half][:, 0:512].rearrange("p (c n) -> p c n", n=128),
                                          bq0[:, c].unsqueeze(2).to_broadcast([128, 4, 128]), ALU.add).then_inc(proj_done, 1)
                    elif j < 4:
                        for r in range(2):
                            p = slice(64 * r, 64 * r + 64)
                            dve.tensor_tensor(kT[p, 8 * half + r:8 * half + 8:2, :],
                                              P0[half][p, 0:4 * T].rearrange("p (c n) -> p c n", n=T),
                                              bk0[p, c].unsqueeze(2).to_broadcast([64, 4, T]), ALU.add).then_inc(proj_done, 1)
                    else:
                        h = slice(8 * half, 8 * half + 8)
                        dve.tensor_tensor(v0[:, u, h, 0:DK0], P0[half][0:T, :].rearrange("p (h d) -> p h d", d=DK0),
                                          bv0[:, h, :], ALU.add).then_inc(proj_done, 1)

            def softmax(b):
                for c, (lo, hi) in enumerate(HEADS0):
                    n = hi - lo
                    sc = S0[c][:, 0:n * T].rearrange("p (h t) -> p h t", t=T)
                    dve.wait_ge(scores_in_psum, 3 * b + c + 1)
                    dve.tensor_reduce(mx0[:, lo:hi], sc, AX.X, ALU.max).then_inc(max_done, 1)
                    dve.wait_ge(max_done, 3 * b + c + 1)
                    dve.tensor_tensor(e0[:, lo:hi, :], sc, mx0[:, lo:hi].unsqueeze(2).to_broadcast([128, n, T]),
                                      ALU.subtract).then_inc(shifted_done, 1)

            def sums(b):
                for c, (lo, hi) in enumerate(HEADS0):
                    dve.wait_ge(exp_done, 3 * b + c + 1)
                    dve.tensor_reduce(sum0[:, lo:hi], e0[:, lo:hi, :], AX.X, ALU.add).then_inc(sums_done, 1)
                dve.wait_ge(sums_done, 4 * b + 3)
                dve.reciprocal(rs0[:, :], sum0[:, :]).then_inc(sums_done, 1)

            def update(b):
                dve.wait_ge(wo_in_psum, b + 1)
                dve.scalar_tensor_tensor(slot(b), WO, tg[:, 0:1], slot(b), ALU.mult, ALU.add).then_inc(x_updated, 1)

            dve.wait_ge(x_loaded, 16)
            dve.wait_ge(pool_ready, 3)
            vector_ln_stats(dve, 0, 0, 0)
            vector_ln_apply(dve, 0, 0, 0)
            vector_ln_stats(dve, 1, 1, 1)
            vector_ln_apply(dve, 1, 1, 1)
            dve.wait_ge(wqkv0_loaded, 6 * 16)
            dve.wait_ge(tg_ready, 1)
            projected(0, 0, range(6))
            softmax(0)

            def body(b, u, more):
                if more >= 1:
                    projected(b + 1, 1 - u, range(2))
                sums(b)
                if more >= 2:
                    vector_ln_stats(dve, b + 2, b + 2, u)
                if more >= 1:
                    projected(b + 1, 1 - u, range(2, 6))
                if more >= 2:
                    vector_ln_apply(dve, b + 2, b + 2, u)
                if more >= 1:
                    softmax(b + 1)
                update(b)
            over_tiles(dve, body)

        def scalar_attn0(act):
            def exps(b):
                for c, (lo, hi) in enumerate(HEADS0):
                    act.wait_ge(shifted_done, 3 * b + c + 1)
                    act.activation(e0[:, lo:hi, :], e0[:, lo:hi, :], ACT.Exp, scale=DK0 ** -0.5).then_inc(exp_done, 1)

            scalar_xnT(act, 0, 0, T0[0])
            exps(0)
            scalar_xnT(act, 1, 1, T0[1])

            def body(b, u, more):
                for j in range(4):
                    act.wait_ge(turn_in_psum, 4 * b + j + 1)
                    act.activation(eT0[:, 4 * j:4 * j + 4, :], T0[(u + j) % 2][0:T, :].rearrange("p (h q) -> p h q", q=128),
                                   ACT.Copy).then_inc(turn_done, 1)
                for j in range(2):
                    act.wait_ge(av_in_psum, 2 * b + j + 1)
                    act.activation(oT0[:, 4 * j:4 * j + 4, :], P0[j][:, :].rearrange("p (h q) -> p h q", q=128),
                                   ACT.Copy).then_inc(av_done, 1)
                if more >= 2:
                    scalar_xnT(act, b + 2, u, T0[u])
                if more >= 1:
                    exps(b + 1)
            over_tiles(act, body)

        def gpsimd_attn0(pool):
            def context(b, u):
                at_least(pool, proj_in_psum, 6 * b - 6)
                pool.tensor_copy(ctx_b[:, u, :], ctxT[:, bass.ds(b, 1), :].rearrange("p a t -> p (a t)")).then_inc(ctx_b_done, 1)

            def normalise(b):
                pool.wait_ge(sums_done, 4 * b + 4)
                for lo, hi in HEADS0:
                    pool.tensor_tensor(e0[:, lo:hi, :], e0[:, lo:hi, :], rs0[:, lo:hi].unsqueeze(2).to_broadcast([128, hi - lo, T]),
                                       ALU.mult).then_inc(probs_done, 1)

            gpsimd_ln_rstd(pool, 0, 0)
            gpsimd_ln_rstd(pool, 1, 1)
            pool.wait_ge(ctx_loaded, 16)
            context(0, 0)
            context(1, 1)

            def body(b, u, more):
                normalise(b)
                if more >= 2:
                    gpsimd_ln_rstd(pool, b + 2, u)
                    context(b + 2, u)
            over_tiles(pool, body)

        LOGITS0 = bank[4]
        RANK0 = bank[7]
        H_BANKS = [bank[0:2], bank[2:4]]
        XE_BANK = [bank[4], bank[5]]
        Y_BANK = [bank[6], bank[7]]

        def over_experts(engine, body):
            body(0, 0, True)
            body(1, 1, True)
            with engine.Fori(1, E0 // 2 - 1) as i:
                body(i * 2, 0, True)
                body(i * 2 + 1, 1, True)
            body(E0 - 2, 0, True)
            body(E0 - 1, 1, False)

        def tensor_moe0(pe):
            pe.wait_ge(route0_loaded, 6 * 16)
            tensor_xnT(pe, 16, 0, T0[0])

            def tile(b, u, more):
                if more >= 1:
                    tensor_xnT(pe, b + 17, 1 - u, T0[1 - u])
                pe.wait_ge(xnT_done, b + 17)
                pe.matmul(LOGITS0[:, bass.ds(b * E0, E0)], xnT[:, u, :], wg0[:, :], start=True, stop=True).then_inc(logits_in_psum, 1)
            over_tiles(pe, tile)
            pe.wait_ge(first_done, 1)
            pe.matmul(RANK0[:, 0:B * E0], tri_b[:, :], first0[:, :, :].rearrange("p b e -> p (b e)"), start=True, stop=False)
            for k in range(1, B):
                m = pe.matmul(RANK0[:, k * E0:B * E0], ones_b[:, :], first0[:, 0:B - k, :].rearrange("p b e -> p (b e)"),
                              start=False, stop=(k == B - 1))
            m.then_inc(rank_in_psum, 1)

            def turn(e, v):
                pe.wait_ge(expert_loaded[v], 80 * (e // 2 + 1) if isinstance(e, int) else (e - v) * 40 + 80)
                at_least(pe, xeT_done, e - 1)
                for j in range(2):
                    m = pe.transpose(XE_BANK[v][:, j * 128:(j + 1) * 128], xe[:, v, j, :], ident[:, :])
                m.then_inc(xeT_in_psum, 1)

            def hidden(e, v):
                pe.wait_ge(xeT_done, e + 1)
                at_least(pe, h_done, 4 * e - 4)
                for c in range(FC0):
                    m = pe.matmul(H_BANKS[v][c // 2][:, (c % 2) * 256:(c % 2 + 1) * 256], w1e[:, v, c * 128:(c + 1) * 128],
                                  xeT[:, v, :], start=True, stop=True)
                    if c % 2:
                        m.then_inc(h_in_psum, 1)

            def rows_out(e, v):
                at_least(pe, y_done, e - 1)
                pe.wait_ge(h_done, 4 * e + 4)
                for j in range(2):
                    for c in range(FC0):
                        pe.matmul(Y_BANK[v][:, j * 128:(j + 1) * 128], hT0[:, v, c, j * 128:(j + 1) * 128], w2e[:, v, c, :],
                                  start=(c == 0), stop=False)
                    m = pe.matmul(Y_BANK[v][:, j * 128:(j + 1) * 128], ones_row[:, :], b2e[:, v, :], start=False, stop=True)
                m.then_inc(y_in_psum, 1)

            turn(0, 0)
            hidden(0, 0)

            def expert(e, v, more):
                if more:
                    turn(e + 1, 1 - v)
                    hidden(e + 1, 1 - v)
                rows_out(e, v)
            over_experts(pe, expert)

        def vector_moe0(dve):
            vector_ln_stats(dve, 0, 16, 0, 1)

            def tile(b, u, more):
                if more >= 1:
                    vector_ln_stats(dve, b + 1, b + 17, 1 - u, b + 2)
                vector_ln_apply(dve, b, b + 16, u, (xn_kept, b - 1))
            over_tiles(dve, tile)

            steps = [0]

            def link(ins):
                steps[0] += 1
                ins.then_inc(route_step, 1)
                dve.wait_ge(route_step, steps[0])

            def wide(a):
                return a[:, :].unsqueeze(2).to_broadcast([128, B, E0])

            def per_expert(a):
                return a[:, :].unsqueeze(1).to_broadcast([128, B, E0])

            lg = LOGITS0[:, 0:B * E0].rearrange("p (b e) -> p b e", e=E0)
            rank = RANK0[:, 0:B * E0].rearrange("p (b e) -> p b e", e=E0)
            dve.wait_ge(logits_in_psum, B)
            dve.wait_ge(route0_loaded, 6 * 16)
            link(dve.tensor_reduce(r0s["max"][:, :], lg, AX.X, ALU.max))
            dve.tensor_tensor(r0["exp"][:, :, :], lg, wide(r0s["max"]), ALU.subtract).then_inc(route_exp, 1)
            dve.wait_ge(route_exp, 2)
            link(dve.tensor_reduce(r0s["sum"][:, :], r0["exp"][:, :, :], AX.X, ALU.add))
            link(dve.reciprocal(r0s["rsum"][:, :], r0s["sum"][:, :]))
            link(dve.tensor_tensor(r0["gate"][:, :, :], r0["exp"][:, :, :], wide(r0s["rsum"]), ALU.mult))
            link(dve.tensor_reduce(r0s["gmax"][:, :], r0["gate"][:, :, :], AX.X, ALU.max))
            link(dve.tensor_tensor(r0["rank"][:, :, :], r0["gate"][:, :, :], wide(r0s["gmax"]), ALU.is_equal))
            link(dve.tensor_tensor(r0["at"][:, :, :], r0["rank"][:, :, :], per_expert(rank_w), ALU.mult))
            link(dve.tensor_reduce(r0s["rmax"][:, :], r0["at"][:, :, :], AX.X, ALU.max))
            dve.tensor_tensor(first0[:, :, :], r0["at"][:, :, :], wide(r0s["rmax"]), ALU.is_equal).then_inc(first_done, 1)
            dve.wait_ge(rank_in_psum, 1)
            link(dve.scalar_tensor_tensor(r0["keep"][:, :, :].rearrange("p b e -> p (b e)"), RANK0[:, 0:B * E0], float(C0),
                                          first0[:, :, :].rearrange("p b e -> p (b e)"), ALU.is_le, ALU.mult))
            link(dve.tensor_tensor(r0["rank"][:, :, :], rank, per_expert(slot_base), ALU.add))
            link(dve.tensor_tensor(r0["at"][:, :, :], r0["rank"][:, :, :], r0["keep"][:, :, :], ALU.mult))
            link(dve.tensor_reduce(r0s["slot"][:, :], r0["at"][:, :, :], AX.X, ALU.add))
            link(dve.tensor_reduce(r0s["kept"][:, :], r0["keep"][:, :, :], AX.X, ALU.add))
            link(dve.tensor_tensor(r0s["alt"][:, :], spare_slot[:, :], r0s["kept"][:, :], ALU.mult))
            link(dve.tensor_tensor(r0s["alt2"][:, :], spare_slot[:, :], r0s["alt"][:, :], ALU.subtract))
            dve.tensor_tensor(scatter_at[:, :], r0s["slot"][:, :], r0s["alt2"][:, :], ALU.add).then_inc(places_done, 1)
            dve.tensor_copy(gather_at[:, :], r0s["slot"][:, :]).then_inc(places_done, 1)
            link(dve.tensor_tensor(r0["gkeep"][:, :, :], r0["gate"][:, :, :], r0["keep"][:, :, :], ALU.mult))
            link(dve.tensor_reduce(r0s["gsel"][:, :], r0["gkeep"][:, :, :], AX.X, ALU.add))
            link(dve.tensor_scalar(r0s["weight"][:, :], r0s["gsel"][:, :], tg[:, 4:5], None, ALU.mult))

            def expert(e, v, more):
                dve.wait_ge(y_in_psum, e + 1)
                if not isinstance(e, int):
                    dve.wait_ge(y_stored[v], (e - v) * 8)
                elif e >= 2:
                    dve.wait_ge(y_stored[v], 16 * (e // 2))
                dve.tensor_copy(ye[:, v, :, :], Y_BANK[v][:, 0:256].rearrange("p (j d) -> p j d", d=D)).then_inc(y_done, 1)
            over_experts(dve, expert)

            for b in range(B):
                if b % 4 == 0:
                    dve.wait_ge(gathered[b // 4], 64)
                dve.scalar_tensor_tensor(X[:, b, :], XN[:, b, :], r0s["weight"][:, b:b + 1], X[:, b, :],
                                         ALU.mult, ALU.add).then_inc(x_updated, 1)

        def scalar_moe0(act):
            def tile(b, u, more):
                scalar_xnT(act, b + 16, u, T0[u])
            over_tiles(act, tile)
            act.wait_ge(route_exp, 1)
            act.activation(r0["exp"][:, :, :], r0["exp"][:, :, :], ACT.Exp).then_inc(route_exp, 1)

            def turn(e, v):
                act.wait_ge(xeT_in_psum, e + 1)
                act.activation(xeT[:, v, :], XE_BANK[v][:, 0:256], ACT.Copy).then_inc(xeT_done, 1)

            turn(0, 0)

            def expert(e, v, more):
                if more:
                    turn(e + 1, 1 - v)
                for c in range(FC0):
                    act.wait_ge(h_in_psum, 2 * e + c // 2 + 1)
                    act.activation(hT0[:, v, c, :], H_BANKS[v][c // 2][:, (c % 2) * 256:(c % 2 + 1) * 256],
                                   ACT.Gelu_apprx_tanh, bias=b1e[:, v, c:c + 1]).then_inc(h_done, 1)
            over_experts(act, expert)

        def gpsimd_moe0(pool):
            gpsimd_ln_rstd(pool, 16, 0)

            def tile(b, u, more):
                if more >= 1:
                    gpsimd_ln_rstd(pool, b + 17, 1 - u)
                pool.wait_ge(xn_done, b + 17)
                pool.tensor_copy(XN[:, bass.ds(b, 1), :].rearrange("p a d -> p (a d)"), xn[:, u, :]).then_inc(xn_kept, 1)
            over_tiles(pool, tile)
            pool.wait_ge(xn_kept, B)
            pool.wait_ge(places_done, 2)
            pool.wait_ge(slots_zeroed, 16)
            for b in range(B):
                pool.indirect_dma_start(out=t["x_slots"], out_offset=bass.IndirectOffsetOnAxis(ap=scatter_at[:, b:b + 1], axis=0),
                                        in_=XN[:, b, :], in_offset=None).then_inc(scattered, 16)
            pool.wait_ge(y_stored[0], E0 // 2 * 16)
            pool.wait_ge(y_stored[1], E0 // 2 * 16)
            for b in range(B):
                pool.indirect_dma_start(out=XN[:, b, :], out_offset=None, in_=t["y_slots"],
                                        in_offset=bass.IndirectOffsetOnAxis(ap=gather_at[:, b:b + 1], axis=0)).then_inc(gathered[b // 4], 16)

        def sync_moe0(sp):
            sp.wait_ge(scattered, B * 16)

            def load(e, v):
                def one(name, pattern=None, **kw):
                    a = t[name][bass.ds(e, 1)]
                    return a.rearrange(pattern, **kw)
                sp.dma_start(xe[:, v, :, :], t["x_slots"][bass.ds(e * C0, C0), :].rearrange("(j p) d -> p j d", p=128)).then_inc(expert_loaded[v], 16)
                sp.dma_start(w1e[:, v, :], one("w1_0", "a p f -> p (a f)")).then_inc(expert_loaded[v], 16)
                sp.dma_start(w2e[:, v, :, :], one("w2_0", "a (c p) d -> p (a c) d", p=128)).then_inc(expert_loaded[v], 16)
                sp.dma_start(b1e[:, v, :], one("b1_0", "a p c -> p (a c)")).then_inc(expert_loaded[v], 16)
                sp.dma_start(b2e[:, v, :], one("b2_0", "a x d -> a (x d)")).then_inc(expert_loaded[v], 16)
            load(0, 0)

            def expert(e, v, more):
                if more:
                    at_least(sp, y_in_psum, e)
                    load(e + 1, 1 - v)
                sp.wait_ge(y_done, e + 1)
                sp.dma_start(t["y_slots"][bass.ds(e * C0, C0), :].rearrange("(j p) d -> p j d", p=128), ye[:, v, :, :]).then_inc(y_stored[v], 16)
            over_experts(sp, expert)

        XT4 = [bank[5], bank[6]]
        K_IN1, K_NEXT1 = (0, 1, 3, 5), (2, 4, 6, 7)
        NORMS_AHEAD = 4

        def vector_g_stats(dve, g, k, updates):
            dve.wait_ge(x_updated, updates)
            for j in range(4):
                dve.bn_stats(g_stats[:, k % 2, j, :], X[:, 4 * g + j, :]).then_inc(g_stats_done, 1)
            dve.wait_ge(g_stats_done, 4 * (k + 1))
            for j in range(4):
                dve.bn_aggr(g_mv[:, k % 2, j, :], g_stats[:, k % 2, j, :]).then_inc(g_var_done, 1)

        def gpsimd_g_rstd(pool, k):
            u = k % 2
            pool.wait_ge(g_var_done, 4 * (k + 1))
            pool.tensor_tensor(g_veps[:, u, :], g_mv[:, u, :, 1], eps[:, :].to_broadcast([128, 4]), ALU.add).then_inc(g_veps_done, 1)
            pool.wait_ge(g_veps_done, k + 1)
            pool.tensor_tensor(g_rstd[:, u, :], g_veps[:, u, :], minus_half[:, :].to_broadcast([128, 4]), ALU.pow).then_inc(g_rstd_done, 1)

        def vector_g_apply(dve, g, n, k, used=0):
            dve.wait_ge(g_rstd_done, k + 1)
            at_least(dve, d3_in_psum, used)
            at_least(dve, g_xnT_in_psum, n - 1)
            for j in range(4):
                dve.tensor_scalar(xn4[:, n % 2, j, :], X[:, 4 * g + j, :], g_mv[:, k % 2, j, 0:1], g_rstd[:, k % 2, j:j + 1],
                                  ALU.subtract, ALU.mult).then_inc(g_xn_done, 1)

        def tensor_g_xnT(pe, n, psum):
            pe.wait_ge(g_xn_done, 4 * (n + 1))
            at_least(pe, g_xnT_done, n)
            for j in range(4):
                m = pe.transpose(psum[:, j * 128:(j + 1) * 128], xn4[:, n % 2, j, :], ident[:, :])
            m.then_inc(g_xnT_in_psum, 1)

        def scalar_g_xnT(act, n, psum):
            act.wait_ge(g_xnT_in_psum, n + 1)
            act.activation(xnT4[:, n % 2, :], psum[:, :], ACT.Copy).then_inc(g_xnT_done, 1)

        MIX = [bank[4], bank[7]]

        def tensor_mix1(pe):
            pe.wait_ge(mix_loaded, 3 * 16)
            pe.wait_ge(ctx_mean_done, 1)
            for b in range(B):
                dst = bank[b // 4][0:1, (b % 4) * D:(b % 4 + 1) * D]
                pe.matmul(dst, ctx_mean[:, b:b + 1], w2x[:, :], start=True, stop=False)
                m = pe.matmul(dst, ones_row[:, 0:1], bx[:, :], start=False, stop=True)
                if b % 4 == 3:
                    m.then_inc(mix_row_in_psum, 1)
            pe.wait_ge(mix_row_done, 4)
            pe.wait_ge(x_updated, 2 * B)
            for g in range(4):
                tensor_g_xnT(pe, g, XT4[g % 2])
                pe.wait_ge(g_xnT_done, g + 1)
                at_least(pe, x_updated, 2 * B + 4 * (g - 1) if g >= 2 else 0)
                for j in range(4):
                    b = 4 * g + j
                    dst = MIX[g % 2][:, j * D:(j + 1) * D]
                    pe.matmul(dst, xnT4[:, g % 2, j * 128:(j + 1) * 128], w1x[:, :], start=True, stop=False)
                    m = pe.matmul(dst, ones_row[:, :], mix_row[:, b * D:(b + 1) * D], start=False, stop=True)
                m.then_inc(mix_in_psum, 1)

        def vector_mix1(dve):
            dve.tensor_reduce(ctx_sum[:, :], ctxT[:, :, :], AX.X, ALU.add).then_inc(quant_step, 1)
            dve.wait_ge(quant_step, 1)
            dve.tensor_scalar(ctx_mean[:, :], ctx_sum[:, :], 1.0 / T, None, ALU.mult).then_inc(ctx_mean_done, 1)
            for g in range(4):
                dve.wait_ge(mix_row_in_psum, g + 1)
                dve.tensor_copy(mix_row[:, g * 512:(g + 1) * 512], bank[g][0:1, :]).then_inc(mix_row_done, 1)

            def next_norm(g):
                k = K_NEXT1[g]
                dve.wait_ge(g_rstd_done, k + 1)
                for j in range(4):
                    dve.tensor_scalar(XN[:, 4 * g + j, :], X[:, 4 * g + j, :], g_mv[:, k % 2, j, 0:1], g_rstd[:, k % 2, j:j + 1],
                                      ALU.subtract, ALU.mult).then_inc(norm1_done, 1)
                dve.wait_ge(norm1_done, 4 * g + 4)
                dve.tensor_reduce(absmax1[:, 4 * g:4 * g + 4], XN[:, 4 * g:4 * g + 4, :], AX.X, ALU.max,
                                  apply_absolute_value=True).then_inc(absmax_done, 1)

            vector_g_stats(dve, 0, K_IN1[0], 2 * B)
            vector_g_stats(dve, 1, K_IN1[1], 2 * B)
            vector_g_apply(dve, 0, 0, K_IN1[0])
            for g in range(4):
                if g < 3:
                    vector_g_apply(dve, g + 1, g + 1, K_IN1[g + 1])
                dve.wait_ge(mix_in_psum, g + 1)
                x = X[:, 4 * g:4 * g + 4, :].rearrange("p b d -> p (b d)")
                dve.scalar_tensor_tensor(x, MIX[g % 2][:, :], tg[:, 1:2], x, ALU.mult, ALU.add).then_inc(x_updated, 4)
                if g >= 1:
                    next_norm(g - 1)
                vector_g_stats(dve, g, K_NEXT1[g], 2 * B + 4 * g + 4)
                if g < 2:
                    vector_g_stats(dve, g + 2, K_IN1[g + 2], 2 * B)
            next_norm(3)

        def scalar_mix1(act):
            for g in range(4):
                scalar_g_xnT(act, g, XT4[g % 2])

        def gpsimd_mix1(pool):
            for k in range(8):
                gpsimd_g_rstd(pool, k)

        GATE_BANK = [bank[0], bank[2], bank[4]]
        UP_BANK = [bank[1], bank[3], bank[7]]
        XQ_BANK = [bank[5], bank[6]]
        DOWN_BANK = [bank[0], bank[2], bank[1], bank[3]]

        def tensor_ffn1(pe):
            for k in range(7):
                pe.wait_ge(w_rounded, k + 1)
                at_least(pe, wT_done, k - 1)
                if k < 6:
                    lo, hi = ROWS1[k % 3]
                    pe.transpose(XQ_BANK[k % 2][:, 0:hi - lo], wgu1[0:hi - lo, k // 3, k % 3, :], ident[0:hi - lo, 0:hi - lo]).then_inc(wT_in_psum, 1)
                else:
                    for c, (lo, hi) in enumerate(ROWS1):
                        m = pe.transpose(XQ_BANK[0][0:hi - lo, c * D:(c + 1) * D], wd1[:, lo:hi], ident[:, :])
                    m.then_inc(wT_in_psum, 1)
            pe.wait_ge(drow_in_psum, 1)
            pe.matmul(bank[0][:, 0:D], ones[:, :], dscale1[:, :], start=True, stop=True).then_inc(drow_in_psum, 1)

            def spread_max(k, col):
                pe.wait_ge(colmax_done, k + 1)
                pe.transpose(bank[0][0:1, 128:256], col[:, :], ident[:, :]).then_inc(maxrow_in_psum, 1)
                pe.wait_ge(cell_done, k + 1)
                pe.matmul(bank[0][:, 256:257], ones_row[:, :], cell1[:, k:k + 1], start=True, stop=True).then_inc(max_in_psum, 1)

            pe.wait_ge(quant_step, DROW_STEP)
            spread_max(0, col1["xmax"])

            def turn(g):
                pe.wait_ge(xq_done, g + 1)
                if g == 0:
                    pe.wait_ge(wT_done, 7)
                at_least(pe, xqT_done, g - 1)
                for j in range(4):
                    m = pe.transpose(XQ_BANK[g % 2][:, j * 128:(j + 1) * 128], xq1[:, j, :], ident[:, :])
                m.then_inc(xqT_in_psum, 1)

            turn(0)
            for g in range(4):
                pe.wait_ge(xqT_done, g + 1)
                for c, (lo, hi) in enumerate(ROWS1):
                    if g == 0 and c == 0:
                        pe.wait_ge(quant_step, XINV_STEP)
                    at_least(pe, silu_done, 3 * (g - 1) + c + 1)
                    at_least(pe, h1_done, 3 * (g - 1) + c + 1)
                    pe.matmul(GATE_BANK[c][0:hi - lo, :], wguT1[:, 0, lo:hi], xqT1[:, g % 2, :], start=True, stop=True)
                    pe.matmul(UP_BANK[c][0:hi - lo, :], wguT1[:, 1, lo:hi], xqT1[:, g % 2, :], start=True, stop=True).then_inc(gu_in_psum, 1)
                if g < 3:
                    turn(g + 1)
            pe.wait_ge(silu_done, 12)
            spread_max(1, col1["hmax"])
            for g in range(4):
                at_least(pe, h1_done, 12)
                pe.wait_ge(hq_done, 3)
                if g == 0:
                    pe.wait_ge(quant_step, HINV_STEP)
                for j in range(4):
                    for c, (lo, hi) in enumerate(ROWS1):
                        tok = (4 * g + j) * 128
                        m = pe.matmul(DOWN_BANK[g][:, j * D:(j + 1) * D], hq1[0:hi - lo, c, tok:tok + 128], wdT1[0:hi - lo, c, :],
                                      start=(c == 0), stop=(c == 2))
                m.then_inc(down_in_psum, 1)

        def vector_ffn1(dve):
            steps = [1]

            def link(ins):
                steps[0] += 1
                ins.then_inc(quant_step, 1)
                dve.wait_ge(quant_step, steps[0])

            dve.wait_ge(ffn1_loaded, 5 * 16)
            dve.memset(wmax1[:, :], 1.0)
            link(dve.memset(hmax1[:, :], 0.0))
            for k in range(6):
                lo, hi = ROWS1[k % 3]
                dve.tensor_reduce(wmax1[0:hi - lo, k:k + 1], wgu1[0:hi - lo, k // 3, k % 3, :], AX.X, ALU.max, apply_absolute_value=True)
            link(dve.tensor_reduce(wmax1[:, 6:7], wd1[:, :], AX.X, ALU.max, apply_absolute_value=True))
            link(dve.tensor_scalar(wscale1[:, :], wmax1[:, :], 1.0 / QMAX, None, ALU.mult))
            link(dve.reciprocal(winv1[:, :], wscale1[:, :]))
            for k in range(6):
                lo, hi = ROWS1[k % 3]
                w = wgu1[0:hi - lo, k // 3, k % 3, :]
                dve.tensor_scalar(w, w, winv1[0:hi - lo, k:k + 1], MAGIC, ALU.mult, ALU.add).then_inc(w_rounded, 1)
            dve.tensor_scalar(wd1[:, :], wd1[:, :], winv1[:, 6:7], MAGIC, ALU.mult, ALU.add).then_inc(w_rounded, 1)
            dve.tensor_scalar(dscale1[:, :], ident[:, :], wscale1[:, 6:7], None, ALU.mult).then_inc(drow_in_psum, 1)
            dve.wait_ge(drow_in_psum, 2)
            link(dve.tensor_copy(drow1[:, :], bank[0][:, 0:D]))
            assert steps[0] == DROW_STEP
            dve.wait_ge(clip_tanh_done, 1)
            link(dve.tensor_scalar(clip_sig[:, :], clip_tanh[:, :], 0.5, 0.5, ALU.mult, ALU.add))

            def scale_of(k, columns, colmax, scale, inv):
                dve.tensor_reduce(colmax[:, :], columns, AX.X, ALU.max).then_inc(colmax_done, 1)
                dve.wait_ge(maxrow_in_psum, k + 1)
                dve.tensor_reduce(cell1[:, k:k + 1], bank[0][0:1, 128:256], AX.X, ALU.max).then_inc(cell_done, 1)
                dve.wait_ge(max_in_psum, k + 1)
                link(dve.tensor_scalar(scale[:, :], bank[0][:, 256:257], clip_sig[:, k:k + 1], 1.0 / QMAX, ALU.mult, ALU.mult))
                link(dve.reciprocal(inv[:, :], scale[:, :]))

            dve.wait_ge(absmax_done, 4)
            scale_of(0, absmax1[:, :], col1["xmax"], col1["xscale"], col1["xinv"])
            assert steps[0] == XINV_STEP
            link(dve.tensor_scalar(guscale1[:, :, :].rearrange("p a c -> p (a c)"), wscale1[:, 0:6], col1["xscale"][:, :], None, ALU.mult))

            def quantise(g):
                at_least(dve, xqT_in_psum, g)
                x4 = XN[:, 4 * g:4 * g + 4, :]
                link(dve.tensor_scalar(x4, x4, col1["xinv"][:, :], QMAX, ALU.mult, ALU.min))
                dve.tensor_scalar(xq1[:, :, :], x4, -QMAX - 1.0, MAGIC, ALU.max, ALU.add).then_inc(xq_done, 1)

            quantise(0)
            for g in range(4):
                if g < 3:
                    quantise(g + 1)
                for c, (lo, hi) in enumerate(ROWS1):
                    h = h1[0:hi - lo, c, g * 512:(g + 1) * 512]
                    dve.wait_ge(silu_done, 3 * g + c + 1)
                    dve.scalar_tensor_tensor(h, UP_BANK[c][0:hi - lo, :], guscale1[0:hi - lo, 1, c:c + 1], silu1[0:hi - lo, c, :],
                                             ALU.mult, ALU.mult).then_inc(h1_done, 1)
                    dve.wait_ge(h1_done, 3 * g + c + 1)
                    m = dve.tensor_reduce(hmax1[0:hi - lo, 3 * g + c:3 * g + c + 1], h, AX.X, ALU.max, apply_absolute_value=True)
            link(m)
            scale_of(1, hmax1[:, :], col1["hmax"], col1["hscale"], col1["hinv"])
            assert steps[0] == HINV_STEP
            for c, (lo, hi) in enumerate(ROWS1):
                h = h1[0:hi - lo, c, :]
                link(dve.tensor_scalar(h, h, col1["hinv"][0:hi - lo, :], QMAX, ALU.mult, ALU.min))
                dve.tensor_scalar(h, h, -QMAX - 1.0, MAGIC, ALU.max, ALU.add).then_inc(hq_rounded, 1)
            link(dve.tensor_tensor(col1["out"][:, :], col1["hscale"][:, :], tg[:, 5:6], ALU.mult))
            for g in range(4):
                dve.wait_ge(down_in_psum, g + 1)
                out = tmp512[:, g % 2, :].rearrange("p (j d) -> p j d", d=D)
                link(dve.scalar_tensor_tensor(out, DOWN_BANK[g][:, :].rearrange("p (j d) -> p j d", d=D), col1["out"][:, :],
                                              drow1[:, :].unsqueeze(1).to_broadcast([128, 4, D]), ALU.mult, ALU.mult))
                dve.tensor_tensor(X[:, 4 * g:4 * g + 4, :], out, X[:, 4 * g:4 * g + 4, :], ALU.add).then_inc(x_updated, 4)

        def scalar_ffn1(act):
            for k in range(7):
                act.wait_ge(wT_in_psum, k + 1)
                if k < 6:
                    lo, hi = ROWS1[k % 3]
                    m = act.activation(wguT1[:, k // 3, lo:hi], XQ_BANK[k % 2][:, 0:hi - lo], ACT.Identity, bias=minus_magic[:, :])
                else:
                    for c, (lo, hi) in enumerate(ROWS1):
                        m = act.activation(wdT1[0:hi - lo, c, :], XQ_BANK[0][0:hi - lo, c * D:(c + 1) * D], ACT.Identity,
                                           bias=minus_magic[0:hi - lo, :])
                m.then_inc(wT_done, 1)

            def turn(g):
                act.wait_ge(xqT_in_psum, g + 1)
                act.activation(xqT1[:, g % 2, :], XQ_BANK[g % 2][:, :], ACT.Identity, bias=minus_magic[:, :]).then_inc(xqT_done, 1)

            turn(0)
            for g in range(4):
                for c, (lo, hi) in enumerate(ROWS1):
                    act.wait_ge(gu_in_psum, 3 * g + c + 1)
                    at_least(act, h1_done, 3 * (g - 1) + c + 1)
                    if g == 0 and c == 0:
                        act.wait_ge(quant_step, GUSCALE_STEP)
                    act.activation(silu1[0:hi - lo, c, :], GATE_BANK[c][0:hi - lo, :], ACT.Silu,
                                   scale=guscale1[0:hi - lo, 0, c:c + 1]).then_inc(silu_done, 1)
                if g < 3:
                    turn(g + 1)
            for c, (lo, hi) in enumerate(ROWS1):
                act.wait_ge(hq_rounded, c + 1)
                act.activation(hq1[0:hi - lo, c, :], h1[0:hi - lo, c, :], ACT.Identity, bias=minus_magic[0:hi - lo, :]).then_inc(hq_done, 1)

        KV2 = [bank[0], bank[1], bank[2], bank[3], bank[4], bank[7], bank[6]]
        Q2, S2, ET2, AV2 = bank[0], bank[1], bank[2], bank[3]
        KB2 = [(0, 6), (6, 12), (12, 16)]

        def tensor_attn2(pe):
            pe.wait_ge(attn2_loaded, 4 * 16)
            pe.wait_ge(x_updated, 4 * B)
            for n, (lo, hi) in enumerate(KB2):
                pe.matmul(KV2[n][:, 0:(hi - lo) * T], wqkv2[:, 1, :], ctxT[:, lo:hi, :].rearrange("p b t -> p (b t)"),
                          start=True, stop=True).then_inc(kv2_in_psum, 1)
            for n in range(4):
                for j in range(4):
                    m = pe.matmul(KV2[3 + n][0:T, j * D:(j + 1) * D], ctxT[:, 4 * n + j, :], wqkv2[:, 2, :], start=True, stop=True)
                m.then_inc(kv2_in_psum, 1)
            tensor_g_xnT(pe, 4, XT4[0])
            pe.wait_ge(v2_done, 4)
            pe.wait_ge(k2_done, 3)
            for g in range(4):
                pe.wait_ge(g_xnT_done, g + 5)
                at_least(pe, q2_done, g)
                pe.matmul(Q2[:, :], wqkv2[:, 0, :], xnT4[:, g % 2, :], start=True, stop=True).then_inc(q2_in_psum, 1)
                pe.wait_ge(q2_done, g + 1)
                at_least(pe, shift2_done, g)
                for j in range(4):
                    m = pe.matmul(S2[:, j * T:(j + 1) * T], qT2[:, j * 128:(j + 1) * 128], kT2[:, 4 * g + j, :], start=True, stop=True)
                m.then_inc(s2_in_psum, 1)
                if g < 3:
                    tensor_g_xnT(pe, g + 5, XT4[(g + 1) % 2])
                pe.wait_ge(exp2_done, g + 1)
                at_least(pe, eT2_done, g)
                for j in range(4):
                    m = pe.transpose(ET2[0:T, j * 128:(j + 1) * 128], e2[:, j, :], ident[:, :])
                m.then_inc(eT2_in_psum, 1)
                pe.wait_ge(eT2_done, g + 1)
                at_least(pe, x_updated, 4 * B + 4 * g)
                for j in range(4):
                    m = pe.matmul(AV2[:, j * D:(j + 1) * D], eT2[:, j * 128:(j + 1) * 128], v2[:, 4 * g + j, :], start=True, stop=True)
                m.then_inc(av2_in_psum, 1)

        def vector_attn2(dve):
            steps = [0]

            def link(ins):
                steps[0] += 1
                ins.then_inc(a2_step, 1)
                dve.wait_ge(a2_step, steps[0])

            vector_g_stats(dve, 0, 8, 4 * B)
            for n in range(4):
                dve.wait_ge(kv2_in_psum, 4 + n)
                dve.tensor_tensor(v2[:, 4 * n:4 * n + 4, :], KV2[3 + n][0:T, :].rearrange("p (j d) -> p j d", d=D),
                                  bv2[:, :].unsqueeze(1).to_broadcast([T, 4, D]), ALU.add).then_inc(v2_done, 1)
            vector_g_apply(dve, 0, 4, 8)

            def softmax(g):
                sc = S2[:, 0:4 * T].rearrange("p (j t) -> p j t", t=T)
                dve.wait_ge(s2_in_psum, g + 1)
                link(dve.tensor_reduce(s2["max"][:, :], sc, AX.X, ALU.max))
                dve.tensor_tensor(e2[:, :, :], sc, s2["max"][:, :].unsqueeze(2).to_broadcast([128, 4, T]), ALU.subtract).then_inc(shift2_done, 1)
                if g < 3:
                    vector_g_apply(dve, g + 1, g + 5, g + 9)
                dve.wait_ge(exp2_done, g + 1)
                link(dve.tensor_reduce(s2["sum"][:, :], e2[:, :, :], AX.X, ALU.add))
                link(dve.reciprocal(s2["rsum"][:, :], s2["sum"][:, :]))
                link(dve.tensor_scalar(s2["out"][:, :], s2["rsum"][:, :], tg[:, 2:3], None, ALU.mult))

            for g in range(4):
                if g < 3:
                    vector_g_stats(dve, g + 1, g + 9, 4 * B)
                softmax(g)
                dve.wait_ge(av2_in_psum, g + 1)
                out = tmp512[:, g % 2, :].rearrange("p (j d) -> p j d", d=D)
                link(dve.tensor_tensor(out, AV2[:, :].rearrange("p (j d) -> p j d", d=D),
                                       s2["out"][:, :].unsqueeze(2).to_broadcast([128, 4, D]), ALU.mult))
                dve.tensor_tensor(X[:, 4 * g:4 * g + 4, :], out, X[:, 4 * g:4 * g + 4, :], ALU.add).then_inc(x_updated, 4)

        def scalar_attn2(act):
            for n, (lo, hi) in enumerate(KB2):
                act.wait_ge(kv2_in_psum, n + 1)
                act.activation(kT2[:, lo:hi, :].rearrange("p b t -> p (b t)"), KV2[n][:, 0:(hi - lo) * T], ACT.Identity,
                               bias=bqk2[:, 1:2]).then_inc(k2_done, 1)
            scalar_g_xnT(act, 4, XT4[0])
            for g in range(4):
                act.wait_ge(q2_in_psum, g + 1)
                act.activation(qT2[:, :], Q2[:, :], ACT.Identity, bias=bqk2[:, 0:1]).then_inc(q2_done, 1)
                act.wait_ge(shift2_done, g + 1)
                act.activation(e2[:, :, :], e2[:, :, :], ACT.Exp, scale=D ** -0.5).then_inc(exp2_done, 1)
                if g < 3:
                    scalar_g_xnT(act, g + 5, XT4[(g + 1) % 2])
                act.wait_ge(eT2_in_psum, g + 1)
                act.activation(eT2[:, :], ET2[0:T, :], ACT.Copy).then_inc(eT2_done, 1)

        def gpsimd_attn2(pool):
            for k in range(8, 12):
                gpsimd_g_rstd(pool, k)

        SETS2 = [(bank[0], bank[1], bank[2]), (bank[3], bank[4], bank[7])]
        MISC2 = bank[6]
        PAIRS2 = [4, 0, 1, 2, 3]

        def tensor_moe2(pe):
            pe.wait_ge(moe2_loaded, 5 * 16)
            tensor_g_xnT(pe, 8, bank[5])
            for g in range(4):
                x4 = xnT4[:, g % 2, :]

                def up(i):
                    n = 5 * g + i
                    at_least(pe, h2_done, n - 1)
                    for a in range(2):
                        m = pe.matmul(SETS2[n % 2][a][:, :], w13_2[:, a, PAIRS2[i], :], x4, start=True, stop=True)
                    m.then_inc(ab2_in_psum, 1)

                pe.wait_ge(g_xnT_done, g + 9)
                pe.wait_ge(x_updated, 5 * B + 4 * g)
                for j in range(4):
                    dst = MISC2[:, j * E2:(j + 1) * E2]
                    pe.matmul(dst, x4[:, j * 128:(j + 1) * 128], rw2[:, :], start=True, stop=False)
                    m = pe.matmul(dst, ones_row[:, :], rb2[:, :], start=False, stop=True)
                m.then_inc(logits2_in_psum, 1)
                up(0)
                up(1)
                if g < 3:
                    tensor_g_xnT(pe, g + 9, bank[5])
                pe.wait_ge(gates2_done, g + 1)
                for j in range(4):
                    m = pe.transpose(MISC2[0:E2, j * 128:(j + 1) * 128], r2["gate"][:, j, :], ident[:, :])
                m.then_inc(gT2_in_psum, 1)
                pe.wait_ge(gT2_done, g + 1)
                for i in range(1, 5):
                    pe.matmul(SETS2[(5 * g + i) % 2][2][:, :], pair_sel[:, PAIRS2[i], :], gT2[:, :], start=True, stop=True).then_inc(g2_in_psum, 1)
                    if i < 4:
                        up(i + 1)
                pe.wait_ge(h2_done, 5 * g + 5)
                for j in range(4):
                    for p in range(5):
                        m = pe.matmul(MISC2[:, j * D:(j + 1) * D], h2[:, p, j * 128:(j + 1) * 128], w2_2[:, p, :],
                                      start=(p == 0), stop=(p == 4))
                m.then_inc(out2_in_psum, 1)

        def vector_moe2(dve):
            steps = [0, 0]

            def link(ins):
                steps[0] += 1
                ins.then_inc(route2_step, 1)
                dve.wait_ge(route2_step, steps[0])

            def link2(ins):
                steps[1] += 1
                ins.then_inc(mul2_step, 1)
                dve.wait_ge(mul2_step, steps[1])

            def wide(a):
                return r2s[a][:, :].unsqueeze(2).to_broadcast([128, 4, E2])

            ranks = rank_w[:, :].unsqueeze(1).to_broadcast([128, 4, E2])
            lg = MISC2[:, 0:4 * E2].rearrange("p (j e) -> p j e", e=E2)

            def best(src, m, r, tmp, onehot):
                link(dve.tensor_reduce(r2s[m][:, :], src, AX.X, ALU.max))
                link(dve.tensor_tensor(r2[tmp][:, :, :], src, wide(m), ALU.is_equal))
                link(dve.tensor_tensor(r2["a"][:, :, :], r2[tmp][:, :, :], ranks, ALU.mult))
                link(dve.tensor_reduce(r2s[r][:, :], r2["a"][:, :, :], AX.X, ALU.max))
                link(dve.tensor_tensor(r2[onehot][:, :, :], r2["a"][:, :, :], wide(r), ALU.is_equal))

            def route(g):
                dve.wait_ge(logits2_in_psum, g + 1)
                best(lg, "m1", "r1", "rank", "first")
                link(dve.scalar_tensor_tensor(r2["rest"][:, :, :].rearrange("p j e -> p (j e)"), r2["first"][:, :, :].rearrange("p j e -> p (j e)"),
                                              MASKED, MISC2[:, 0:4 * E2], ALU.mult, ALU.add))
                best(r2["rest"][:, :, :], "m2", "r2", "rank2", "second")
                dve.tensor_tensor(r2s["d"][:, :], r2s["m2"][:, :], r2s["m1"][:, :], ALU.subtract).then_inc(gap2_done, 1)
                dve.wait_ge(gap2_exp, g + 1)
                link(dve.tensor_scalar(r2s["den"][:, :], r2s["e"][:, :], 1.0, None, ALU.add))
                link(dve.reciprocal(r2s["g1"][:, :], r2s["den"][:, :]))
                link(dve.tensor_tensor(r2s["g2"][:, :], r2s["e"][:, :], r2s["g1"][:, :], ALU.mult))
                dve.tensor_tensor(r2["a"][:, :, :], r2["first"][:, :, :], wide("g1"), ALU.mult)
                link(dve.tensor_tensor(r2["b"][:, :, :], r2["second"][:, :, :], wide("g2"), ALU.mult))
                dve.tensor_tensor(r2["gate"][:, :, :], r2["a"][:, :, :], r2["b"][:, :, :], ALU.add).then_inc(gates2_done, 1)

            def activate(g, i):
                n = 5 * g + i
                a, b, gate = SETS2[n % 2]
                u = u2[:, n % 2, :]
                p = PAIRS2[i]
                dve.wait_ge(tanh2_done, n + 1)
                link2(dve.scalar_tensor_tensor(u, th2[:, n % 2, :], 1.0, a[:, :], ALU.add, ALU.mult))
                if i == 0:
                    at_least(dve, out2_in_psum, g)
                    dve.scalar_tensor_tensor(h2[:, p, :], u, 0.5, b[:, :], ALU.mult, ALU.mult).then_inc(h2_done, 1)
                else:
                    link2(dve.tensor_tensor(u, u, b[:, :], ALU.mult))
                    dve.wait_ge(g2_in_psum, 4 * g + i)
                    dve.tensor_tensor(h2[:, p, :], u, gate[:, :], ALU.mult).then_inc(h2_done, 1)

            vector_g_stats(dve, 0, 12, 5 * B)
            vector_g_apply(dve, 0, 8, 12)
            for g in range(4):
                if g < 3:
                    vector_g_stats(dve, g + 1, g + 13, 5 * B)
                route(g)
                if g < 3:
                    vector_g_apply(dve, g + 1, g + 9, g + 13)
                for i in range(5):
                    activate(g, i)
                dve.wait_ge(out2_in_psum, g + 1)
                x4 = X[:, 4 * g:4 * g + 4, :].rearrange("p j d -> p (j d)")
                dve.scalar_tensor_tensor(x4, MISC2[:, :], tg[:, 6:7], x4, ALU.mult, ALU.add).then_inc(x_updated, 4)

        def scalar_moe2(act):
            def tanh(g, i):
                n = 5 * g + i
                act.wait_ge(ab2_in_psum, n + 1)
                act.activation(th2[:, n % 2, :], SETS2[n % 2][0][:, :], ACT.Tanh, scale=0.5).then_inc(tanh2_done, 1)

            scalar_g_xnT(act, 8, bank[5])
            for g in range(4):
                act.wait_ge(gap2_done, g + 1)
                act.activation(r2s["e"][:, :], r2s["d"][:, :], ACT.Exp).then_inc(gap2_exp, 1)
                tanh(g, 0)
                tanh(g, 1)
                if g < 3:
                    scalar_g_xnT(act, g + 9, bank[5])
                act.wait_ge(gT2_in_psum, g + 1)
                act.activation(gT2[:, :], MISC2[0:E2, :], ACT.Copy).then_inc(gT2_done, 1)
                for i in range(2, 5):
                    tanh(g, i)

        def gpsimd_moe2(pool):
            for k in range(12, 16):
                gpsimd_g_rstd(pool, k)

        RING3 = bank[0:4]
        PROJ3, SUMS3 = bank[4], [bank[7], bank[0]]
        CHUNKS3 = [(half, aux, odd) for aux in range(2) for half in range(2) for odd in range(2)]

        def heads3(half, odd):
            return slice(8 * half + odd, 8 * half + 8, 2)

        NORMS3 = 2 * B
        SCORES_RING3, EXP_RING3 = RING3[2:4], RING3[0:2]

        def turned3(b, more):
            return 5 * b + 5 + (1 if first(b) else 0) - (3 if more == 0 else 0)

        def first(b):
            return isinstance(b, int) and b == 0

        def tensor_attn3(pe):
            def project_early(b, u):
                pe.wait_ge(xnT_done, NORMS3 + b + 1)
                pe.wait_ge(ctx_b_done, B + b + 1)
                at_least(pe, v3_done, 2 * b)
                pe.matmul(PROJ3[:, 0:2 * D], xnT[:, u, :], wqkv3[:, 0:2 * D], start=True, stop=True)
                pe.matmul(PROJ3[0:T, 2 * D:3 * D], ctx_b[:, u, :], wkva3[:, 0:D], start=True, stop=True).then_inc(qkv3_in_psum, 1)

            def project_late(b, u):
                pe.wait_ge(proj3_done, 2 * b + 2)
                pe.matmul(PROJ3[:, 0:D], xnT[:, u, :], wqkv3[:, 2 * D:3 * D], start=True, stop=True)
                pe.matmul(PROJ3[0:T, D:2 * D], ctx_b[:, u, :], wkva3[:, D:2 * D], start=True, stop=True).then_inc(qkv3_in_psum, 1)

            def turn(b, u, n, free):
                src, p, w = ((sk3, 128, 128), (sa3, T, T + 1), (sq3[:, u], 128, 128))[n]
                at_least(pe, *free)
                pe.wait_ge(split3_done, 3 * b + n + 1)
                dst = T0[(n + 1) % 2][:, :].bitcast(BF16)
                for c in range(8):
                    m = pe.transpose(dst[:, c * w:c * w + p], src[:, 2 * c:2 * c + 2, :].rearrange("p a d -> p (a d)"),
                                     ident_b[0:p, 0:p])
                m.then_inc(t3_in_psum, 1)

            def output(b, count):
                pe.wait_ge(t3_done, count)
                pe.matmul(PROJ3[:, 3 * D:4 * D], oT3[:, :], wo3[:, :], start=True, stop=False)
                pe.matmul(PROJ3[:, 3 * D:4 * D], ones_row[:, :], bo3[:, :], start=False, stop=True).then_inc(wo3_in_psum, 1)

            def sums(b, u, aux, i):
                e, v = (ea3, va3) if aux else (em3, v3)
                for j in range(4):
                    m = pe.matmul(SUMS3[aux][32 * j:32 * j + 32, i * 128:(i + 1) * 128], v[:, u, 4 * i + j, :], e[:, 4 * i + j, :],
                                  start=True, stop=True)
                return m

            def scores(b, u, j):
                half, aux, odd = CHUNKS3[j]
                p, n = 64 * odd, (T if aux else 128)
                k = (kaT3 if aux else kT3)[:, u]
                at_least(pe, max3_done, 8 * b + j - 1)
                for i in range(4):
                    c = 4 * half + i
                    m = pe.matmul(SCORES_RING3[j % 2][:, i * n:(i + 1) * n], qT3[p:p + PARTS3, c, :], k[p:p + PARTS3, c, 0:n],
                                  start=True, stop=True)
                m.then_inc(s3_in_psum, 1)

            def scores_shifted(b, u, j):
                half, aux, odd = CHUNKS3[j]
                p, n = 64 * odd, (T if aux else 128)
                k = (kaT3 if aux else kT3)[:, u]
                if j < 2:
                    at_least(pe, o3_done, b)
                else:
                    pe.wait_ge(exp3_done, 8 * b + j - 1)
                for i in range(4):
                    c = 4 * half + i
                    m = pe.matmul(EXP_RING3[j % 2][0:n, i * 128:(i + 1) * 128], k[p:p + MAXES3, c, 0:n], qmT3[p:p + MAXES3, c, :],
                                  start=True, stop=True)
                m.then_inc(sT3_in_psum, 1)

            pe.wait_ge(attn3_loaded, 7 * 16)
            pe.wait_ge(x_updated, 6 * B)
            tensor_xnT(pe, NORMS3 + 0, 0, T0[0])
            tensor_xnT(pe, NORMS3 + 1, 1, T0[1])
            project_early(0, 0)
            project_late(0, 0)
            turn(0, 0, 0, (xnT_done, NORMS3 + 2))
            turn(0, 0, 1, (xnT_done, NORMS3 + 1))
            turn(0, 0, 2, (t3_done, 1))
            pe.wait_ge(t3_done, 2)
            tensor_xnT(pe, NORMS3 + 2, 0, T0[0])
            project_early(1, 1)
            project_late(1, 1)
            pe.wait_ge(t3_done, 3)
            for j in range(8):
                scores(0, 0, j)
            turn(1, 1, 0, (t3_done, 3))
            turn(1, 1, 1, (xnT_done, NORMS3 + 3))
            turn(1, 1, 2, (t3_done, 4))
            project_early(2, 0)

            def tile(b, u, more):
                t = turned3(b, more)
                o = 0 if first(b) else 1
                pe.wait_ge(t3_done, t)
                pe.wait_ge(maxcols3_done, b + 1)
                for c in range(8):
                    m = pe.transpose(T0[0][:, :].bitcast(BF16)[:, c * 128:(c + 1) * 128],
                                     sq3[:, u, 2 * c:2 * c + 2, :].rearrange("p a d -> p (a d)"), ident_b[:, :])
                m.then_inc(t3_in_psum, 1)
                if more >= 1:
                    scores(b + 1, 1 - u, 0)
                    scores(b + 1, 1 - u, 1)
                if o:
                    pe.wait_ge(o3_done, b)
                    pe.transpose(T0[1][:, 0:128], o3[:, :], ident[:, :]).then_inc(t3_in_psum, 1)
                    if more >= 2:
                        pe.wait_ge(proj3_done, 2 * b + 6)
                    output(b - 1, t + 2)
                pe.wait_ge(t3_done, t + 1)
                for j in range(8):
                    scores_shifted(b, u, j)
                    if more >= 1 and j < 6:
                        scores(b + 1, 1 - u, j + 2)
                    if j >= 4:
                        pe.wait_ge(exp3_done, 8 * b + 4)
                        m = sums(b, u, 0, j - 4)
                m.then_inc(av3_in_psum, 1)
                for i in range(4):
                    pe.wait_ge(exp3_done, 8 * b + (7 if i < 2 else 8))
                    m = sums(b, u, 1, i)
                m.then_inc(av3_in_psum, 1)
                if o:
                    pe.wait_ge(x_updated, 6 * B + b)
                if more >= 2:
                    project_late(b + 2, u)
                if more >= 3:
                    pe.wait_ge(t3_done, t + 1)
                    tensor_xnT(pe, NORMS3 + b + 3, 1 - u, T0[0])
                if more >= 2:
                    turn(b + 2, u, 0, (t3_done, t + 2 * o))
                    turn(b + 2, u, 1, (xnT_done, NORMS3 + b + 4) if more >= 3 else (t3_done, t + 1))
                pe.wait_ge(ovT3_done, 2 * b + 2)
                for aux in range(2):
                    for i in range(4):
                        m = pe.transpose(SUMS3[aux][:, i * 128:(i + 1) * 128], ovT3[:, aux, i, :], ident[:, :])
                m.then_inc(av3_in_psum, 1)
                if more >= 2:
                    turn(b + 2, u, 2, (t3_done, t + o + 2))
                if more >= 3:
                    project_early(b + 3, 1 - u)
            over_tiles(pe, tile, 2)
            pe.wait_ge(o3_done, B)
            pe.transpose(T0[1][:, 0:128], o3[:, :], ident[:, :]).then_inc(t3_in_psum, 1)
            output(B - 1, 5 * B)

        def vector_attn3(dve):
            def early(b, u):
                dve.wait_ge(qkv3_in_psum, 2 * b + 1)
                at_least(dve, split3_done, 3 * b)
                dve.tensor_tensor(qk3[:, :, :, :].rearrange("p a h d -> p (a h d)"), PROJ3[:, 0:2 * D], bqkv3[:, 0:2 * D], ALU.add).then_inc(proj3_done, 1)
                dve.tensor_tensor(ka3[:, :, :].rearrange("p h d -> p (h d)"), PROJ3[0:T, 2 * D:3 * D], bkva3[:, 0:D], ALU.add).then_inc(proj3_done, 1)

            def late(b, u):
                dve.wait_ge(qkv3_in_psum, 2 * b + 2)
                dve.tensor_tensor(v3[:, u, :, 0:8], PROJ3[:, 0:D].rearrange("p (h d) -> p h d", d=8),
                                  bqkv3[:, 2 * D:3 * D].rearrange("p (h d) -> p h d", d=8), ALU.add).then_inc(v3_done, 1)
                dve.tensor_tensor(va3[:, u, :, 0:8], PROJ3[0:T, D:2 * D].rearrange("p (h d) -> p h d", d=8),
                                  bkva3[:, D:2 * D].rearrange("p (h d) -> p h d", d=8), ALU.add).then_inc(v3_done, 1)

            def update(b):
                dve.wait_ge(wo3_in_psum, b + 1)
                dve.scalar_tensor_tensor(slot(b), PROJ3[:, 3 * D:4 * D], tg[:, 3:4], slot(b), ALU.mult, ALU.add).then_inc(x_updated, 1)

            def maxima(b, first_chunk, last_chunk):
                for j in range(first_chunk, last_chunk):
                    half, aux, odd = CHUNKS3[j]
                    n = T if aux else 128
                    dve.wait_ge(s3_in_psum, 8 * b + j + 1)
                    dve.tensor_reduce(mx3[:, aux, heads3(half, odd)], SCORES_RING3[j % 2][:, 0:4 * n].rearrange("p (h k) -> p h k", k=n),
                                      AX.X, ALU.max, negate=True).then_inc(max3_done, 1)

            def split_maxima(b, u):
                cols = sq3[:, u, :, PARTS3:MAXES3].rearrange("p h (a c) -> p h a c", c=3)
                m = mx3[:, :, :].rearrange("p a h -> p h a")
                left = mleft3[:, :, :].rearrange("p a h -> p h a")
                dve.wait_ge(max3_done, 8 * b + 8)
                dve.tensor_copy(cols[:, :, :, 0], m).then_inc(maxsplit3_step, 1)
                dve.wait_ge(maxsplit3_step, 3 * b + 3)
                dve.tensor_tensor(left, m, cols[:, :, :, 0], ALU.subtract).then_inc(maxsplit3_step, 1)
                dve.wait_ge(maxsplit3_step, 3 * b + 4)
                dve.tensor_copy(cols[:, :, :, 1], left).then_inc(maxsplit3_step, 1)
                dve.wait_ge(maxsplit3_step, 3 * b + 5)
                dve.tensor_tensor(cols[:, :, :, 2], left, cols[:, :, :, 1], ALU.subtract).then_inc(maxcols3_done, 1)

            vector_ln_stats(dve, 0, NORMS3 + 0, 0, 6 * B)
            vector_ln_apply(dve, 0, NORMS3 + 0, 0)
            vector_ln_stats(dve, 1, NORMS3 + 1, 1, 6 * B)
            vector_ln_apply(dve, 1, NORMS3 + 1, 1)
            dve.wait_ge(g3_tanh_done, 1)
            dve.tensor_scalar(gate3[:, 1, :], g3_tanh[:, :], 0.5, 0.5, ALU.mult, ALU.add).then_inc(maxsplit3_step, 1)
            dve.wait_ge(maxsplit3_step, 1)
            dve.tensor_scalar(gate3[:, 0, :], gate3[:, 1, :], -1.0, 1.0, ALU.mult, ALU.add).then_inc(maxsplit3_step, 1)
            dve.wait_ge(stack3_ready, 2)
            vector_ln_stats(dve, 2, NORMS3 + 2, 0, 6 * B)
            early(0, 0)
            late(0, 0)
            vector_ln_apply(dve, 2, NORMS3 + 2, 0)
            vector_ln_stats(dve, 3, NORMS3 + 3, 1, 6 * B)
            early(1, 1)
            late(1, 1)
            maxima(0, 0, 8)
            split_maxima(0, 0)

            def tile(b, u, more):
                if more >= 2:
                    early(b + 2, u)
                if more >= 1:
                    maxima(b + 1, 0, 2)
                if not first(b):
                    update(b - 1)
                if more >= 1:
                    maxima(b + 1, 2, 4)
                if more >= 3:
                    vector_ln_apply(dve, b + 3, NORMS3 + b + 3, 1 - u)
                if more >= 4:
                    vector_ln_stats(dve, b + 4, NORMS3 + b + 4, u)
                if more >= 1:
                    maxima(b + 1, 4, 8)
                    split_maxima(b + 1, 1 - u)
                for aux in range(2):
                    dve.wait_ge(av3_in_psum, 3 * b + 1 + aux)
                    dve.tensor_copy(ovT3[:, aux, :, :].rearrange("p i q -> p (i q)"), SUMS3[aux][:, :]).then_inc(ovT3_done, 1)
                if more >= 2:
                    late(b + 2, u)
                sums = [SUMS3[aux][:, :].rearrange("p (h d) -> p h d", d=32) for aux in range(2)]
                dve.wait_ge(av3_in_psum, 3 * b + 3)
                for aux in range(2):
                    dve.reciprocal(rs3[:, aux, :], sums[aux][:, :, 8]).then_inc(o3_step, 1)
                dve.wait_ge(o3_step, 5 * b + 2)
                dve.tensor_tensor(rg3[:, :, :], rs3[:, :, :], gate3[:, :, :], ALU.mult).then_inc(o3_step, 1)
                dve.wait_ge(o3_step, 5 * b + 3)
                for aux in range(2):
                    dve.tensor_tensor(ov3[:, aux, :, :], sums[aux][:, :, 0:8], rg3[:, aux, :].unsqueeze(2).to_broadcast([128, H3, 8]),
                                      ALU.mult).then_inc(o3_step, 1)
                dve.wait_ge(o3_step, 5 * b + 5)
                dve.tensor_tensor(o3[:, :], ov3[:, 0, :, :].rearrange("p h d -> p (h d)"), ov3[:, 1, :, :].rearrange("p h d -> p (h d)"),
                                  ALU.add).then_inc(o3_done, 1)
            over_tiles(dve, tile, 2)
            update(B - 1)

        def scalar_attn3(act):
            def stack(u, n, count):
                dst, w = ((kT3[:, u], 128), (kaT3[:, u], T + 1), (qT3, 128))[n]
                k = T if n == 1 else w
                act.wait_ge(t3_in_psum, count)
                src = T0[(n + 1) % 2][:, :].bitcast(BF16)[:, 0:8 * w].rearrange("p (c k) -> p c k", k=w)
                act.activation(dst[:, :, 0:k], src[:, :, 0:k], ACT.Copy).then_inc(t3_done, 1)

            def turned_outputs(count):
                act.wait_ge(t3_in_psum, count)
                act.activation(oT3[:, :], T0[1][:, 0:128], ACT.Copy).then_inc(t3_done, 1)

            scalar_xnT(act, NORMS3 + 0, 0, T0[0])
            scalar_xnT(act, NORMS3 + 1, 1, T0[1])
            for n in range(3):
                stack(0, n, n + 1)
            scalar_xnT(act, NORMS3 + 2, 0, T0[0])
            for n in range(3):
                stack(1, n, n + 4)

            def tile(b, u, more):
                t = turned3(b, more)
                o = 0 if first(b) else 1
                act.wait_ge(t3_in_psum, t + 1)
                act.activation(qmT3[:, :, :].rearrange("p c k -> p (c k)"), T0[0][:, :].bitcast(BF16)[:, :], ACT.Copy).then_inc(t3_done, 1)
                if o:
                    turned_outputs(t + 2)
                for j, (half, aux, odd) in enumerate(CHUNKS3):
                    n = T if aux else 128
                    act.wait_ge(sT3_in_psum, 8 * b + j + 1)
                    act.activation((ea3 if aux else em3)[:, heads3(half, odd), :], EXP_RING3[j % 2][0:n, :].rearrange("p (h q) -> p h q", q=128),
                                   ACT.Exp, scale=8 ** -0.5).then_inc(exp3_done, 1)
                if more >= 3:
                    scalar_xnT(act, NORMS3 + b + 3, 1 - u, T0[0])
                if more >= 2:
                    for n in range(3):
                        stack(u, n, t + o + 2 + n)
            over_tiles(act, tile, 2)
            turned_outputs(5 * B)

        def gpsimd_attn3(pool):
            pool.wait_ge(x_updated, 2 * B)
            pool.memset(sq3[:, :, :, :], 0.0)
            pool.memset(sk3[:, :, :], 0.0)
            pool.memset(sa3[:, :, :], 0.0)
            pool.wait_ge(x_updated, 6 * B)
            pool.memset(v3[:, :, :, :], 0.0)
            pool.memset(va3[:, :, :, :], 0.0).then_inc(stack3_ready, 1)
            pool.wait_ge(stack3_ready, 1)
            pool.memset(v3[:, :, :, 8:9], 1.0)
            pool.memset(va3[:, :, :, 8:9], 1.0)
            pool.memset(sk3[:, :, PARTS3:PARTS3 + 3], 1.0)
            pool.memset(sa3[:, :, PARTS3 + 3:MAXES3], 1.0).then_inc(stack3_ready, 1)
            pool.wait_ge(stack3_ready, 2)

            def context(b, u):
                at_least(pool, qkv3_in_psum, 2 * b - 2)
                pool.tensor_tensor(ctx_b[:, u, :], ctxT[:, bass.ds(b, 1), :].rearrange("p a t -> p (a t)"),
                                   zero[:, 0:1].to_broadcast([128, T]), ALU.add).then_inc(ctx_b_done, 1)

            def part(stack, n, slots):
                first, step, count = slots
                v = stack[:, :, 0:PARTS3].rearrange("p h (s d) -> p h s d", d=8)
                return v[:, :, first:first + step * (count - 1) + 1:step, :]

            def split(b, u, q_free=0):
                Q_AT = ((0, 1, 3), (3, 1, 2), (5, 1, 1))
                K_AT = ((0, 3, 2), (1, 3, 2), (2, 1, 1))
                work = ((qk3[:, 1], sk3, 128, K_AT), (ka3[:, :, :], sa3, T, K_AT), (qk3[:, 0], sq3[:, u], 128, Q_AT))
                pool.wait_ge(proj3_done, 2 * b + 2)
                for n, (x, stack, p, at) in enumerate(work):
                    left = left3[n][0:p, :, :]
                    if n == 2:
                        at_least(pool, t3_in_psum, q_free)

                    def spread(src, slots):
                        return src.unsqueeze(2).to_broadcast([p, H3, slots[2], 8])

                    def nothing(slots):
                        return zero[0:p, :].unsqueeze(2).unsqueeze(3).to_broadcast([p, H3, slots[2], 8])
                    pool.tensor_tensor(part(stack, n, at[0]), spread(x, at[0]), nothing(at[0]), ALU.add).then_inc(split3_step, 1)
                    if n < 2:
                        pool.tensor_copy(part(stack, n, (5, 1, 1))[:, :, 0, :], x)
                    pool.wait_ge(split3_step, 9 * b + 3 * n + 1)
                    pool.tensor_tensor(left, x, stack[:, :, 0:8], ALU.subtract).then_inc(split3_step, 1)
                    pool.wait_ge(split3_step, 9 * b + 3 * n + 2)
                    pool.tensor_tensor(part(stack, n, at[1]), spread(left, at[1]), nothing(at[1]), ALU.add).then_inc(split3_step, 1)
                    pool.wait_ge(split3_step, 9 * b + 3 * n + 3)
                    pool.tensor_tensor(part(stack, n, at[2])[:, :, 0, :], left, part(stack, n, at[1])[:, :, 0, :], ALU.subtract).then_inc(split3_done, 1)

            gpsimd_ln_rstd(pool, NORMS3 + 0, 0)
            gpsimd_ln_rstd(pool, NORMS3 + 1, 1)
            context(0, 0)
            context(1, 1)
            gpsimd_ln_rstd(pool, NORMS3 + 2, 0)
            split(0, 0)
            context(2, 0)
            gpsimd_ln_rstd(pool, NORMS3 + 3, 1)
            split(1, 1)
            context(3, 1)

            def tile(b, u, more):
                if more >= 2:
                    split(b + 2, u, turned3(b, more) + 1)
                if more >= 4:
                    gpsimd_ln_rstd(pool, NORMS3 + b + 4, u)
                    context(b + 4, u)
            over_tiles(pool, tile, 2)

        D_BANK = bank[0:4]
        LOGITS3, PT_BANK = bank[6], bank[4]
        IN_BANK = bank[4:8]
        F_BANK = [bank[0:4], bank[4:8]]
        ROWS_BANK, COMB_BANK = bank[0:2], bank[2:4]

        def tensor_moe3(pe):
            pe.wait_ge(moe3_loaded, 4 * 16)
            pe.wait_ge(x_updated, 7 * B)
            tensor_g_xnT(pe, 12, bank[5])
            for g in range(4):
                pe.wait_ge(g_xnT_done, g + 13)
                pe.matmul(LOGITS3[:, :], ctrl3[:, :], xnT4[:, g % 2, :], start=True, stop=True).then_inc(l3_in_psum, 1)
                pe.wait_ge(perm3_done, g + 1)
                at_least(pe, pt3_done, g)
                for j in range(4):
                    tok = (4 * g + j) * 128
                    m = pe.transpose(PT_BANK[:, j * 128:(j + 1) * 128], perm3[:, tok:tok + 128], ident[:, :])
                m.then_inc(pt3_in_psum, 1)
                if g < 3:
                    tensor_g_xnT(pe, g + 13, bank[5])
                pe.wait_ge(pt3_done, g + 1)
                at_least(pe, d3_act_done, 2 * g)
                at_least(pe, d3_dve_done, 2 * g)
                for j in range(4):
                    for r in range(4):
                        p = slice(G3 * r, G3 * r + G3)
                        m = pe.matmul(D_BANK[r][:, j * 128:(j + 1) * 128], xn4[p, g % 2, j, :], pt3[p, g % 2, j, :], start=True, stop=True)
                m.then_inc(d3_in_psum, 1)
            pe.wait_ge(f1_loaded, 16)
            pe.wait_ge(d3_act_done, 8)
            pe.wait_ge(d3_dve_done, 8)
            for e in range(E3):
                for s_ in range(SETS3):
                    m = pe.matmul(IN_BANK[e // 8][F3 * s_:F3 * s_ + F3, (e % 8) * NG3:(e % 8 + 1) * NG3], f1_3[:, SETS3 * e + s_, :],
                                  d3[:, :, SETS3 * e + s_], start=True, stop=True)
                if e % 8 == 7:
                    m.then_inc(in3_in_psum, 1)
            for r in range(4):
                pe.wait_ge(in3_done, r + 1 if r % 2 == 0 else 4)
                if r >= 2:
                    pe.wait_ge(out3_act_done, 2 * (r - 1))
                    pe.wait_ge(out3_dve_done, 2 * (r - 1))
                for e in range(8 * r, 8 * r + 8):
                    for s_ in range(SETS3):
                        p = slice(F3 * s_, F3 * s_ + F3)
                        m = pe.matmul(F_BANK[r % 2][s_][:, (e % 8) * NG3:(e % 8 + 1) * NG3], f2_3[p, e, :], in3[p, e, :], start=True, stop=True)
                m.then_inc(f3_in_psum, 1)
            pe.wait_ge(out3_act_done, 8)
            pe.wait_ge(out3_dve_done, 8)

            def rows(b):
                at_least(pe, rows3_done, b - 1)
                for r in range(4):
                    m = pe.transpose(ROWS_BANK[b % 2][:, r * 128:(r + 1) * 128], out3[:, 4 * b + r, :], ident[:, :])
                m.then_inc(rows3_in_psum, 1)

            rows(0)
            for b in range(B):
                if b + 1 < B:
                    rows(b + 1)
                pe.wait_ge(rows3_done, b + 1)
                at_least(pe, x_updated, 7 * B + b - 1)
                for r in range(4):
                    tok = 128 * b + G3 * r
                    m = pe.matmul(COMB_BANK[b % 2][G3 * r:G3 * r + G3, 0:D], perm3[:, tok:tok + G3], rows3[:, b % 2, r, :], start=True, stop=True)
                m.then_inc(comb3_in_psum, 1)

        def d3_view(g, r):
            return d3[:, 16 * g + r:16 * g + 13 + r:4, :]

        def out3_view(r, s_):
            at = 8 * SETS3 * r + s_
            return out3[:, :, at:at + 7 * SETS3 + 1:SETS3].rearrange("p g e -> p e g")

        def vector_moe3(dve):
            steps = [0]

            def link(ins):
                steps[0] += 1
                ins.then_inc(tie3_step, 1)
                dve.wait_ge(tie3_step, steps[0])

            vector_g_stats(dve, 0, 16, 7 * B)
            vector_g_apply(dve, 0, 12, 16)
            dve.wait_ge(moe3_loaded, 4 * 16)
            for g in range(4):
                if g < 3:
                    vector_g_stats(dve, g + 1, g + 17, 7 * B)
                dve.wait_ge(l3_in_psum, g + 1)
                lt = tmp512[:, g % 2, :].rearrange("p (g t) -> p g t", t=G3)
                link(dve.tensor_tensor(lt, LOGITS3[:, :].rearrange("p (g t) -> p g t", t=G3), tie3[:, :].unsqueeze(1).to_broadcast([128, 16, G3]), ALU.add))
                link(dve.tensor_reduce(gmax3[:, :], lt, AX.X, ALU.max))
                dve.tensor_tensor(perm3[:, g * 512:(g + 1) * 512].rearrange("p (g t) -> p g t", t=G3), lt,
                                  gmax3[:, :].unsqueeze(2).to_broadcast([128, 16, G3]), ALU.is_equal).then_inc(perm3_done, 1)
                if g < 3:
                    vector_g_apply(dve, g + 1, g + 13, g + 17, g)
                dve.wait_ge(d3_in_psum, g + 1)
                for r in (2, 3):
                    dve.tensor_copy(d3_view(g, r), D_BANK[r][:, :].rearrange("p (j e) -> p j e", e=ES3)).then_inc(d3_dve_done, 1)
            for r in range(4):
                dve.wait_ge(in3_in_psum, r + 1)
                dve.tensor_tensor(in3[:, 8 * r:8 * r + 8, :], IN_BANK[r][:, :].rearrange("p (e g) -> p e g", g=NG3),
                                  bias3[:, 8 * r:8 * r + 8].unsqueeze(2).to_broadcast([128, 8, NG3]), ALU.add).then_inc(in3_biased, 1)
            for r in range(4):
                dve.wait_ge(f3_in_psum, r + 1)
                for s_ in (2, 3):
                    dve.tensor_copy(out3_view(r, s_), F_BANK[r % 2][s_][:, :].rearrange("p (e g) -> p e g", g=NG3)).then_inc(out3_dve_done, 1)
            for b in range(B):
                dve.wait_ge(comb3_in_psum, b + 1)
                dve.scalar_tensor_tensor(X[:, b, :], COMB_BANK[b % 2][:, 0:D], tg[:, 7:8], X[:, b, :], ALU.mult, ALU.add).then_inc(x_updated, 1)

        def scalar_moe3(act):
            scalar_g_xnT(act, 12, bank[5])
            for g in range(4):
                act.wait_ge(pt3_in_psum, g + 1)
                act.activation(pt3[:, g % 2, :, :].rearrange("p j e -> p (j e)"), PT_BANK[:, :], ACT.Copy).then_inc(pt3_done, 1)
                if g < 3:
                    scalar_g_xnT(act, g + 13, bank[5])
                act.wait_ge(d3_in_psum, g + 1)
                for r in (0, 1):
                    act.activation(d3_view(g, r), D_BANK[r][:, :].rearrange("p (j e) -> p j e", e=ES3), ACT.Copy).then_inc(d3_act_done, 1)
            for r in range(4):
                act.wait_ge(in3_biased, r + 1)
                v = in3[:, 8 * r:8 * r + 8, :]
                act.activation(v, v, ACT.Relu).then_inc(in3_done, 1)
            for r in range(4):
                act.wait_ge(f3_in_psum, r + 1)
                for s_ in (0, 1):
                    act.activation(out3_view(r, s_), F_BANK[r % 2][s_][:, :].rearrange("p (e g) -> p e g", g=NG3), ACT.Copy).then_inc(out3_act_done, 1)
            for b in range(B):
                act.wait_ge(rows3_in_psum, b + 1)
                at_least(act, comb3_in_psum, b - 1)
                act.activation(rows3[:, b % 2, :, :].rearrange("p r d -> p (r d)"), ROWS_BANK[b % 2][:, :], ACT.Copy).then_inc(rows3_done, 1)

        def gpsimd_moe3(pool):
            for k in range(16, 20):
                gpsimd_g_rstd(pool, k)

        @block.sync
        def _(sp):
            sp.dma_start(X[:, :, :], t["x"]).then_inc(x_loaded, 16)
            sp.dma_start(ident[:, :], t["ident"]).then_inc(const_loaded, 16)
            sp.dma_start(ident_b[:, :], t["ident_b"]).then_inc(const_loaded, 16)
            sp.dma_start(gates_in[:, :], t["gates"]).then_inc(const_loaded, 16)
            sp.dma_start(ones[:, :], t["ones"]).then_inc(const_loaded, 16)
            sp.dma_start(ctxT[:, :, :], t["ctxT"]).then_inc(ctx_loaded, 16)
            sp.dma_start(wq0[:, :], t["wq0"]).then_inc(wqkv0_loaded, 16)
            sp.dma_start(bq0[:, :], t["bq0"]).then_inc(wqkv0_loaded, 16)
            sp.dma_start(bk0[:, :], t["bk0"]).then_inc(wqkv0_loaded, 16)
            sp.dma_start(wk0[:, :], t["wk0"]).then_inc(wqkv0_loaded, 16)
            sp.dma_start(wv0[:, :], t["wv0"]).then_inc(wqkv0_loaded, 16)
            sp.dma_start(bv0[:, :, :], t["bv0"]).then_inc(wqkv0_loaded, 16)
            sp.dma_start(wo0[:, :, :], t["wo0"]).then_inc(wo0_loaded, 16)
            sp.dma_start(bo0[:, :], t["bo0"]).then_inc(wo0_loaded, 16)
            for name, dst in (("wg0", wg0), ("rank_w", rank_w), ("slot_base", slot_base), ("spare_slot", spare_slot),
                              ("tri_b", tri_b), ("ones_b", ones_b)):
                sp.dma_start(dst[:, :], t[name]).then_inc(route0_loaded, 16)
            sp.wait_ge(pool_ready, 4)
            sp.dma_start(t["x_slots"][0:NT, :].rearrange("(t p) d -> p t d", p=128), XN[:, :, :]).then_inc(slots_zeroed, 16)
            for dst, name in ((w1x, "w1x"), (w2x, "w2x"), (bx, "bx")):
                sp.dma_start(dst[:, :], t[name]).then_inc(mix_loaded, 16)
            for g in range(2):
                sp.dma_start(wgu1[:, g, 0:2, :], t["wgu1"][g, 0:256, :].rearrange("(c p) d -> p c d", p=128)).then_inc(ffn1_loaded, 16)
            sp.dma_start(wgu1[0:I1 - 256, :, 2, :], t["wgu1"][:, 256:I1, :].rearrange("g p d -> p g d")).then_inc(ffn1_loaded, 16)
            sp.dma_start(wd1[:, :], t["wd1"]).then_inc(ffn1_loaded, 16)
            sp.dma_start(clips[:, :], t["clips"]).then_inc(ffn1_loaded, 16)
            for dst, name in ((wqkv2[:, :, :], "wqkv2"), (bqk2[:, 0:1], "bq2"), (bqk2[:, 1:2], "bk2"), (bv2[:, :], "bv2")):
                sp.dma_start(dst, t[name]).then_inc(attn2_loaded, 16)
            for dst, name in ((rw2[:, :], "rw2"), (rb2[:, :], "rb2"), (pair_sel[:, :, :], "pair_sel")):
                sp.dma_start(dst, t[name]).then_inc(moe2_loaded, 16)
            for dst, name in ((wqkv3, "wqkv3"), (wkva3, "wkva3"), (bqkv3, "bqkv3"), (bkva3, "bkva3"), (wo3, "wo3"), (bo3, "bo3"), (g3, "g3")):
                sp.dma_start(dst[:, :], t[name]).then_inc(attn3_loaded, 16)
            for dst, name in ((f2_3[:, :, :], "f2_3"), (ctrl3[:, :], "ctrl3"), (tie3[:, :], "tie3"), (bias3[:, :], "bias3")):
                sp.dma_start(dst, t[name]).then_inc(moe3_loaded, 16)
            sp.wait_ge(x_updated, B)
            for dst, name in ((w13_2[:, :, :, :], "w13_2"), (w2_2[:, :, :], "w2_2")):
                sp.dma_start(dst, t[name]).then_inc(moe2_loaded, 16)
            if LAST_STAGE >= 2:
                sync_moe0(sp)
            if LAST_STAGE >= 8:
                sp.wait_ge(x_updated, 6 * B)
                sp.dma_start(f1_3, t["f1_3"]).then_inc(f1_loaded, 16)
            sp.wait_ge(x_updated, 16 * LAST_STAGE)
            sp.dma_start(t["out"], X[:, :, :]).then_inc(out_stored, 16)
            sp.wait_ge(out_stored, 16)

        @block.gpsimd
        def _(pool):
            pool.memset(minus_half[:, :], -0.5)
            pool.memset(zero[:, :], 0.0)
            pool.memset(minus_magic[:, :], -MAGIC)
            pool.memset(eps[:, :], LN_EPS).then_inc(pool_ready, 1)
            pool.memset(kT[:, :, :], 0.0).then_inc(pool_ready, 1)
            pool.wait_ge(mask_loaded, 16)
            pool.tensor_scalar(mask_bias[:, :, :], mask_u8[:, :, :], -MASKED, MASKED, ALU.mult, ALU.add).then_inc(pool_ready, 1)
            pool.memset(XN[:, :, :], 0.0).then_inc(pool_ready, 1)
            gpsimd_attn0(pool)
            pool.wait_ge(slots_zeroed, 16)
            if LAST_STAGE >= 2:
                gpsimd_moe0(pool)
            if LAST_STAGE >= 3:
                gpsimd_mix1(pool)
            if LAST_STAGE >= 5:
                gpsimd_attn2(pool)
            if LAST_STAGE >= 6:
                gpsimd_moe2(pool)
            if LAST_STAGE >= 7:
                gpsimd_attn3(pool)
            if LAST_STAGE >= 8:
                gpsimd_moe3(pool)

        @block.scalar
        def _(act):
            act.dma_start(mask_u8[:, :, :], t["mask"]).then_inc(mask_loaded, 16)
            act.wait_ge(const_loaded, 4 * 16)
            act.activation(tg[:, :], gates_in[:, :], ACT.Tanh).then_inc(tg_ready, 1)
            scalar_attn0(act)
            act.wait_ge(ffn1_loaded, 5 * 16)
            act.activation(clip_tanh[:, :], clips[:, :], ACT.Tanh, scale=0.5).then_inc(clip_tanh_done, 1)
            act.wait_ge(attn3_loaded, 7 * 16)
            act.activation(g3_tanh[:, :], g3[:, :], ACT.Tanh, scale=0.5).then_inc(g3_tanh_done, 1)
            if LAST_STAGE >= 2:
                scalar_moe0(act)
            if LAST_STAGE >= 3:
                scalar_mix1(act)
            if LAST_STAGE >= 4:
                scalar_ffn1(act)
            if LAST_STAGE >= 5:
                scalar_attn2(act)
            if LAST_STAGE >= 6:
                scalar_moe2(act)
            if LAST_STAGE >= 7:
                scalar_attn3(act)
            if LAST_STAGE >= 8:
                scalar_moe3(act)

        @block.vector
        def _(dve):
            vector_attn0(dve)
            if LAST_STAGE >= 2:
                vector_moe0(dve)
            if LAST_STAGE >= 3:
                vector_mix1(dve)
            if LAST_STAGE >= 4:
                vector_ffn1(dve)
            if LAST_STAGE >= 5:
                vector_attn2(dve)
            if LAST_STAGE >= 6:
                vector_moe2(dve)
            if LAST_STAGE >= 7:
                vector_attn3(dve)
            if LAST_STAGE >= 8:
                vector_moe3(dve)

        @block.tensor
        def _(pe):
            tensor_attn0(pe)
            if LAST_STAGE >= 2:
                tensor_moe0(pe)
            if LAST_STAGE >= 3:
                tensor_mix1(pe)
            if LAST_STAGE >= 4:
                tensor_ffn1(pe)
            if LAST_STAGE >= 5:
                tensor_attn2(pe)
            if LAST_STAGE >= 6:
                tensor_moe2(pe)
            if LAST_STAGE >= 7:
                tensor_attn3(pe)
            if LAST_STAGE >= 8:
                tensor_moe3(pe)


def kernel(**inputs):
    import numpy as np
    from concourse.bass_utils import run_bass_kernel_spmd

    a = {k: np.asarray(v) for k, v in inputs.items()}

    def rows(v, n):
        v = np.asarray(v)
        return np.broadcast_to(v.reshape(1, -1), (n, v.size))

    def pairs(routed, shared):
        both = np.concatenate([routed, shared])
        return both.reshape(5, 2, *both.shape[1:])

    ins = {
        "x": a["x"].transpose(1, 0, 2),
        "ctxT": a["ctx_1024"].transpose(2, 0, 1),
        "mask": a["mask_BxSxS2_bk1"].transpose(1, 0, 2),
        "ident": np.eye(128, dtype=np.float32),
        "ident_b": np.eye(128, dtype=mybir.dt.np(BF16)),
        "ones": np.ones((128, 128), np.float32),
        "gates": rows(np.concatenate([a["g_xattn"], a["g_ffn"]]), 128),
        "wq0": a["L0_xattn_wq"].transpose(1, 0, 2).reshape(128, 1024),
        "wk0": a["L0_xattn_wk"].transpose(1, 0, 2).reshape(128, 1024),
        "wv0": a["L0_xattn_wv"].transpose(1, 0, 2).reshape(128, 1024),
        "wo0": a["L0_xattn_wo"].reshape(8, 128, 128).transpose(1, 0, 2),
        "bq0": a["L0_xattn_bq"].reshape(8, 128).T,
        "bk0": a["L0_xattn_bk"].reshape(8, 128).T,
        "bv0": rows(a["L0_xattn_bv"], T).reshape(T, H0, DK0),
        "bo0": a["L0_xattn_bo"].reshape(1, 128),
        "wg0": a["L0_ffn_wg"],
        "w1x": a["L1_xattn_W"][:, :D].T,
        "w2x": a["L1_xattn_W"][:, D:].T,
        "bx": a["L1_xattn_b"].reshape(1, D),
        "wgu1": np.stack([a["L1_ffn_w_gate"], a["L1_ffn_w_up"]]),
        "wd1": a["L1_ffn_w_down"],
        "wqkv2": np.stack([a["L2_xattn_Wq"], a["L2_xattn_Wk"], a["L2_xattn_Wv"]]).transpose(1, 0, 2),
        "bq2": a["L2_xattn_bq"].reshape(D, 1),
        "bk2": a["L2_xattn_bk"].reshape(D, 1),
        "bv2": rows(a["L2_xattn_bv"], T),
        "rw2": a["L2_ffn_router_w"],
        "rb2": a["L2_ffn_router_b"].reshape(1, E2),
        "w13_2": np.stack([pairs(a[f"L2_ffn_routed_{w}"], a[f"L2_ffn_shared_{w}"]).transpose(2, 0, 1, 3).reshape(D, 5, 128)
                           for w in ("w1", "w3")], axis=1),
        "w2_2": pairs(a["L2_ffn_routed_w2"], a["L2_ffn_shared_w2"]).reshape(5, 128, D).transpose(1, 0, 2),
        "pair_sel": 0.5 * np.kron(np.eye(E2, dtype=np.float32), np.ones((1, H2), np.float32)).reshape(E2, 4, 128),
        "wqkv3": a["L3_xattn_Wqkv"],
        "wkva3": a["L3_xattn_Wqkv_aux"][:, D:],
        "bqkv3": rows(a["L3_xattn_bqkv"], 128),
        "bkva3": rows(a["L3_xattn_bqkv_aux"][D:], T),
        "wo3": a["L3_xattn_Wo"],
        "bo3": a["L3_xattn_bo"].reshape(1, D),
        "g3": rows(a["L3_xattn_g"], 128),
        "f1_3": a["L3_ffn_f1"].reshape(D, ES3, F3),
        "f2_3": a["L3_ffn_f2"].transpose(1, 2, 0, 3).reshape(SETS3 * F3, E3, D),
        "ctrl3": a["L3_ffn_controller"].reshape(D, ES3),
        "tie3": rows(np.linspace(0.0, 1e-06, G3, dtype=np.float32), 128),
        "bias3": a["L3_ffn_bias"].transpose(1, 2, 0).reshape(SETS3 * F3, E3),
        "clips": rows(np.concatenate([a["L1_ffn_clip_x"], a["L1_ffn_clip_down"]]), 128),
        "rank_w": rows(np.arange(E0, 0, -1, dtype=np.float32), 128),
        "slot_base": rows(np.arange(E0, dtype=np.float32) * C0 - 1, 128),
        "spare_slot": NT + np.arange(NT, dtype=np.float32).reshape(B, 128).T,
        "tri_b": np.triu(np.ones((128, 128))).astype(mybir.dt.np(BF16)),
        "ones_b": np.ones((128, 128)).astype(mybir.dt.np(BF16)),
        "w1_0": a["L0_ffn_w1"],
        "w2_0": a["L0_ffn_w2"],
        "b1_0": a["L0_ffn_b1"].reshape(E0, FC0, 128).transpose(0, 2, 1),
        "b2_0": a["L0_ffn_b2"].reshape(E0, 1, D),
    }
    ins = {k: np.ascontiguousarray(v) for k, v in ins.items()}
    nc = bacc.Bacc("TRN2", target_bir_lowering=False, num_devices=1)
    t = {k: nc.dram_tensor(f"in_{k}", v.shape, mybir.dt.from_np(v.dtype), kind="ExternalInput").ap() for k, v in ins.items()}
    t["out"] = nc.dram_tensor("out", (S, B, D), F32, kind="ExternalOutput").ap()
    t["x_slots"] = nc.dram_tensor("x_slots", (2 * NT, D), F32, kind="Internal").ap()
    t["y_slots"] = nc.dram_tensor("y_slots", (NT, D), F32, kind="Internal").ap()
    build(nc, t)
    r = run_bass_kernel_spmd(nc, [{f"in_{k}": v for k, v in ins.items()}], core_ids=[0])
    return np.ascontiguousarray(r.results[0]["out"].transpose(1, 0, 2))
```

```python
import concourse.bass as bass
import concourse.bacc as bacc
from concourse import mybir
from contextlib import ExitStack


F32 = mybir.dt.float32
BF16 = mybir.dt.bfloat16
U8 = mybir.dt.uint8
I32 = mybir.dt.int32
ALU = mybir.AluOpType
ACT = mybir.ActivationFunctionType
AX = mybir.AxisListType

B, S, D = 16, 128, 128
T = 77
H0, DK0 = 16, 64
E0, F0, C0 = 8, 512, 256
FC0 = F0 // 128
NT = B * S
E2, H2 = 8, 64
H3 = 16
PARTS3 = 48
MAXES3 = PARTS3 + 6
E3, SETS3, F3 = 32, 4, 32
ES3 = E3 * SETS3
G3 = 32
NG3 = B * S // G3
I1 = 352
ROWS1 = [(0, 128), (128, 256), (256, I1)]
QMAX = 127.0
DROW_STEP, XINV_STEP, GUSCALE_STEP, HINV_STEP = 6, 9, 10, 17
MAGIC = 1.5 * 2 ** 23
AREA_A, AREA_B = 15400, 9600
MASKED = -float(2 ** 100)
LN_EPS = 1e-5


def at_least(engine, sem, value):
    if not (isinstance(value, int) and value <= 0):
        engine.wait_ge(sem, value)


def over_tiles(engine, body, tail=1):
    body(0, 0, 2 * tail)
    body(1, 1, 2 * tail)
    with engine.Fori(1, B // 2 - tail) as i:
        body(i * 2, 0, 2 * tail)
        body(i * 2 + 1, 1, 2 * tail)
    for b in range(B - 2 * tail, B):
        body(b, b % 2, B - 1 - b)


def build(nc, t):
    ctx = ExitStack()
    with ctx:
        def sb(name, shape, dt=F32):
            return ctx.enter_context(nc.sbuf_tensor(name, shape, dt))

        def sem(name):
            return ctx.enter_context(nc.semaphore(name))

        area = {"A": sb("area_a", [128, AREA_A]), "B": sb("area_b", [128, AREA_B])}

        def carve(which, sizes, p=128, dt=F32):
            at, shape = sizes
            n = 1
            for d in shape:
                n *= d
            words = n if dt == F32 else n // 2
            v = area[which][0:p, at[0]:at[0] + words]
            at[0] += words
            assert at[0] <= (AREA_A if which == "A" else AREA_B), at[0]
            if dt != F32:
                v = v.bitcast(dt)
            names = "abcd"[:len(shape)]
            return v.rearrange(f"p ({' '.join(names)}) -> p {' '.join(names)}", **dict(zip(names, shape))) if len(shape) > 1 else v

        bank = [ctx.enter_context(nc.psum_tensor(f"bank{i}", [128, 512], F32)) for i in range(8)]

        X = sb("X", [128, B, D])
        ident = sb("ident", [128, 128])
        ident_b = sb("ident_b", [128, 128], BF16)
        ones = sb("ones", [128, 128])
        ones_row = ones[0:1, :]
        gates_in = sb("gates_in", [128, 8])
        tg = sb("tg", [128, 8])
        ctxT = sb("ctxT", [128, B, T])
        mask_u8 = sb("mask_u8", [128, B, T], U8)
        mask_bias = sb("mask_bias", [128, B, T], BF16)
        ln_stats = sb("ln_stats", [128, 3, 6])
        ln_mv = sb("ln_mv", [128, 3, 2])
        ln_veps = sb("ln_veps", [128, 3])
        ln_rstd = sb("ln_rstd", [128, 3])
        eps = sb("eps", [128, 1])
        zero = sb("zero", [128, 1])
        scrap = sb("scrap", [128, 6])
        minus_half = sb("minus_half", [128, 1])
        xn = sb("xn", [128, 2, D])
        xnT = sb("xnT", [128, 2, 128])
        ctx_b = sb("ctx_b", [128, 2, T])
        at0, at1, at2, at_moe = [0], [0], [0], [0]
        wq0 = carve("A", (at0, (H0 * DK0,)), 128)
        wk0 = carve("A", (at0, (H0 * DK0,)), 128)
        wv0 = carve("A", (at0, (H0 * DK0,)), 128)
        wo0 = carve("A", (at0, (8, D,)), 128)
        bq0 = sb("bq0", [128, 8])
        bk0 = sb("bk0", [128, 8])
        bv0 = carve("A", (at0, (H0, DK0,)), T)
        bo0 = sb("bo0", [1, D])
        qT = carve("A", (at0, (8, 128,)), 128)
        kT = carve("A", (at0, (H0, T,)), 128)
        v0 = carve("A", (at0, (2, H0, DK0,)), T)
        e0 = carve("A", (at0, (H0, T,)), 128)
        mx0 = sb("mx0", [128, H0])
        eT0 = carve("A", (at0, (H0, 128,)), T)
        sum0 = sb("sum0", [128, H0])
        rs0 = sb("rs0", [128, H0])
        oT0 = carve("A", (at0, (8, 128,)), 128)

        XN = sb("XN", [128, B, D])
        wg0 = sb("wg0", [128, E0])
        r0 = {k: sb(f"r0_{k}", [128, B, E0]) for k in ("exp", "gate", "rank", "keep", "at", "gkeep")}
        r0s = {k: sb(f"r0_{k}", [128, B]) for k in ("max", "sum", "rsum", "gmax", "rmax", "slot", "kept", "gsel", "weight", "alt", "alt2")}
        first0 = sb("first0", [128, B, E0], BF16)
        scatter_at = sb("scatter_at", [128, B], I32)
        gather_at = sb("gather_at", [128, B], I32)
        rank_w = sb("rank_w", [128, E0])
        slot_base = sb("slot_base", [128, E0])
        spare_slot = sb("spare_slot", [128, B])
        tri_b = sb("tri_b", [128, 128], BF16)
        ones_b = sb("ones_b", [128, 128], BF16)
        lg0 = sb("lg0", [128, B, E0])
        xnK = sb("xnK", [128, D])
        xnM = sb("xnM", [128, 128])
        w1e = carve("B", (at_moe, (4, F0,)), 128)
        w2e = carve("B", (at_moe, (4, FC0, D,)), 128)
        b1e = sb("b1e", [128, E0, FC0])
        b2e = carve("B", (at_moe, (E0, D)), 1)
        xe = carve("B", (at_moe, (4, 2, D,)), 128)
        xeT = carve("B", (at_moe, (2, 2 * 128,)), 128)
        hT0 = carve("B", (at_moe, (2, FC0, 2 * 128,)), 128)
        ye = carve("B", (at_moe, (2, 2, D,)), 128)

        w1x = sb("w1x", [128, D])
        w2x = sb("w2x", [128, D])
        bx = sb("bx", [1, D])
        ctx_mean = sb("ctx_mean", [128, B])
        ctx_sum = sb("ctx_sum", [128, B])
        mix_row = sb("mix_row", [1, B * D])
        absmax1 = sb("absmax1", [128, B])
        clips = sb("clips", [128, 2])
        clip_tanh = sb("clip_tanh", [128, 2])
        clip_sig = sb("clip_sig", [128, 2])
        minus_magic = sb("minus_magic", [128, 1])
        wgu1 = sb("wgu1", [128, 2, 3, D])
        wd1 = sb("wd1", [128, I1])
        wmax1 = sb("wmax1", [128, 7])
        wscale1 = sb("wscale1", [128, 7])
        winv1 = sb("winv1", [128, 7])
        wguT1 = sb("wguT1", [128, 2, I1], BF16)
        wdT1 = sb("wdT1", [128, 3, D], BF16)
        dscale1 = sb("dscale1", [128, D])
        drow1 = sb("drow1", [128, D])
        col1 = {k: sb(f"col1_{k}", [128, 1]) for k in ("xmax", "xscale", "xinv", "hmax", "hscale", "hinv", "out")}
        cell1 = sb("cell1", [1, 2])
        guscale1 = sb("guscale1", [128, 2, 3])
        xq1 = sb("xq1", [128, 4, D])
        xqT1 = sb("xqT1", [128, 2, 512], BF16)
        silu1 = carve("A", (at1, (3, 512,)), 128)
        h1 = carve("A", (at1, (3, NT)), 128)
        hq1 = carve("A", (at1, (3, NT,)), 128, BF16)
        hmax1 = sb("hmax1", [128, 12])
        tmp512 = sb("tmp512", [128, 2, 512])

        g_stats = sb("g_stats", [128, 2, 4, 6])
        g_mv = sb("g_mv", [128, 2, 4, 2])
        g_veps = sb("g_veps", [128, 2, 4])
        g_rstd = sb("g_rstd", [128, 2, 4])
        xn4 = sb("xn4", [128, 2, 4, D])
        xnT4 = sb("xnT4", [128, 2, 512])
        wqkv2 = sb("wqkv2", [128, 3, D])
        bqk2 = sb("bqk2", [128, 2])
        bv2 = sb("bv2", [T, D])
        kT2 = carve("A", (at2, (B, T,)), 128)
        v2 = carve("A", (at2, (B, D,)), T)
        qT2 = carve("A", (at2, (512,)), 128)
        e2 = carve("A", (at2, (2, 4, T)), 128)
        eT2 = carve("A", (at2, (512,)), T)
        s2 = {k: sb(f"s2_{k}", [128, 4]) for k in ("max", "sum", "rsum", "out")}
        rw2 = sb("rw2", [128, E2])
        rb2 = sb("rb2", [128, E2])
        at_w2 = [13000]
        w13_2 = carve("A", (at_w2, (2, 5, 128)), 128)
        w2_2 = carve("A", (at_w2, (5, D)), 128)
        pair_sel = sb("pair_sel", [3 * E2, 4, 128], BF16)
        r2s = {k: sb(f"r2s_{k}", [128, B]) for k in ("m1", "r1", "m2", "r2", "d", "e", "den", "g1", "g2")}
        gT2 = sb("gT2", [3 * E2, 512], BF16)
        th2 = carve("A", (at2, (2, 512,)), 128)
        u2 = carve("A", (at2, (2, 512,)), 128)
        h2 = carve("A", (at2, (5, 512,)), 128)
        gate_parts = carve("A", (at2, (B, 3, E2)), 128, BF16)
        r2 = {k: carve("A", (at2, (B, E2)), 128) for k in ("rank", "rank2", "first", "second", "rest", "a", "b", "gate", "logit")}

        at3 = [0]
        em3 = carve("B", (at3, (H3, 128)), 128)
        ea3 = carve("B", (at3, (H3, 128)), T)
        sq3 = carve("B", (at3, (2, H3, 64)), 128, BF16)
        sk3 = carve("B", (at3, (H3, 64)), 128, BF16)
        sa3 = carve("B", (at3, (H3, 64)), T, BF16)
        qT3 = carve("B", (at3, (8, 128)), 128, BF16)
        qmT3 = carve("B", (at3, (8, 128)), 128, BF16)
        xnT2 = carve("B", (at3, (4, 512)), 128)
        at3a = [0]
        kT3 = carve("A", (at3a, (2, 8, 128)), 128, BF16)
        kaT3 = carve("A", (at3a, (2, 8, T + 1)), 128, BF16)
        wqkv3 = sb("wqkv3", [128, 3 * D])
        wkva3 = sb("wkva3", [128, 2 * D])
        bqkv3 = sb("bqkv3", [128, 3 * D])
        bkva3 = sb("bkva3", [T, 2 * D])
        wo3 = sb("wo3", [128, D])
        bo3 = sb("bo3", [1, D])
        g3 = sb("g3", [128, H3])
        g3_tanh = sb("g3_tanh", [128, H3])
        gate3 = sb("gate3", [128, 2, H3])
        qk3 = sb("qk3", [128, 2, H3, 8])
        ka3 = sb("ka3", [T, H3, 8])
        v3 = carve("A", (at3a, (2, H3, 32)), 128)
        va3 = carve("A", (at3a, (2, H3, 32)), T)
        ovT3 = carve("A", (at3a, (2, 4, 128)), 128)
        left3 = [sb(f"left3_{i}", [128, H3, 8]) for i in range(3)]
        mx3 = sb("mx3", [128, 2, H3])
        mleft3 = sb("mleft3", [128, 2, H3])
        rs3 = sb("rs3", [128, 2, H3])
        rg3 = sb("rg3", [128, 2, H3])
        ov3 = sb("ov3", [128, 2, H3, 8])
        o3 = sb("o3", [128, D])
        oT3 = sb("oT3", [128, 128])

        at4, at5 = [0], [0]
        d3 = carve("A", (at4, (NG3, ES3)), 128)
        bd3 = carve("A", ([0], (E3, SETS3, NG3)), 128)
        f1_3 = carve("A", (at4, (ES3, F3)), 128)
        in3 = carve("A", (at4, (E3, NG3)), 128)
        out3 = carve("B", (at5, (NG3, ES3)), 128)
        perm3 = XN[:, :, :].rearrange("p b d -> p (b d)")
        f2_3 = sb("f2_3", [128, E3, D])
        ctrl3 = sb("ctrl3", [128, ES3])
        tie3 = sb("tie3", [128, G3])
        bias3 = sb("bias3", [128, E3])
        gmax3 = sb("gmax3", [128, 16])
        pt3 = carve("B", (at5, (2, 4, ES3)), 128)
        rows3 = carve("A", (at4, (2, 4, D)), 128)

        x_loaded = sem("x_loaded")
        const_loaded = sem("const_loaded")
        ctx_loaded = sem("ctx_loaded")
        mask_loaded = sem("mask_loaded")
        wqkv0_loaded = sem("wqkv0_loaded")
        wo0_loaded = sem("wo0_loaded")
        out_stored = sem("out_stored")
        pool_ready = sem("pool_ready")
        tg_ready = sem("tg_ready")
        stats_done = sem("stats_done")
        var_done = sem("var_done")
        veps_done = sem("veps_done")
        rstd_done = sem("rstd_done")
        xn_done = sem("xn_done")
        xnT_in_psum = sem("xnT_in_psum")
        xnT_done = sem("xnT_done")
        ctx_b_done = sem("ctx_b_done")
        x_updated = sem("x_updated")
        proj_in_psum = sem("proj_in_psum")
        proj_done = sem("proj_done")
        scores_in_psum = sem("scores_in_psum")
        max_done = sem("max_done")
        shifted_done = sem("shifted_done")
        exp_done = sem("exp_done")
        turn_in_psum = sem("turn_in_psum")
        turn_done = sem("turn_done")
        av_in_psum = sem("av_in_psum")
        sums_done = sem("sums_done")
        probs_done = sem("probs_done")
        av_done = sem("av_done")
        wo_in_psum = sem("wo_in_psum")
        route0_loaded = sem("route0_loaded")
        route_exp = sem("route_exp")
        vector_step = sem("vector_step")
        tanh_done = sem("tanh_done")
        norm0_done = sem("norm0_done")
        xn_kept = sem("xn_kept")
        norm0T_in_psum = sem("norm0T_in_psum")
        norm0T_done = sem("norm0T_done")
        logits0_kept = sem("logits0_kept")
        combined0 = sem("combined0")
        first_done = sem("first_done")
        rank_in_psum = sem("rank_in_psum")
        places_done = sem("places_done")
        slots_zeroed = sem("slots_zeroed")
        scattered = sem("scattered")
        expert_loaded = [sem(f"expert_loaded{i}") for i in range(4)]
        xeT_in_psum = sem("xeT_in_psum")
        xeT_done = sem("xeT_done")
        h_in_psum = sem("h_in_psum")
        h_done = sem("h_done")
        y_in_psum = sem("y_in_psum")
        y_done = sem("y_done")
        y_stored = [sem(f"y_stored{i}") for i in range(2)]
        gathered = [sem(f"gathered{i}") for i in range(4)]
        mix_loaded = sem("mix_loaded")
        ctx_mean_done = sem("ctx_mean_done")
        mix_row_in_psum = sem("mix_row_in_psum")
        mix_row_done = sem("mix_row_done")
        mix_in_psum = sem("mix_in_psum")
        absmax_done = sem("absmax_done")
        ffn1_loaded = sem("ffn1_loaded")
        quant_step = sem("quant_step")
        w_rounded = sem("w_rounded")
        wT_in_psum = sem("wT_in_psum")
        wT_done = sem("wT_done")
        drow_in_psum = sem("drow_in_psum")
        colmax_done = sem("colmax_done")
        maxrow_in_psum = sem("maxrow_in_psum")
        cell_done = sem("cell_done")
        max_in_psum = sem("max_in_psum")
        xq_done = sem("xq_done")
        xqT_in_psum = sem("xqT_in_psum")
        xqT_done = sem("xqT_done")
        gu_in_psum = sem("gu_in_psum")
        silu_done = sem("silu_done")
        h1_done = sem("h1_done")
        hq_rounded = sem("hq_rounded")
        hq_done = sem("hq_done")
        down_in_psum = sem("down_in_psum")
        g_stats_done = sem("g_stats_done")
        moe3_loaded = sem("moe3_loaded")
        f1_loaded = sem("f1_loaded")
        l3_in_psum = sem("l3_in_psum")
        perm3_done = sem("perm3_done")
        pt3_in_psum = sem("pt3_in_psum")
        pt3_done = sem("pt3_done")
        d3_in_psum = sem("d3_in_psum")
        d3_act_done = sem("d3_act_done")
        d3_dve_done = sem("d3_dve_done")
        in3_in_psum = sem("in3_in_psum")
        in3_biased = sem("in3_biased")
        in3_done = sem("in3_done")
        bd3_zeroed = sem("bd3_zeroed")
        f3_in_psum = sem("f3_in_psum")
        out3_act_done = sem("out3_act_done")
        out3_dve_done = sem("out3_dve_done")
        rows3_in_psum = sem("rows3_in_psum")
        rows3_done = sem("rows3_done")
        comb3_in_psum = sem("comb3_in_psum")
        attn3_loaded = sem("attn3_loaded")
        qkv3_in_psum = sem("qkv3_in_psum")
        proj3_done = sem("proj3_done")
        v3_done = sem("v3_done")
        split3_step = sem("split3_step")
        split3_done = sem("split3_done")
        stack3_ready = sem("stack3_ready")
        t3_in_psum = sem("t3_in_psum")
        t3_done = sem("t3_done")
        s3_in_psum = sem("s3_in_psum")
        max3_done = sem("max3_done")
        maxsplit3_step = sem("maxsplit3_step")
        maxcols3_done = sem("maxcols3_done")
        sT3_in_psum = sem("sT3_in_psum")
        exp3_done = sem("exp3_done")
        av3_in_psum = sem("av3_in_psum")
        ovT3_done = sem("ovT3_done")
        o3_step = sem("o3_step")
        o3_done = sem("o3_done")
        wo3_in_psum = sem("wo3_in_psum")
        g_var_done = sem("g_var_done")
        g_veps_done = sem("g_veps_done")
        g_rstd_done = sem("g_rstd_done")
        g_xn_done = sem("g_xn_done")
        g_xnT_in_psum = sem("g_xnT_in_psum")
        g_xnT_done = sem("g_xnT_done")
        attn2_loaded = sem("attn2_loaded")
        kv2_in_psum = sem("kv2_in_psum")
        k2_done = sem("k2_done")
        v2_done = sem("v2_done")
        q2_in_psum = sem("q2_in_psum")
        q2_done = sem("q2_done")
        s2_in_psum = sem("s2_in_psum")
        shift2_done = sem("shift2_done")
        exp2_done = sem("exp2_done")
        eT2_in_psum = sem("eT2_in_psum")
        eT2_done = sem("eT2_done")
        av2_in_psum = sem("av2_in_psum")
        moe2_loaded = sem("moe2_loaded")
        logits2_in_psum = sem("logits2_in_psum")
        gap2_done = sem("gap2_done")
        gap2_exp = sem("gap2_exp")
        gates2_done = sem("gates2_done")
        gT2_in_psum = sem("gT2_in_psum")
        gT2_done = sem("gT2_done")
        ab2_in_psum = sem("ab2_in_psum")
        g2_in_psum = sem("g2_in_psum")
        tanh2_done = sem("tanh2_done")
        h2_done = sem("h2_done")
        out2_in_psum = sem("out2_in_psum")

        block = ctx.enter_context(nc.Block())

        vector_steps = [0]

        def linked(dve, ins):
            vector_steps[0] += 1
            ins.then_inc(vector_step, 1)
            dve.wait_ge(vector_step, vector_steps[0])

        def slot(b):
            return X[:, bass.ds(b, 1), :].rearrange("p a d -> p (a d)")

        def vector_ln_stats(dve, b, n, u, updates=0):
            if not (isinstance(updates, int) and updates == 0):
                dve.wait_ge(x_updated, updates)
            if not isinstance(updates, int):
                dve.memset(scrap[:, 3 + u:4 + u], 0.0)
            dve.bn_stats(ln_stats[:, u, :], slot(b)).then_inc(stats_done, 1)
            dve.wait_ge(stats_done, n + 1)
            dve.memset(scrap[:, u:u + 1], 0.0)
            dve.bn_aggr(ln_mv[:, u, :], ln_stats[:, u, :]).then_inc(var_done, 1)

        def gpsimd_ln_rstd(pool, n, u):
            pool.wait_ge(var_done, n + 1)
            pool.tensor_tensor(ln_veps[:, u:u + 1], ln_mv[:, u, 1:2], eps[:, :], ALU.add).then_inc(veps_done, 1)
            pool.wait_ge(veps_done, n + 1)
            pool.tensor_tensor(ln_rstd[:, u:u + 1], ln_veps[:, u:u + 1], minus_half[:, :], ALU.pow).then_inc(rstd_done, 1)

        def vector_ln_apply(dve, b, n, u, norms):
            dve.wait_ge(rstd_done, norms + 1)
            at_least(dve, xnT_in_psum, n - 1)
            dve.tensor_scalar(xn[:, u, :], slot(b), ln_mv[:, u, 0:1], ln_rstd[:, u:u + 1],
                              ALU.subtract, ALU.mult).then_inc(xn_done, 1)

        def tensor_xnT(pe, n, u, psum):
            pe.wait_ge(xn_done, n + 1)
            at_least(pe, xnT_done, n - 1)
            pe.transpose(psum[:, 0:128], xn[:, u, :], ident[:, :]).then_inc(xnT_in_psum, 1)

        def scalar_xnT(act, n, u, psum):
            act.wait_ge(xnT_in_psum, n + 1)
            act.activation(xnT[:, u, :], psum[:, 0:128], ACT.Copy).then_inc(xnT_done, 1)

        P0 = [bank[0], bank[1]]
        S0 = [bank[2], bank[3], bank[4]]
        T0 = [bank[5], bank[6]]
        HEADS0 = [(0, 6), (6, 12), (12, 16)]
        WO, LOGITS0 = bank[7][:, 0:128], bank[7][:, 128:128 + E0]

        def tensor_attn0(pe):
            def project(b, u):
                for j in range(6):
                    if j == 0:
                        pe.wait_ge(xnT_done, b + 1)
                    if j == 4:
                        pe.wait_ge(ctx_b_done, b + 1)
                    if j < 2:
                        at_least(pe, av_done, 2 * b - 3 + j)
                    else:
                        pe.wait_ge(proj_done, 8 * b + [1, 2, 4, 6][j - 2])
                    dst = P0[j % 2]
                    half = j % 2
                    if j < 4:
                        w, rhs, n = (wq0, xnT[:, u, :], 128) if j < 2 else (wk0, ctxT[:, bass.ds(b, 1), :].rearrange("p a t -> p (a t)"), T)
                        for c in range(4):
                            m = pe.matmul(dst[:, c * n:(c + 1) * n], w[:, (4 * half + c) * 128:(4 * half + c + 1) * 128],
                                          rhs, start=True, stop=True)
                    else:
                        m = pe.matmul(dst[0:T, :], ctx_b[:, u, :], wv0[:, half * 512:(half + 1) * 512], start=True, stop=True)
                    m.then_inc(proj_in_psum, 1)

            def scores(b):
                pe.wait_ge(proj_done, 8 * b + 6)
                for c, (lo, hi) in enumerate(HEADS0):
                    at_least(pe, shifted_done, 3 * b - 2 + c)
                    n = hi - lo
                    pe.matmul(S0[c][:, 0:n * T], ident_b[:, :],
                              mask_bias[:, bass.ds(b, 1), :].to_broadcast([128, n, T]), start=True, stop=False)
                    for h in range(lo, hi, 2):
                        m = pe.matmul(S0[c][:, (h - lo) * T:(h - lo + 2) * T], qT[:, h // 2, :],
                                      kT[:, h:h + 2, :].rearrange("p a t -> p (a t)"), start=False, stop=(h == hi - 2))
                    m.then_inc(scores_in_psum, 1)

            def turn(b, u, j, more):
                pe.wait_ge(probs_done, 3 * b + (4 * j + 3) // 6 + 1)
                at_least(pe, turn_done, 4 * b + max(j - 1, 0))
                if j == 0:
                    at_least(pe, norm0T_done, b - 1)
                if j == 1 and more >= 1:
                    pe.wait_ge(xnT_done, b + 2)
                for h in range(4 * j, 4 * j + 4):
                    m = pe.transpose(T0[j % 2][0:T, (h % 4) * 128:(h % 4 + 1) * 128], e0[:, h, :], ident[:, :])
                m.then_inc(turn_in_psum, 1)

            def attend(b, u, j, more):
                pe.wait_ge(turn_done, 4 * b + j + 1)
                if more >= 1 and j % 2 == 0:
                    pe.wait_ge(proj_done, 8 * b + 15 + j // 2)
                for h in range(4 * j, 4 * j + 4):
                    c, p = h // 2, 64 * (h % 2)
                    m = pe.matmul(P0[c // 4][p:p + 64, (c % 4) * 128:(c % 4 + 1) * 128], v0[:, u, h, :], eT0[:, h, :], start=True, stop=True)
                if j % 2 == 1:
                    m.then_inc(av_in_psum, 1)

            def output(b):
                at_least(pe, x_updated, b)
                pe.wait_ge(av_done, 2 * b + 2)
                for c in range(8):
                    pe.matmul(WO, oT0[:, c, :], wo0[:, c, :], start=(c == 0), stop=False)
                m = pe.matmul(WO, ones_row[:, :], bo0[:, :], start=False, stop=True)
                if not (isinstance(b, int) and b == 0):
                    m = logits(b - 1)
                m.then_inc(wo_in_psum, 1)

            def turn_norm(b):
                pe.wait_ge(norm0_done, b + 1)
                pe.transpose(T0[0][:, 0:128], xnK[:, :], ident[:, :]).then_inc(norm0T_in_psum, 1)

            def logits(b):
                pe.wait_ge(norm0T_done, b + 1)
                return pe.matmul(LOGITS0, xnM[:, :], wg0[:, :], start=True, stop=True)

            pe.wait_ge(const_loaded, 4 * 16)
            pe.wait_ge(pool_ready, 3)
            pe.wait_ge(ctx_loaded, 16)
            tensor_xnT(pe, 0, 0, T0[0])
            pe.wait_ge(wqkv0_loaded, 6 * 16)
            project(0, 0)
            scores(0)
            tensor_xnT(pe, 1, 1, T0[1])
            pe.wait_ge(wo0_loaded, 2 * 16)
            pe.wait_ge(route0_loaded, 8 * 16)

            def body(b, u, more):
                if more >= 1:
                    project(b + 1, 1 - u)
                turn(b, u, 0, more)
                turn(b, u, 1, more)
                turn(b, u, 2, more)
                attend(b, u, 0, more)
                turn(b, u, 3, more)
                for j in range(1, 4):
                    attend(b, u, j, more)
                if not (isinstance(b, int) and b == 0):
                    pe.wait_ge(turn_done, 4 * b + 3)
                    turn_norm(b - 1)
                if more >= 2:
                    pe.wait_ge(turn_done, 4 * b + 4)
                    tensor_xnT(pe, b + 2, u, T0[1])
                if more >= 1:
                    scores(b + 1)
                output(b)
            over_tiles(pe, body)
            turn_norm(B - 1)
            pe.wait_ge(x_updated, B)
            logits(B - 1).then_inc(wo_in_psum, 1)

        def vector_attn0(dve):
            def projected(b, u, parts):
                for j in parts:
                    dve.wait_ge(proj_in_psum, 6 * b + j + 1)
                    half = j % 2
                    c = slice(4 * half, 4 * half + 4)
                    if j < 2:
                        dve.tensor_tensor(qT[:, c, :], P0[half][:, 0:512].rearrange("p (c n) -> p c n", n=128),
                                          bq0[:, c].unsqueeze(2).to_broadcast([128, 4, 128]), ALU.add).then_inc(proj_done, 1)
                    elif j < 4:
                        for r in range(2):
                            p = slice(64 * r, 64 * r + 64)
                            dve.tensor_tensor(kT[p, 8 * half + r:8 * half + 8:2, :],
                                              P0[half][p, 0:4 * T].rearrange("p (c n) -> p c n", n=T),
                                              bk0[p, c].unsqueeze(2).to_broadcast([64, 4, T]), ALU.add).then_inc(proj_done, 1)
                    else:
                        h = slice(8 * half, 8 * half + 8)
                        dve.tensor_tensor(v0[:, u, h, 0:DK0], P0[half][0:T, :].rearrange("p (h d) -> p h d", d=DK0),
                                          bv0[:, h, :], ALU.add).then_inc(proj_done, 1)

            def softmax(b):
                for c, (lo, hi) in enumerate(HEADS0):
                    n = hi - lo
                    sc = S0[c][:, 0:n * T].rearrange("p (h t) -> p h t", t=T)
                    dve.wait_ge(scores_in_psum, 3 * b + c + 1)
                    dve.tensor_reduce(mx0[:, lo:hi], sc, AX.X, ALU.max).then_inc(max_done, 1)
                    dve.wait_ge(max_done, 3 * b + c + 1)
                    dve.tensor_tensor(e0[:, lo:hi, :], sc, mx0[:, lo:hi].unsqueeze(2).to_broadcast([128, n, T]),
                                      ALU.subtract).then_inc(shifted_done, 1)

            def sums(b):
                for c, (lo, hi) in enumerate(HEADS0):
                    dve.wait_ge(exp_done, 3 * b + c + 1)
                    dve.tensor_reduce(sum0[:, lo:hi], e0[:, lo:hi, :], AX.X, ALU.add).then_inc(sums_done, 1)
                dve.wait_ge(sums_done, 4 * b + 3)
                dve.reciprocal(rs0[:, :], sum0[:, :]).then_inc(sums_done, 1)

            def keep_logits(b):
                dve.wait_ge(wo_in_psum, b + 2)
                dve.tensor_tensor(lg0[:, bass.ds(b, 1), :].rearrange("p a e -> p (a e)"), LOGITS0, zero[:, :].to_broadcast([128, E0]),
                                  ALU.add).then_inc(logits0_kept, 1)

            def norm_for_experts(b, norms):
                dve.wait_ge(rstd_done, norms + 1)
                at_least(dve, xn_kept, b)
                at_least(dve, norm0T_in_psum, b)
                dve.tensor_scalar(xnK[:, :], slot(b), ln_mv[:, 2, 0:1], ln_rstd[:, 2:3],
                                  ALU.subtract, ALU.mult).then_inc(norm0_done, 1)

            def update(b):
                dve.wait_ge(wo_in_psum, b + 1)
                if not (isinstance(b, int) and b == 0):
                    keep_logits(b - 1)
                dve.scalar_tensor_tensor(slot(b), WO, tg[:, 0:1], slot(b), ALU.mult, ALU.add).then_inc(x_updated, 1)

            dve.wait_ge(x_loaded, 16)
            dve.wait_ge(pool_ready, 3)
            vector_ln_stats(dve, 0, 0, 0)
            vector_ln_apply(dve, 0, 0, 0, 0)
            vector_ln_stats(dve, 1, 1, 1)
            vector_ln_apply(dve, 1, 1, 1, 1)
            dve.wait_ge(wqkv0_loaded, 6 * 16)
            dve.wait_ge(tg_ready, 1)
            projected(0, 0, range(6))
            softmax(0)

            def body(b, u, more):
                if more >= 1:
                    projected(b + 1, 1 - u, range(2))
                sums(b)
                if more >= 2:
                    vector_ln_stats(dve, b + 2, 2 * b + 2, u)
                if not (isinstance(b, int) and b == 0):
                    norm_for_experts(b - 1, 2 * b + (1 if more >= 1 else 0))
                if more >= 1:
                    projected(b + 1, 1 - u, range(2, 6))
                if more >= 2:
                    vector_ln_apply(dve, b + 2, b + 2, u, 2 * b + 2)
                if more >= 1:
                    softmax(b + 1)
                update(b)
                vector_ln_stats(dve, b, 2 * b + 1 + more, 2, b + 1)
            over_tiles(dve, body)
            norm_for_experts(B - 1, 2 * B - 1)
            keep_logits(B - 1)

        def scalar_attn0(act):
            def exps(b):
                for c, (lo, hi) in enumerate(HEADS0):
                    act.wait_ge(shifted_done, 3 * b + c + 1)
                    act.activation(e0[:, lo:hi, :], e0[:, lo:hi, :], ACT.Exp, scale=DK0 ** -0.5).then_inc(exp_done, 1)

            def turned_norm(b):
                act.wait_ge(norm0T_in_psum, b + 1)
                act.activation(xnM[:, :], T0[0][:, 0:128], ACT.Copy).then_inc(norm0T_done, 1)

            scalar_xnT(act, 0, 0, T0[0])
            exps(0)
            scalar_xnT(act, 1, 1, T0[1])

            def body(b, u, more):
                for j in range(4):
                    act.wait_ge(turn_in_psum, 4 * b + j + 1)
                    act.activation(eT0[:, 4 * j:4 * j + 4, :], T0[j % 2][0:T, :].rearrange("p (h q) -> p h q", q=128),
                                   ACT.Copy).then_inc(turn_done, 1)
                for j in range(2):
                    act.wait_ge(av_in_psum, 2 * b + j + 1)
                    act.activation(oT0[:, 4 * j:4 * j + 4, :], P0[j][:, :].rearrange("p (h q) -> p h q", q=128),
                                   ACT.Copy).then_inc(av_done, 1)
                if not (isinstance(b, int) and b == 0):
                    turned_norm(b - 1)
                if more >= 2:
                    scalar_xnT(act, b + 2, u, T0[1])
                if more >= 1:
                    exps(b + 1)
            over_tiles(act, body)
            turned_norm(B - 1)

        def gpsimd_attn0(pool):
            def context(b, u):
                at_least(pool, proj_in_psum, 6 * b - 6)
                pool.tensor_copy(ctx_b[:, u, :], ctxT[:, bass.ds(b, 1), :].rearrange("p a t -> p (a t)")).then_inc(ctx_b_done, 1)

            def keep(b):
                if isinstance(b, int) and b == 0:
                    pool.wait_ge(slots_zeroed, 16)
                pool.wait_ge(norm0_done, b + 1)
                pool.tensor_tensor(XN[:, bass.ds(b, 1), :].rearrange("p a d -> p (a d)"), xnK[:, :], zero[:, :].to_broadcast([128, D]),
                                   ALU.add).then_inc(xn_kept, 1)

            def normalise(b):
                pool.wait_ge(sums_done, 4 * b + 4)
                for lo, hi in HEADS0:
                    pool.tensor_tensor(e0[:, lo:hi, :], e0[:, lo:hi, :], rs0[:, lo:hi].unsqueeze(2).to_broadcast([128, hi - lo, T]),
                                       ALU.mult).then_inc(probs_done, 1)

            gpsimd_ln_rstd(pool, 0, 0)
            gpsimd_ln_rstd(pool, 1, 1)
            pool.wait_ge(ctx_loaded, 16)
            context(0, 0)
            context(1, 1)

            def body(b, u, more):
                normalise(b)
                if more >= 2:
                    gpsimd_ln_rstd(pool, 2 * b + 2, u)
                    context(b + 2, u)
                if not (isinstance(b, int) and b == 0):
                    keep(b - 1)
                gpsimd_ln_rstd(pool, 2 * b + 1 + more, 2)
            over_tiles(pool, body)
            keep(B - 1)

        RANK0 = bank[7]
        H_BANKS = [bank[0:2], bank[2:4]]
        XE_BANK = [bank[4], bank[5]]
        Y_BANK = [bank[6], bank[7]]

        XQ_BANK = [bank[5], bank[6]]

        def tensor_ahead(pe):
            pe.wait_ge(mix_loaded, 3 * 16)
            pe.wait_ge(ctx_mean_done, 1)
            for b in range(B):
                dst = bank[b // 4][0:1, (b % 4) * D:(b % 4 + 1) * D]
                pe.matmul(dst, ctx_mean[:, b:b + 1], w2x[:, :], start=True, stop=False)
                m = pe.matmul(dst, ones_row[:, 0:1], bx[:, :], start=False, stop=True)
                if b % 4 == 3:
                    m.then_inc(mix_row_in_psum, 1)
            for k in range(7):
                pe.wait_ge(w_rounded, k + 1)
                at_least(pe, wT_done, k - 1)
                if k < 6:
                    lo, hi = ROWS1[k % 3]
                    pe.transpose(XQ_BANK[k % 2][:, 0:hi - lo], wgu1[0:hi - lo, k // 3, k % 3, :], ident[0:hi - lo, 0:hi - lo]).then_inc(wT_in_psum, 1)
                else:
                    for c, (lo, hi) in enumerate(ROWS1):
                        m = pe.transpose(XQ_BANK[0][0:hi - lo, c * D:(c + 1) * D], wd1[:, lo:hi], ident[:, :])
                    m.then_inc(wT_in_psum, 1)
            pe.wait_ge(drow_in_psum, 1)
            pe.matmul(bank[0][:, 0:D], ones[:, :], dscale1[:, :], start=True, stop=True).then_inc(drow_in_psum, 1)

            pe.wait_ge(mix_row_done, 4)
            pe.wait_ge(wT_done, 7)
            pe.wait_ge(quant_step, DROW_STEP)

        steps = [1]

        def link(dve, ins):
            steps[0] += 1
            ins.then_inc(quant_step, 1)
            dve.wait_ge(quant_step, steps[0])

        def vector_ahead(dve):
            dve.tensor_reduce(ctx_sum[:, :], ctxT[:, :, :], AX.X, ALU.add).then_inc(quant_step, 1)
            dve.wait_ge(quant_step, 1)
            dve.tensor_scalar(ctx_mean[:, :], ctx_sum[:, :], 1.0 / T, None, ALU.mult).then_inc(ctx_mean_done, 1)
            for g in range(4):
                dve.wait_ge(mix_row_in_psum, g + 1)
                dve.tensor_copy(mix_row[:, g * 512:(g + 1) * 512], bank[g][0:1, :]).then_inc(mix_row_done, 1)
            dve.wait_ge(ffn1_loaded, 5 * 16)
            dve.memset(wmax1[:, :], 1.0)
            link(dve, dve.memset(hmax1[:, :], 0.0))
            for k in range(6):
                lo, hi = ROWS1[k % 3]
                dve.tensor_reduce(wmax1[0:hi - lo, k:k + 1], wgu1[0:hi - lo, k // 3, k % 3, :], AX.X, ALU.max, apply_absolute_value=True)
            link(dve, dve.tensor_reduce(wmax1[:, 6:7], wd1[:, :], AX.X, ALU.max, apply_absolute_value=True))
            link(dve, dve.tensor_scalar(wscale1[:, :], wmax1[:, :], 1.0 / QMAX, None, ALU.mult))
            link(dve, dve.reciprocal(winv1[:, :], wscale1[:, :]))
            for k in range(6):
                lo, hi = ROWS1[k % 3]
                w = wgu1[0:hi - lo, k // 3, k % 3, :]
                dve.tensor_scalar(w, w, winv1[0:hi - lo, k:k + 1], MAGIC, ALU.mult, ALU.add).then_inc(w_rounded, 1)
            dve.tensor_scalar(wd1[:, :], wd1[:, :], winv1[:, 6:7], MAGIC, ALU.mult, ALU.add).then_inc(w_rounded, 1)
            dve.tensor_scalar(dscale1[:, :], ident[:, :], wscale1[:, 6:7], None, ALU.mult).then_inc(drow_in_psum, 1)
            dve.wait_ge(drow_in_psum, 2)
            link(dve, dve.tensor_copy(drow1[:, :], bank[0][:, 0:D]))
            assert steps[0] == DROW_STEP
            dve.wait_ge(tanh_done, 1)
            link(dve, dve.tensor_scalar(clip_sig[:, :], clip_tanh[:, :], 0.5, 0.5, ALU.mult, ALU.add))

        def scalar_ahead(act):
            for k in range(7):
                act.wait_ge(wT_in_psum, k + 1)
                if k < 6:
                    lo, hi = ROWS1[k % 3]
                    m = act.activation(wguT1[:, k // 3, lo:hi], XQ_BANK[k % 2][:, 0:hi - lo], ACT.Identity, bias=minus_magic[:, :])
                else:
                    for c, (lo, hi) in enumerate(ROWS1):
                        m = act.activation(wdT1[0:hi - lo, c, :], XQ_BANK[0][0:hi - lo, c * D:(c + 1) * D], ACT.Identity,
                                           bias=minus_magic[0:hi - lo, :])
                m.then_inc(wT_done, 1)


        def tensor_moe0(pe):
            pe.wait_ge(first_done, 1)
            pe.matmul(RANK0[:, 0:B * E0], tri_b[:, :], first0[:, :, :].rearrange("p b e -> p (b e)"), start=True, stop=False)
            for k in range(1, B):
                m = pe.matmul(RANK0[:, k * E0:B * E0], ones_b[:, :], first0[:, 0:B - k, :].rearrange("p b e -> p (b e)"),
                              start=False, stop=(k == B - 1))
            m.then_inc(rank_in_psum, 1)
            tensor_ahead(pe)

            def turn(e, v):
                pe.wait_ge(expert_loaded[e % 4], 3 * 16 * (e // 4 + 1))
                at_least(pe, xeT_done, e - 1)
                for j in range(2):
                    m = pe.transpose(XE_BANK[v][:, j * 128:(j + 1) * 128], xe[:, e % 4, j, :], ident[:, :])
                m.then_inc(xeT_in_psum, 1)

            def hidden(e, v):
                pe.wait_ge(xeT_done, e + 1)
                at_least(pe, h_done, 4 * e - 4)
                for c in range(FC0):
                    m = pe.matmul(H_BANKS[v][c // 2][:, (c % 2) * 256:(c % 2 + 1) * 256], w1e[:, e % 4, c * 128:(c + 1) * 128],
                                  xeT[:, v, :], start=True, stop=True)
                    if c % 2:
                        m.then_inc(h_in_psum, 1)

            def rows_out(e, v):
                at_least(pe, y_done, e - 1)
                pe.wait_ge(h_done, 4 * e + 4)
                for j in range(2):
                    for c in range(FC0):
                        pe.matmul(Y_BANK[v][:, j * 128:(j + 1) * 128], hT0[:, v, c, j * 128:(j + 1) * 128], w2e[:, e % 4, c, :],
                                  start=(c == 0), stop=False)
                    m = pe.matmul(Y_BANK[v][:, j * 128:(j + 1) * 128], ones_row[:, :], b2e[:, e, :], start=False, stop=True)
                m.then_inc(y_in_psum, 1)

            turn(0, 0)
            hidden(0, 0)

            for e in range(E0):
                if e + 1 < E0:
                    turn(e + 1, (e + 1) % 2)
                    hidden(e + 1, (e + 1) % 2)
                rows_out(e, e % 2)

        def vector_moe0(dve):
            def wide(a):
                return a[:, :].unsqueeze(2).to_broadcast([128, B, E0])

            def per_expert(a):
                return a[:, :].unsqueeze(1).to_broadcast([128, B, E0])

            lg = lg0[:, :, :]
            rank = RANK0[:, 0:B * E0].rearrange("p (b e) -> p b e", e=E0)
            dve.wait_ge(logits0_kept, B)
            dve.wait_ge(route0_loaded, 8 * 16)
            linked(dve, dve.tensor_reduce(r0s["max"][:, :], lg, AX.X, ALU.max))
            dve.tensor_tensor(r0["exp"][:, :, :], lg, wide(r0s["max"]), ALU.subtract).then_inc(route_exp, 1)
            dve.wait_ge(route_exp, 2)
            linked(dve, dve.tensor_reduce(r0s["sum"][:, :], r0["exp"][:, :, :], AX.X, ALU.add))
            linked(dve, dve.reciprocal(r0s["rsum"][:, :], r0s["sum"][:, :]))
            linked(dve, dve.tensor_tensor(r0["gate"][:, :, :], r0["exp"][:, :, :], wide(r0s["rsum"]), ALU.mult))
            linked(dve, dve.tensor_reduce(r0s["gmax"][:, :], r0["gate"][:, :, :], AX.X, ALU.max))
            linked(dve, dve.tensor_tensor(r0["rank"][:, :, :], r0["gate"][:, :, :], wide(r0s["gmax"]), ALU.is_equal))
            linked(dve, dve.tensor_tensor(r0["at"][:, :, :], r0["rank"][:, :, :], per_expert(rank_w), ALU.mult))
            linked(dve, dve.tensor_reduce(r0s["rmax"][:, :], r0["at"][:, :, :], AX.X, ALU.max))
            dve.tensor_tensor(first0[:, :, :], r0["at"][:, :, :], wide(r0s["rmax"]), ALU.is_equal).then_inc(first_done, 1)
            dve.wait_ge(rank_in_psum, 1)
            linked(dve, dve.scalar_tensor_tensor(r0["keep"][:, :, :].rearrange("p b e -> p (b e)"), RANK0[:, 0:B * E0], float(C0),
                                          first0[:, :, :].rearrange("p b e -> p (b e)"), ALU.is_le, ALU.mult))
            linked(dve, dve.tensor_tensor(r0["rank"][:, :, :], rank, per_expert(slot_base), ALU.add))
            linked(dve, dve.tensor_tensor(r0["at"][:, :, :], r0["rank"][:, :, :], r0["keep"][:, :, :], ALU.mult))
            linked(dve, dve.tensor_reduce(r0s["slot"][:, :], r0["at"][:, :, :], AX.X, ALU.add))
            linked(dve, dve.tensor_reduce(r0s["kept"][:, :], r0["keep"][:, :, :], AX.X, ALU.add))
            linked(dve, dve.tensor_tensor(r0s["alt"][:, :], spare_slot[:, :], r0s["kept"][:, :], ALU.mult))
            linked(dve, dve.tensor_tensor(r0s["alt2"][:, :], spare_slot[:, :], r0s["alt"][:, :], ALU.subtract))
            dve.tensor_tensor(scatter_at[:, :], r0s["slot"][:, :], r0s["alt2"][:, :], ALU.add).then_inc(places_done, 1)
            dve.tensor_copy(gather_at[:, :], r0s["slot"][:, :]).then_inc(places_done, 1)
            linked(dve, dve.tensor_tensor(r0["gkeep"][:, :, :], r0["gate"][:, :, :], r0["keep"][:, :, :], ALU.mult))
            linked(dve, dve.tensor_reduce(r0s["gsel"][:, :], r0["gkeep"][:, :, :], AX.X, ALU.add))
            linked(dve, dve.tensor_scalar(r0s["weight"][:, :], r0s["gsel"][:, :], tg[:, 4:5], None, ALU.mult))

            vector_ahead(dve)
            for e in range(E0):
                dve.wait_ge(y_in_psum, e + 1)
                if e >= 2:
                    dve.wait_ge(y_stored[e % 2], 16 * (e // 2))
                dve.tensor_copy(ye[:, e % 2, :, :], Y_BANK[e % 2][:, 0:256].rearrange("p (j d) -> p j d", d=D)).then_inc(y_done, 1)

        def scalar_moe0(act):
            act.wait_ge(route_exp, 1)
            act.activation(r0["exp"][:, :, :], r0["exp"][:, :, :], ACT.Exp).then_inc(route_exp, 1)

            scalar_ahead(act)

            def turn(e, v):
                act.wait_ge(xeT_in_psum, e + 1)
                act.activation(xeT[:, v, :], XE_BANK[v][:, 0:256], ACT.Copy).then_inc(xeT_done, 1)

            turn(0, 0)

            for e in range(E0):
                v = e % 2
                if e + 1 < E0:
                    turn(e + 1, 1 - v)
                for c in range(FC0):
                    act.wait_ge(h_in_psum, 2 * e + c // 2 + 1)
                    act.activation(hT0[:, v, c, :], H_BANKS[v][c // 2][:, (c % 2) * 256:(c % 2 + 1) * 256],
                                   ACT.Gelu_apprx_tanh, bias=b1e[:, e, c:c + 1]).then_inc(h_done, 1)

        def gpsimd_moe0(pool):
            pool.wait_ge(xn_kept, B)
            pool.wait_ge(places_done, 2)
            pool.wait_ge(slots_zeroed, 16)
            for b in range(B):
                pool.indirect_dma_start(out=t["x_slots"], out_offset=bass.IndirectOffsetOnAxis(ap=scatter_at[:, b:b + 1], axis=0),
                                        in_=XN[:, b, :], in_offset=None).then_inc(scattered, 16)
            pool.wait_ge(y_stored[0], E0 // 2 * 16)
            pool.wait_ge(y_stored[1], E0 // 2 * 16)
            gather(pool, 0)
            gather(pool, 1)

        def gather(pool, g):
            for b in range(4 * g, 4 * g + 4):
                pool.indirect_dma_start(out=XN[:, b, :], out_offset=None, in_=t["y_slots"],
                                        in_offset=bass.IndirectOffsetOnAxis(ap=gather_at[:, b:b + 1], axis=0)).then_inc(gathered[g], 16)

        def load_expert(sp, e):
            sp.dma_start(w1e[:, e % 4, :], t["w1_0"][e]).then_inc(expert_loaded[e % 4], 16)
            sp.dma_start(w2e[:, e % 4, :, :], t["w2_0"][e].rearrange("(c p) d -> p c d", p=128)).then_inc(expert_loaded[e % 4], 16)

        def sync_moe0(sp):
            def load_tokens(e):
                sp.dma_start(xe[:, e % 4, :, :], t["x_slots"][e * C0:(e + 1) * C0, :].rearrange("(j p) d -> p j d", p=128)).then_inc(expert_loaded[e % 4], 16)

            sp.wait_ge(scattered, B * 16)
            for e in range(4):
                load_tokens(e)
            for e in range(E0):
                sp.wait_ge(y_done, e + 1)
                sp.dma_start(t["y_slots"][e * C0:(e + 1) * C0, :].rearrange("(j p) d -> p j d", p=128), ye[:, e % 2, :, :]).then_inc(y_stored[e % 2], 16)
                if e + 4 < E0:
                    load_tokens(e + 4)
                    load_expert(sp, e + 4)

        XT4 = [bank[5], bank[6]]
        K_IN1, K_NEXT1 = (0, 1, 3, 5), (2, 4, 6, 7)

        def vector_g_stats(dve, g, k, updates):
            dve.wait_ge(x_updated, updates)
            for j in range(4):
                dve.bn_stats(g_stats[:, k % 2, j, :], X[:, 4 * g + j, :]).then_inc(g_stats_done, 1)
            dve.wait_ge(g_stats_done, 4 * (k + 1))
            for j in range(4):
                dve.bn_aggr(g_mv[:, k % 2, j, :], g_stats[:, k % 2, j, :]).then_inc(g_var_done, 1)

        def gpsimd_g_rstd(pool, k):
            u = k % 2
            pool.wait_ge(g_var_done, 4 * (k + 1))
            pool.tensor_tensor(g_veps[:, u, :], g_mv[:, u, :, 1], eps[:, :].to_broadcast([128, 4]), ALU.add).then_inc(g_veps_done, 1)
            pool.wait_ge(g_veps_done, k + 1)
            pool.tensor_tensor(g_rstd[:, u, :], g_veps[:, u, :], minus_half[:, :].to_broadcast([128, 4]), ALU.pow).then_inc(g_rstd_done, 1)

        def vector_g_apply(dve, g, n, k, used=0):
            dve.wait_ge(g_rstd_done, k + 1)
            at_least(dve, d3_in_psum, used)
            at_least(dve, g_xnT_in_psum, n - 1)
            for j in range(4):
                dve.tensor_scalar(xn4[:, n % 2, j, :], X[:, 4 * g + j, :], g_mv[:, k % 2, j, 0:1], g_rstd[:, k % 2, j:j + 1],
                                  ALU.subtract, ALU.mult).then_inc(g_xn_done, 1)

        def tensor_g_xnT(pe, n, psum):
            pe.wait_ge(g_xn_done, 4 * (n + 1))
            at_least(pe, g_xnT_done, n)
            for j in range(4):
                m = pe.transpose(psum[:, j * 128:(j + 1) * 128], xn4[:, n % 2, j, :], ident[:, :])
            m.then_inc(g_xnT_in_psum, 1)

        def scalar_g_xnT(act, n, psum):
            act.wait_ge(g_xnT_in_psum, n + 1)
            act.activation(xnT4[:, n % 2, :], psum[:, :], ACT.Copy).then_inc(g_xnT_done, 1)

        MIX = [bank[4], bank[7]]

        def tensor_mix1(pe):
            pe.wait_ge(y_done, E0)
            for g in range(4):
                tensor_g_xnT(pe, g, XT4[g % 2])
                pe.wait_ge(g_xnT_done, g + 1)
                at_least(pe, x_updated, B + 8 * (g - 1) if g >= 2 else 0)
                for j in range(4):
                    b = 4 * g + j
                    dst = MIX[g % 2][:, j * D:(j + 1) * D]
                    pe.matmul(dst, xnT4[:, g % 2, j * 128:(j + 1) * 128], w1x[:, :], start=True, stop=False)
                    m = pe.matmul(dst, ones_row[:, :], mix_row[:, b * D:(b + 1) * D], start=False, stop=True)
                m.then_inc(mix_in_psum, 1)

        def vector_mix1(dve):
            def next_norm(g):
                k = K_NEXT1[g]
                dve.wait_ge(g_rstd_done, k + 1)
                for j in range(4):
                    m = dve.tensor_scalar(XN[:, 4 * g + j, :], X[:, 4 * g + j, :], g_mv[:, k % 2, j, 0:1], g_rstd[:, k % 2, j:j + 1],
                                          ALU.subtract, ALU.mult)
                linked(dve, m)
                dve.tensor_reduce(absmax1[:, 4 * g:4 * g + 4], XN[:, 4 * g:4 * g + 4, :], AX.X, ALU.max,
                                  apply_absolute_value=True).then_inc(absmax_done, 1)

            def experts_added(g):
                dve.wait_ge(gathered[g], 64)
                for b in range(4 * g, 4 * g + 4):
                    dve.scalar_tensor_tensor(X[:, b, :], XN[:, b, :], r0s["weight"][:, b:b + 1], X[:, b, :],
                                             ALU.mult, ALU.add).then_inc(combined0, 1)
                dve.wait_ge(combined0, 4 * g + 4)

            experts_added(0)
            vector_g_stats(dve, 0, K_IN1[0], B)
            experts_added(1)
            vector_g_stats(dve, 1, K_IN1[1], B)
            vector_g_apply(dve, 0, 0, K_IN1[0])
            for g in range(4):
                if g < 3:
                    vector_g_apply(dve, g + 1, g + 1, K_IN1[g + 1])
                dve.wait_ge(mix_in_psum, g + 1)
                x = X[:, 4 * g:4 * g + 4, :].rearrange("p b d -> p (b d)")
                dve.scalar_tensor_tensor(x, MIX[g % 2][:, :], tg[:, 1:2], x, ALU.mult, ALU.add).then_inc(x_updated, 8)
                if g >= 1:
                    next_norm(g - 1)
                vector_g_stats(dve, g, K_NEXT1[g], B + 8 * g + 8)
                if g < 2:
                    experts_added(g + 2)
                    vector_g_stats(dve, g + 2, K_IN1[g + 2], B)
            next_norm(3)

        def scalar_mix1(act):
            for g in range(4):
                scalar_g_xnT(act, g, XT4[g % 2])

        def gpsimd_mix1(pool):
            for k in range(8):
                gpsimd_g_rstd(pool, k)
                if k < 2:
                    gather(pool, k + 2)

        GATE_BANK = [bank[0], bank[2], bank[4]]
        UP_BANK = [bank[1], bank[3], bank[7]]
        DOWN_BANK = [bank[0], bank[2], bank[1], bank[3]]

        def tensor_ffn1(pe):
            def spread_max(k, col):
                pe.wait_ge(colmax_done, k + 1)
                pe.transpose(bank[0][0:1, 128:256], col[:, :], ident[:, :]).then_inc(maxrow_in_psum, 1)
                pe.wait_ge(cell_done, k + 1)
                pe.matmul(bank[0][:, 256:257], ones_row[:, :], cell1[:, k:k + 1], start=True, stop=True).then_inc(max_in_psum, 1)

            spread_max(0, col1["xmax"])

            def turn(g):
                pe.wait_ge(xq_done, g + 1)
                at_least(pe, xqT_done, g - 1)
                for j in range(4):
                    m = pe.transpose(XQ_BANK[g % 2][:, j * 128:(j + 1) * 128], xq1[:, j, :], ident[:, :])
                m.then_inc(xqT_in_psum, 1)

            turn(0)
            for g in range(4):
                pe.wait_ge(xqT_done, g + 1)
                for c, (lo, hi) in enumerate(ROWS1):
                    if g == 0 and c == 0:
                        pe.wait_ge(quant_step, XINV_STEP)
                    at_least(pe, silu_done, 3 * (g - 1) + c + 1)
                    at_least(pe, h1_done, 3 * (g - 1) + c + 1)
                    pe.matmul(GATE_BANK[c][0:hi - lo, :], wguT1[:, 0, lo:hi], xqT1[:, g % 2, :], start=True, stop=True)
                    pe.matmul(UP_BANK[c][0:hi - lo, :], wguT1[:, 1, lo:hi], xqT1[:, g % 2, :], start=True, stop=True).then_inc(gu_in_psum, 1)
                if g < 3:
                    turn(g + 1)
            pe.wait_ge(silu_done, 12)
            spread_max(1, col1["hmax"])
            for g in range(4):
                at_least(pe, h1_done, 12)
                pe.wait_ge(hq_done, 3 * g + 3)
                if g == 0:
                    pe.wait_ge(quant_step, HINV_STEP)
                for j in range(4):
                    for c, (lo, hi) in enumerate(ROWS1):
                        tok = (4 * g + j) * 128
                        m = pe.matmul(DOWN_BANK[g][:, j * D:(j + 1) * D], hq1[0:hi - lo, c, tok:tok + 128], wdT1[0:hi - lo, c, :],
                                      start=(c == 0), stop=(c == 2))
                m.then_inc(down_in_psum, 1)

        def vector_ffn1(dve):
            def scale_of(k, columns, colmax, scale, inv):
                dve.tensor_reduce(colmax[:, :], columns, AX.X, ALU.max).then_inc(colmax_done, 1)
                dve.wait_ge(maxrow_in_psum, k + 1)
                dve.tensor_reduce(cell1[:, k:k + 1], bank[0][0:1, 128:256], AX.X, ALU.max).then_inc(cell_done, 1)
                dve.wait_ge(max_in_psum, k + 1)
                link(dve, dve.tensor_scalar(scale[:, :], bank[0][:, 256:257], clip_sig[:, k:k + 1], 1.0 / QMAX, ALU.mult, ALU.mult))
                link(dve, dve.reciprocal(inv[:, :], scale[:, :]))

            dve.wait_ge(absmax_done, 4)
            scale_of(0, absmax1[:, :], col1["xmax"], col1["xscale"], col1["xinv"])
            assert steps[0] == XINV_STEP
            link(dve, dve.tensor_scalar(guscale1[:, :, :].rearrange("p a c -> p (a c)"), wscale1[:, 0:6], col1["xscale"][:, :], None, ALU.mult))

            def quantise(g):
                at_least(dve, xqT_in_psum, g)
                x4 = XN[:, 4 * g:4 * g + 4, :]
                link(dve, dve.tensor_scalar(x4, x4, col1["xinv"][:, :], QMAX, ALU.mult, ALU.min))
                dve.tensor_scalar(xq1[:, :, :], x4, -QMAX - 1.0, MAGIC, ALU.max, ALU.add).then_inc(xq_done, 1)

            quantise(0)
            for g in range(4):
                if g < 3:
                    quantise(g + 1)
                for c, (lo, hi) in enumerate(ROWS1):
                    h = h1[0:hi - lo, c, g * 512:(g + 1) * 512]
                    dve.wait_ge(silu_done, 3 * g + c + 1)
                    dve.scalar_tensor_tensor(h, UP_BANK[c][0:hi - lo, :], guscale1[0:hi - lo, 1, c:c + 1], silu1[0:hi - lo, c, :],
                                             ALU.mult, ALU.mult).then_inc(h1_done, 1)
                    dve.wait_ge(h1_done, 3 * g + c + 1)
                    m = dve.tensor_reduce(hmax1[0:hi - lo, 3 * g + c:3 * g + c + 1], h, AX.X, ALU.max, apply_absolute_value=True)
            link(dve, m)
            scale_of(1, hmax1[:, :], col1["hmax"], col1["hscale"], col1["hinv"])
            assert steps[0] == HINV_STEP
            for g in range(4):
                tok = slice(512 * g, 512 * g + 512)
                for c, (lo, hi) in enumerate(ROWS1):
                    h = h1[0:hi - lo, c, tok]
                    m = dve.tensor_scalar(h, h, col1["hinv"][0:hi - lo, :], QMAX, ALU.mult, ALU.min)
                link(dve, m)
                for c, (lo, hi) in enumerate(ROWS1):
                    h = h1[0:hi - lo, c, tok]
                    dve.tensor_scalar(h, h, -QMAX - 1.0, MAGIC, ALU.max, ALU.add).then_inc(hq_rounded, 1)
            link(dve, dve.tensor_tensor(col1["out"][:, :], col1["hscale"][:, :], tg[:, 5:6], ALU.mult))
            for g in range(4):
                dve.wait_ge(down_in_psum, g + 1)
                out = tmp512[:, g % 2, :].rearrange("p (j d) -> p j d", d=D)
                link(dve, dve.scalar_tensor_tensor(out, DOWN_BANK[g][:, :].rearrange("p (j d) -> p j d", d=D), col1["out"][:, :],
                                              drow1[:, :].unsqueeze(1).to_broadcast([128, 4, D]), ALU.mult, ALU.mult))
                dve.tensor_tensor(X[:, 4 * g:4 * g + 4, :], out, X[:, 4 * g:4 * g + 4, :], ALU.add).then_inc(x_updated, 4)

        def scalar_ffn1(act):
            def turn(g):
                act.wait_ge(xqT_in_psum, g + 1)
                act.activation(xqT1[:, g % 2, :], XQ_BANK[g % 2][:, :], ACT.Identity, bias=minus_magic[:, :]).then_inc(xqT_done, 1)

            turn(0)
            for g in range(4):
                for c, (lo, hi) in enumerate(ROWS1):
                    act.wait_ge(gu_in_psum, 3 * g + c + 1)
                    at_least(act, h1_done, 3 * (g - 1) + c + 1)
                    if g == 0 and c == 0:
                        act.wait_ge(quant_step, GUSCALE_STEP)
                    act.activation(silu1[0:hi - lo, c, :], GATE_BANK[c][0:hi - lo, :], ACT.Silu,
                                   scale=guscale1[0:hi - lo, 0, c:c + 1]).then_inc(silu_done, 1)
                if g < 3:
                    turn(g + 1)
            for g in range(4):
                tok = slice(512 * g, 512 * g + 512)
                for c, (lo, hi) in enumerate(ROWS1):
                    act.wait_ge(hq_rounded, 3 * g + c + 1)
                    act.activation(hq1[0:hi - lo, c, tok], h1[0:hi - lo, c, tok], ACT.Identity, bias=minus_magic[0:hi - lo, :]).then_inc(hq_done, 1)

        KV2 = [bank[0], bank[1], bank[2], bank[3], bank[4], bank[7], bank[6]]
        Q2, S2, ET2, AV2 = bank[0], (bank[1], bank[4]), bank[2], bank[3]
        KB2 = [(0, 6), (6, 12), (12, 16)]

        def tensor_attn2(pe):
            pe.wait_ge(attn2_loaded, 4 * 16)
            pe.wait_ge(x_updated, 4 * B)
            for n, (lo, hi) in enumerate(KB2):
                pe.matmul(KV2[n][:, 0:(hi - lo) * T], wqkv2[:, 1, :], ctxT[:, lo:hi, :].rearrange("p b t -> p (b t)"),
                          start=True, stop=True).then_inc(kv2_in_psum, 1)
            for n in range(4):
                for j in range(4):
                    m = pe.matmul(KV2[3 + n][0:T, j * D:(j + 1) * D], ctxT[:, 4 * n + j, :], wqkv2[:, 2, :], start=True, stop=True)
                m.then_inc(kv2_in_psum, 1)
            tensor_g_xnT(pe, 4, XT4[0])
            pe.wait_ge(v2_done, 4)
            pe.wait_ge(k2_done, 3)
            tensor_g_xnT(pe, 5, XT4[1])

            def scores(g):
                pe.wait_ge(g_xnT_done, g + 5)
                at_least(pe, q2_done, g)
                pe.matmul(Q2[:, :], wqkv2[:, 0, :], xnT4[:, g % 2, :], start=True, stop=True).then_inc(q2_in_psum, 1)
                pe.wait_ge(q2_done, g + 1)
                at_least(pe, shift2_done, g - 1)
                for j in range(4):
                    m = pe.matmul(S2[g % 2][:, j * T:(j + 1) * T], qT2[:, j * 128:(j + 1) * 128], kT2[:, 4 * g + j, :], start=True, stop=True)
                m.then_inc(s2_in_psum, 1)

            scores(0)
            for g in range(4):
                if g < 3:
                    scores(g + 1)
                if g < 2:
                    tensor_g_xnT(pe, g + 6, XT4[g % 2])
                pe.wait_ge(exp2_done, g + 1)
                at_least(pe, eT2_done, g)
                for j in range(4):
                    m = pe.transpose(ET2[0:T, j * 128:(j + 1) * 128], e2[:, g % 2, j, :], ident[:, :])
                m.then_inc(eT2_in_psum, 1)
                pe.wait_ge(eT2_done, g + 1)
                at_least(pe, x_updated, 4 * B + 4 * g)
                for j in range(4):
                    m = pe.matmul(AV2[:, j * D:(j + 1) * D], eT2[:, j * 128:(j + 1) * 128], v2[:, 4 * g + j, :], start=True, stop=True)
                m.then_inc(av2_in_psum, 1)

        def vector_attn2(dve):
            vector_g_stats(dve, 0, 8, 4 * B)
            for n in range(4):
                dve.wait_ge(kv2_in_psum, 4 + n)
                dve.tensor_tensor(v2[:, 4 * n:4 * n + 4, :], KV2[3 + n][0:T, :].rearrange("p (j d) -> p j d", d=D),
                                  bv2[:, :].unsqueeze(1).to_broadcast([T, 4, D]), ALU.add).then_inc(v2_done, 1)
            vector_g_apply(dve, 0, 4, 8)

            def shifted(g):
                sc = S2[g % 2][:, 0:4 * T].rearrange("p (j t) -> p j t", t=T)
                dve.wait_ge(s2_in_psum, g + 1)
                linked(dve, dve.tensor_reduce(s2["max"][:, :], sc, AX.X, ALU.max))
                at_least(dve, eT2_in_psum, g - 1)
                dve.tensor_tensor(e2[:, g % 2, :, :], sc, s2["max"][:, :].unsqueeze(2).to_broadcast([128, 4, T]), ALU.subtract).then_inc(shift2_done, 1)

            def sums(g):
                dve.wait_ge(exp2_done, g + 1)
                linked(dve, dve.tensor_reduce(s2["sum"][:, :], e2[:, g % 2, :, :], AX.X, ALU.add))
                linked(dve, dve.reciprocal(s2["rsum"][:, :], s2["sum"][:, :]))
                linked(dve, dve.tensor_scalar(s2["out"][:, :], s2["rsum"][:, :], tg[:, 2:3], None, ALU.mult))

            vector_g_stats(dve, 1, 9, 4 * B)
            vector_g_apply(dve, 1, 5, 9)
            vector_g_stats(dve, 2, 10, 4 * B)
            shifted(0)
            for g in range(4):
                if g < 3:
                    if g < 2:
                        vector_g_apply(dve, g + 2, g + 6, g + 10)
                    if g < 1:
                        vector_g_stats(dve, 3, 11, 4 * B)
                    shifted(g + 1)
                sums(g)
                dve.wait_ge(av2_in_psum, g + 1)
                out = tmp512[:, g % 2, :].rearrange("p (j d) -> p j d", d=D)
                linked(dve, dve.tensor_tensor(out, AV2[:, :].rearrange("p (j d) -> p j d", d=D),
                                       s2["out"][:, :].unsqueeze(2).to_broadcast([128, 4, D]), ALU.mult))
                dve.tensor_tensor(X[:, 4 * g:4 * g + 4, :], out, X[:, 4 * g:4 * g + 4, :], ALU.add).then_inc(x_updated, 4)

        def scalar_attn2(act):
            for n, (lo, hi) in enumerate(KB2):
                act.wait_ge(kv2_in_psum, n + 1)
                act.activation(kT2[:, lo:hi, :].rearrange("p b t -> p (b t)"), KV2[n][:, 0:(hi - lo) * T], ACT.Identity,
                               bias=bqk2[:, 1:2]).then_inc(k2_done, 1)
            scalar_g_xnT(act, 4, XT4[0])
            scalar_g_xnT(act, 5, XT4[1])

            def queries(g):
                act.wait_ge(q2_in_psum, g + 1)
                act.activation(qT2[:, :], Q2[:, :], ACT.Identity, bias=bqk2[:, 0:1]).then_inc(q2_done, 1)

            def exps(g):
                act.wait_ge(shift2_done, g + 1)
                act.activation(e2[:, g % 2, :, :], e2[:, g % 2, :, :], ACT.Exp, scale=D ** -0.5).then_inc(exp2_done, 1)

            queries(0)
            exps(0)
            for g in range(4):
                if g < 3:
                    queries(g + 1)
                if g < 2:
                    scalar_g_xnT(act, g + 6, XT4[g % 2])
                if g < 3:
                    exps(g + 1)
                act.wait_ge(eT2_in_psum, g + 1)
                act.activation(eT2[:, :], ET2[0:T, :], ACT.Copy).then_inc(eT2_done, 1)

        def gpsimd_attn2(pool):
            for k in range(8, 12):
                gpsimd_g_rstd(pool, k)

        SETS2 = [(bank[0], bank[1], bank[2]), (bank[3], bank[4], bank[7])]
        MISC2 = bank[6]
        GT2 = bank[5]
        PAIRS2 = [4, 0, 1, 2, 3]

        def tensor_moe2(pe):
            pe.wait_ge(moe2_loaded, 5 * 16)
            pe.wait_ge(x_updated, 5 * B)
            for g in range(4):
                tensor_g_xnT(pe, g + 8, GT2)
                pe.wait_ge(g_xnT_done, g + 9)
                for j in range(4):
                    dst = MISC2[:, (4 * g + j) * E2:(4 * g + j + 1) * E2]
                    m = pe.matmul(dst, xnT2[:, g, j * 128:(j + 1) * 128], rw2[:, :], start=True, stop=True)
            m.then_inc(logits2_in_psum, 1)

            def up(n):
                at_least(pe, h2_done, n - 1)
                for a in range(2):
                    m = pe.matmul(SETS2[n % 2][a][:, :], w13_2[:, a, PAIRS2[n % 5], :], xnT2[:, n // 5, :], start=True, stop=True)
                m.then_inc(ab2_in_psum, 1)

            def turn_gates(g):
                at_least(pe, gT2_done, g)
                for j in range(4):
                    m = pe.transpose(GT2[:, :].bitcast(BF16)[0:3 * E2, j * 128:(j + 1) * 128],
                                     gate_parts[:, 4 * g + j, :, :].rearrange("p s e -> p (s e)"), ident_b[:, :])
                m.then_inc(gT2_in_psum, 1)

            up(0)
            up(1)
            pe.wait_ge(gates2_done, 1)
            turn_gates(0)
            for g in range(4):
                pe.wait_ge(gT2_done, g + 1)
                for i in range(1, 5):
                    n = 5 * g + i
                    pe.matmul(SETS2[n % 2][2][:, :], pair_sel[:, PAIRS2[i], :], gT2[:, :], start=True, stop=True).then_inc(g2_in_psum, 1)
                    if i == 4 and g < 3:
                        turn_gates(g + 1)
                    if n < 19:
                        up(n + 1)
                at_least(pe, x_updated, 5 * B + 4 * g)
                pe.wait_ge(h2_done, 5 * g + 5)
                for j in range(4):
                    for p in range(5):
                        m = pe.matmul(MISC2[:, j * D:(j + 1) * D], h2[:, p, j * 128:(j + 1) * 128], w2_2[:, p, :],
                                      start=(p == 0), stop=(p == 4))
                m.then_inc(out2_in_psum, 1)
                if g < 3:
                    up(5 * g + 6)

        def vector_moe2(dve):
            def wide(a):
                return r2s[a][:, :].unsqueeze(2).to_broadcast([128, B, E2])

            ranks = rank_w[:, :].unsqueeze(1).to_broadcast([128, B, E2])
            lg = MISC2[:, 0:B * E2].rearrange("p (j e) -> p j e", e=E2)

            def best(src, m, r, tmp, onehot):
                linked(dve, dve.tensor_reduce(r2s[m][:, :], src, AX.X, ALU.max))
                linked(dve, dve.tensor_tensor(r2[tmp][:, :, :], src, wide(m), ALU.is_equal))
                linked(dve, dve.tensor_tensor(r2["a"][:, :, :], r2[tmp][:, :, :], ranks, ALU.mult))
                linked(dve, dve.tensor_reduce(r2s[r][:, :], r2["a"][:, :, :], AX.X, ALU.max))
                linked(dve, dve.tensor_tensor(r2[onehot][:, :, :], r2["a"][:, :, :], wide(r), ALU.is_equal))

            def route():
                dve.wait_ge(logits2_in_psum, 1)
                linked(dve, dve.tensor_tensor(r2["logit"][:, :, :], lg, rb2[:, :].unsqueeze(1).to_broadcast([128, B, E2]), ALU.add))
                best(r2["logit"][:, :, :], "m1", "r1", "rank", "first")
                linked(dve, dve.scalar_tensor_tensor(r2["rest"][:, :, :].rearrange("p j e -> p (j e)"), r2["first"][:, :, :].rearrange("p j e -> p (j e)"),
                                              MASKED, r2["logit"][:, :, :].rearrange("p j e -> p (j e)"), ALU.mult, ALU.add))
                best(r2["rest"][:, :, :], "m2", "r2", "rank2", "second")
                dve.tensor_tensor(r2s["d"][:, :], r2s["m2"][:, :], r2s["m1"][:, :], ALU.subtract).then_inc(gap2_done, 1)
                dve.wait_ge(gap2_exp, 1)
                linked(dve, dve.tensor_scalar(r2s["den"][:, :], r2s["e"][:, :], 1.0, None, ALU.add))
                linked(dve, dve.reciprocal(r2s["g1"][:, :], r2s["den"][:, :]))
                linked(dve, dve.tensor_tensor(r2s["g2"][:, :], r2s["e"][:, :], r2s["g1"][:, :], ALU.mult))
                dve.tensor_tensor(r2["a"][:, :, :], r2["first"][:, :, :], wide("g1"), ALU.mult)
                linked(dve, dve.tensor_tensor(r2["b"][:, :, :], r2["second"][:, :, :], wide("g2"), ALU.mult))
                linked(dve, dve.tensor_tensor(r2["gate"][:, :, :], r2["a"][:, :, :], r2["b"][:, :, :], ALU.add))
                linked(dve, dve.tensor_copy(gate_parts[:, :, 0, :], r2["gate"][:, :, :]))
                linked(dve, dve.tensor_tensor(r2["a"][:, :, :], r2["gate"][:, :, :], gate_parts[:, :, 0, :], ALU.subtract))
                linked(dve, dve.tensor_copy(gate_parts[:, :, 1, :], r2["a"][:, :, :]))
                dve.tensor_tensor(gate_parts[:, :, 2, :], r2["a"][:, :, :], gate_parts[:, :, 1, :], ALU.subtract).then_inc(gates2_done, 1)

            def activate(g, i):
                n = 5 * g + i
                a, b, gate = SETS2[n % 2]
                u = u2[:, n % 2, :]
                p = PAIRS2[i]
                dve.wait_ge(tanh2_done, n + 1)
                linked(dve, dve.scalar_tensor_tensor(u, th2[:, n % 2, :], 1.0, a[:, :], ALU.add, ALU.mult))
                if i == 0:
                    at_least(dve, out2_in_psum, g)
                    dve.scalar_tensor_tensor(h2[:, p, :], u, 0.5, b[:, :], ALU.mult, ALU.mult).then_inc(h2_done, 1)
                else:
                    linked(dve, dve.tensor_tensor(u, u, b[:, :], ALU.mult))
                    dve.wait_ge(g2_in_psum, 4 * g + i)
                    dve.tensor_tensor(h2[:, p, :], u, gate[:, :], ALU.mult).then_inc(h2_done, 1)

            vector_g_stats(dve, 0, 12, 4 * B + 4)
            for g in range(4):
                if g < 3:
                    vector_g_stats(dve, g + 1, g + 13, 4 * B + 4 * g + 8)
                vector_g_apply(dve, g, g + 8, g + 12)
            route()
            for g in range(4):
                for i in range(5):
                    activate(g, i)
                dve.wait_ge(out2_in_psum, g + 1)
                x4 = X[:, 4 * g:4 * g + 4, :].rearrange("p j d -> p (j d)")
                dve.scalar_tensor_tensor(x4, MISC2[:, :], tg[:, 6:7], x4, ALU.mult, ALU.add).then_inc(x_updated, 4)

        def scalar_moe2(act):
            def tanh(g, i):
                n = 5 * g + i
                act.wait_ge(ab2_in_psum, n + 1)
                act.activation(th2[:, n % 2, :], SETS2[n % 2][0][:, :], ACT.Tanh, scale=0.5).then_inc(tanh2_done, 1)

            for g in range(4):
                act.wait_ge(g_xnT_in_psum, g + 9)
                act.activation(xnT2[:, g, :], GT2[:, :], ACT.Copy).then_inc(g_xnT_done, 1)
            tanh(0, 0)
            tanh(0, 1)
            act.wait_ge(gap2_done, 1)
            act.activation(r2s["e"][:, :], r2s["d"][:, :], ACT.Exp).then_inc(gap2_exp, 1)

            def gates(g):
                act.wait_ge(gT2_in_psum, g + 1)
                at_least(act, g2_in_psum, 4 * g)
                act.activation(gT2[:, :], GT2[:, :].bitcast(BF16)[0:3 * E2, 0:512], ACT.Copy).then_inc(gT2_done, 1)

            gates(0)
            for g in range(4):
                for i in range(2 if g == 0 else 0, 5):
                    tanh(g, i)
                    if i == 3 and g < 3:
                        gates(g + 1)

        def gpsimd_moe2(pool):
            for k in range(12, 16):
                gpsimd_g_rstd(pool, k)

        RING3 = bank[0:4]
        PROJ3, SUMS3 = bank[4], [bank[7], bank[0]]
        CHUNKS3 = [(half, aux, odd) for aux in range(2) for half in range(2) for odd in range(2)]

        def heads3(half, odd):
            return slice(8 * half + odd, 8 * half + 8, 2)

        TILES3, NORMS3 = B, 2 * B
        SCORES_RING3, EXP_RING3 = RING3[2:4], RING3[0:2]

        def turned3(b, more):
            return 5 * b + 5 + (1 if first(b) else 0) - (3 if more == 0 else 0)

        def first(b):
            return isinstance(b, int) and b == 0

        def tensor_attn3(pe):
            def project_early(b, u):
                pe.wait_ge(xnT_done, TILES3 + b + 1)
                pe.wait_ge(ctx_b_done, B + b + 1)
                at_least(pe, v3_done, 2 * b)
                pe.matmul(PROJ3[:, 0:2 * D], xnT[:, u, :], wqkv3[:, 0:2 * D], start=True, stop=True)
                pe.matmul(PROJ3[0:T, 2 * D:3 * D], ctx_b[:, u, :], wkva3[:, 0:D], start=True, stop=True).then_inc(qkv3_in_psum, 1)

            def project_late(b, u):
                pe.wait_ge(proj3_done, 2 * b + 2)
                pe.matmul(PROJ3[:, 0:D], xnT[:, u, :], wqkv3[:, 2 * D:3 * D], start=True, stop=True)
                pe.matmul(PROJ3[0:T, D:2 * D], ctx_b[:, u, :], wkva3[:, D:2 * D], start=True, stop=True).then_inc(qkv3_in_psum, 1)

            def turn(b, u, n, free):
                src, p, w = ((sk3, 128, 128), (sa3, T, T + 1), (sq3[:, u], 128, 128))[n]
                at_least(pe, *free)
                pe.wait_ge(split3_done, 3 * b + n + 1)
                dst = T0[(n + 1) % 2][:, :].bitcast(BF16)
                for c in range(8):
                    m = pe.transpose(dst[:, c * w:c * w + p], src[:, 2 * c:2 * c + 2, :].rearrange("p a d -> p (a d)"),
                                     ident_b[0:p, 0:p])
                m.then_inc(t3_in_psum, 1)

            def output(b, count):
                pe.wait_ge(t3_done, count)
                pe.matmul(PROJ3[:, 3 * D:4 * D], oT3[:, :], wo3[:, :], start=True, stop=False)
                pe.matmul(PROJ3[:, 3 * D:4 * D], ones_row[:, :], bo3[:, :], start=False, stop=True).then_inc(wo3_in_psum, 1)

            def sums(b, u, aux, i):
                e, v = (ea3, va3) if aux else (em3, v3)
                for j in range(4):
                    m = pe.matmul(SUMS3[aux][32 * j:32 * j + 32, i * 128:(i + 1) * 128], v[:, u, 4 * i + j, :], e[:, 4 * i + j, :],
                                  start=True, stop=True)
                return m

            def scores(b, u, j):
                half, aux, odd = CHUNKS3[j]
                p, n = 64 * odd, (T if aux else 128)
                k = (kaT3 if aux else kT3)[:, u]
                at_least(pe, max3_done, 8 * b + j - 1)
                for i in range(4):
                    c = 4 * half + i
                    m = pe.matmul(SCORES_RING3[j % 2][:, i * n:(i + 1) * n], qT3[p:p + PARTS3, c, :], k[p:p + PARTS3, c, 0:n],
                                  start=True, stop=True)
                m.then_inc(s3_in_psum, 1)

            def scores_shifted(b, u, j):
                half, aux, odd = CHUNKS3[j]
                p, n = 64 * odd, (T if aux else 128)
                k = (kaT3 if aux else kT3)[:, u]
                if j < 2:
                    at_least(pe, o3_done, b)
                else:
                    pe.wait_ge(exp3_done, 8 * b + j - 1)
                for i in range(4):
                    c = 4 * half + i
                    m = pe.matmul(EXP_RING3[j % 2][0:n, i * 128:(i + 1) * 128], k[p:p + MAXES3, c, 0:n], qmT3[p:p + MAXES3, c, :],
                                  start=True, stop=True)
                m.then_inc(sT3_in_psum, 1)

            pe.wait_ge(attn3_loaded, 7 * 16)
            pe.wait_ge(x_updated, 6 * B)
            tensor_xnT(pe, TILES3 + 0, 0, T0[0])
            tensor_xnT(pe, TILES3 + 1, 1, T0[1])
            project_early(0, 0)
            project_late(0, 0)
            turn(0, 0, 0, (xnT_done, TILES3 + 2))
            turn(0, 0, 1, (xnT_done, TILES3 + 1))
            turn(0, 0, 2, (t3_done, 1))
            pe.wait_ge(t3_done, 2)
            tensor_xnT(pe, TILES3 + 2, 0, T0[0])
            project_early(1, 1)
            project_late(1, 1)
            pe.wait_ge(t3_done, 3)
            for j in range(8):
                scores(0, 0, j)
            turn(1, 1, 0, (t3_done, 3))
            turn(1, 1, 1, (xnT_done, TILES3 + 3))
            turn(1, 1, 2, (t3_done, 4))

            def tile(b, u, more):
                t = turned3(b, more)
                o = 0 if first(b) else 1
                pe.wait_ge(t3_done, t - 1)
                pe.wait_ge(maxcols3_done, b + 1)
                for c in range(8):
                    m = pe.transpose(T0[0][:, :].bitcast(BF16)[:, c * 128:(c + 1) * 128],
                                     sq3[:, u, 2 * c:2 * c + 2, :].rearrange("p a d -> p (a d)"), ident_b[:, :])
                m.then_inc(t3_in_psum, 1)
                pe.wait_ge(t3_done, t)
                if more >= 1:
                    scores(b + 1, 1 - u, 0)
                    scores(b + 1, 1 - u, 1)
                if o:
                    pe.wait_ge(o3_done, b)
                    pe.transpose(T0[1][:, 0:128], o3[:, :], ident[:, :]).then_inc(t3_in_psum, 1)
                if more >= 2:
                    project_early(b + 2, u)
                pe.wait_ge(t3_done, t + 1)
                for j in range(8):
                    if j == 2 and o:
                        if more >= 2:
                            pe.wait_ge(proj3_done, 2 * b + 6)
                        output(b - 1, t + 2)
                    scores_shifted(b, u, j)
                    if more >= 1 and j < 6:
                        scores(b + 1, 1 - u, j + 2)
                    if j >= 4:
                        pe.wait_ge(exp3_done, 8 * b + 4)
                        m = sums(b, u, 0, j - 4)
                m.then_inc(av3_in_psum, 1)
                for i in range(4):
                    pe.wait_ge(exp3_done, 8 * b + (7 if i < 2 else 8))
                    m = sums(b, u, 1, i)
                m.then_inc(av3_in_psum, 1)
                if o:
                    pe.wait_ge(x_updated, 6 * B + b)
                if more >= 2:
                    project_late(b + 2, u)
                if more >= 3:
                    pe.wait_ge(t3_done, t + 1)
                    tensor_xnT(pe, TILES3 + b + 3, 1 - u, T0[0])
                if more >= 2:
                    turn(b + 2, u, 0, (t3_done, t + 2 * o))
                    turn(b + 2, u, 1, (xnT_done, TILES3 + b + 4) if more >= 3 else (t3_done, t + 1))
                pe.wait_ge(ovT3_done, 2 * b + 2)
                for aux in range(2):
                    for i in range(4):
                        m = pe.transpose(SUMS3[aux][:, i * 128:(i + 1) * 128], ovT3[:, aux, i, :], ident[:, :])
                m.then_inc(av3_in_psum, 1)
                if more >= 2:
                    turn(b + 2, u, 2, (t3_done, t + o + 2))
            over_tiles(pe, tile, 2)
            pe.wait_ge(o3_done, B)
            pe.transpose(T0[1][:, 0:128], o3[:, :], ident[:, :]).then_inc(t3_in_psum, 1)
            output(B - 1, 5 * B)

        def vector_attn3(dve):
            def early(b, u):
                dve.wait_ge(qkv3_in_psum, 2 * b + 1)
                at_least(dve, split3_done, 3 * b)
                dve.tensor_tensor(qk3[:, :, :, :].rearrange("p a h d -> p (a h d)"), PROJ3[:, 0:2 * D], bqkv3[:, 0:2 * D], ALU.add).then_inc(proj3_done, 1)
                dve.tensor_tensor(ka3[:, :, :].rearrange("p h d -> p (h d)"), PROJ3[0:T, 2 * D:3 * D], bkva3[:, 0:D], ALU.add).then_inc(proj3_done, 1)

            def late(b, u):
                dve.wait_ge(qkv3_in_psum, 2 * b + 2)
                dve.tensor_tensor(v3[:, u, :, 0:8], PROJ3[:, 0:D].rearrange("p (h d) -> p h d", d=8),
                                  bqkv3[:, 2 * D:3 * D].rearrange("p (h d) -> p h d", d=8), ALU.add).then_inc(v3_done, 1)
                dve.tensor_tensor(va3[:, u, :, 0:8], PROJ3[0:T, D:2 * D].rearrange("p (h d) -> p h d", d=8),
                                  bkva3[:, D:2 * D].rearrange("p (h d) -> p h d", d=8), ALU.add).then_inc(v3_done, 1)

            def update(b):
                dve.wait_ge(wo3_in_psum, b + 1)
                dve.scalar_tensor_tensor(slot(b), PROJ3[:, 3 * D:4 * D], tg[:, 3:4], slot(b), ALU.mult, ALU.add).then_inc(x_updated, 1)

            def maxima(b, first_chunk, last_chunk):
                for j in range(first_chunk, last_chunk):
                    half, aux, odd = CHUNKS3[j]
                    n = T if aux else 128
                    dve.wait_ge(s3_in_psum, 8 * b + j + 1)
                    dve.tensor_reduce(mx3[:, aux, heads3(half, odd)], SCORES_RING3[j % 2][:, 0:4 * n].rearrange("p (h k) -> p h k", k=n),
                                      AX.X, ALU.max, negate=True).then_inc(max3_done, 1)

            def split_maxima(b, u):
                cols = sq3[:, u, :, PARTS3:MAXES3].rearrange("p h (a c) -> p h a c", c=3)
                m = mx3[:, :, :].rearrange("p a h -> p h a")
                left = mleft3[:, :, :].rearrange("p a h -> p h a")
                dve.wait_ge(max3_done, 8 * b + 8)
                dve.tensor_copy(cols[:, :, :, 0], m).then_inc(maxsplit3_step, 1)
                dve.wait_ge(maxsplit3_step, 3 * b + 3)
                dve.tensor_tensor(left, m, cols[:, :, :, 0], ALU.subtract).then_inc(maxsplit3_step, 1)
                dve.wait_ge(maxsplit3_step, 3 * b + 4)
                dve.tensor_copy(cols[:, :, :, 1], left).then_inc(maxsplit3_step, 1)
                dve.wait_ge(maxsplit3_step, 3 * b + 5)
                dve.tensor_tensor(cols[:, :, :, 2], left, cols[:, :, :, 1], ALU.subtract).then_inc(maxcols3_done, 1)

            vector_ln_stats(dve, 0, NORMS3 + 0, 0, 6 * B)
            vector_ln_apply(dve, 0, TILES3 + 0, 0, NORMS3 + 0)
            vector_ln_stats(dve, 1, NORMS3 + 1, 1, 6 * B)
            vector_ln_apply(dve, 1, TILES3 + 1, 1, NORMS3 + 1)
            dve.wait_ge(tanh_done, 2)
            dve.tensor_scalar(gate3[:, 1, :], g3_tanh[:, :], 0.5, 0.5, ALU.mult, ALU.add).then_inc(maxsplit3_step, 1)
            dve.wait_ge(maxsplit3_step, 1)
            dve.tensor_scalar(gate3[:, 0, :], gate3[:, 1, :], -1.0, 1.0, ALU.mult, ALU.add).then_inc(maxsplit3_step, 1)
            dve.wait_ge(stack3_ready, 2)
            vector_ln_stats(dve, 2, NORMS3 + 2, 0, 6 * B)
            early(0, 0)
            late(0, 0)
            vector_ln_apply(dve, 2, TILES3 + 2, 0, NORMS3 + 2)
            vector_ln_stats(dve, 3, NORMS3 + 3, 1, 6 * B)
            early(1, 1)
            late(1, 1)
            maxima(0, 0, 8)
            split_maxima(0, 0)

            def tile(b, u, more):
                if more >= 1:
                    maxima(b + 1, 0, 2)
                if more >= 2:
                    early(b + 2, u)
                if more >= 1:
                    maxima(b + 1, 2, 4)
                if not first(b):
                    update(b - 1)
                if more >= 1:
                    maxima(b + 1, 4, 8)
                    split_maxima(b + 1, 1 - u)
                if more >= 3:
                    vector_ln_apply(dve, b + 3, TILES3 + b + 3, 1 - u, NORMS3 + b + 3)
                if more >= 4:
                    vector_ln_stats(dve, b + 4, NORMS3 + b + 4, u)
                for aux in range(2):
                    dve.wait_ge(av3_in_psum, 3 * b + 1 + aux)
                    dve.tensor_copy(ovT3[:, aux, :, :].rearrange("p i q -> p (i q)"), SUMS3[aux][:, :]).then_inc(ovT3_done, 1)
                if more >= 2:
                    late(b + 2, u)
                sums = [SUMS3[aux][:, :].rearrange("p (h d) -> p h d", d=32) for aux in range(2)]
                dve.wait_ge(av3_in_psum, 3 * b + 3)
                for aux in range(2):
                    dve.reciprocal(rs3[:, aux, :], sums[aux][:, :, 8]).then_inc(o3_step, 1)
                dve.wait_ge(o3_step, 5 * b + 2)
                dve.tensor_tensor(rg3[:, :, :], rs3[:, :, :], gate3[:, :, :], ALU.mult).then_inc(o3_step, 1)
                dve.wait_ge(o3_step, 5 * b + 3)
                for aux in range(2):
                    dve.tensor_tensor(ov3[:, aux, :, :], sums[aux][:, :, 0:8], rg3[:, aux, :].unsqueeze(2).to_broadcast([128, H3, 8]),
                                      ALU.mult).then_inc(o3_step, 1)
                dve.wait_ge(o3_step, 5 * b + 5)
                dve.tensor_tensor(o3[:, :], ov3[:, 0, :, :].rearrange("p h d -> p (h d)"), ov3[:, 1, :, :].rearrange("p h d -> p (h d)"),
                                  ALU.add).then_inc(o3_done, 1)
            over_tiles(dve, tile, 2)
            update(B - 1)

        def scalar_attn3(act):
            def stack(u, n, count):
                dst, w = ((kT3[:, u], 128), (kaT3[:, u], T + 1), (qT3, 128))[n]
                k = T if n == 1 else w
                act.wait_ge(t3_in_psum, count)
                src = T0[(n + 1) % 2][:, :].bitcast(BF16)[:, 0:8 * w].rearrange("p (c k) -> p c k", k=w)
                act.activation(dst[:, :, 0:k], src[:, :, 0:k], ACT.Copy).then_inc(t3_done, 1)

            def turned_outputs(count):
                act.wait_ge(t3_in_psum, count)
                act.activation(oT3[:, :], T0[1][:, 0:128], ACT.Copy).then_inc(t3_done, 1)

            scalar_xnT(act, TILES3 + 0, 0, T0[0])
            scalar_xnT(act, TILES3 + 1, 1, T0[1])
            for n in range(3):
                stack(0, n, n + 1)
            scalar_xnT(act, TILES3 + 2, 0, T0[0])
            for n in range(3):
                stack(1, n, n + 4)

            def tile(b, u, more):
                t = turned3(b, more)
                o = 0 if first(b) else 1
                act.wait_ge(t3_in_psum, t + 1)
                act.activation(qmT3[:, :, :].rearrange("p c k -> p (c k)"), T0[0][:, :].bitcast(BF16)[:, :], ACT.Copy).then_inc(t3_done, 1)
                if o:
                    turned_outputs(t + 2)
                for j, (half, aux, odd) in enumerate(CHUNKS3):
                    n = T if aux else 128
                    act.wait_ge(sT3_in_psum, 8 * b + j + 1)
                    act.activation((ea3 if aux else em3)[:, heads3(half, odd), :], EXP_RING3[j % 2][0:n, :].rearrange("p (h q) -> p h q", q=128),
                                   ACT.Exp, scale=8 ** -0.5).then_inc(exp3_done, 1)
                if more >= 3:
                    scalar_xnT(act, TILES3 + b + 3, 1 - u, T0[0])
                if more >= 2:
                    for n in range(3):
                        stack(u, n, t + o + 2 + n)
            over_tiles(act, tile, 2)
            turned_outputs(5 * B)

        def gpsimd_attn3(pool):
            pool.wait_ge(x_updated, 3 * B)
            pool.memset(sq3[:, :, :, :], 0.0)
            pool.memset(sk3[:, :, :], 0.0)
            pool.memset(sa3[:, :, :], 0.0)
            pool.wait_ge(x_updated, 6 * B)
            pool.memset(v3[:, :, :, :], 0.0)
            pool.memset(va3[:, :, :, :], 0.0).then_inc(stack3_ready, 1)
            pool.wait_ge(stack3_ready, 1)
            pool.memset(v3[:, :, :, 8:9], 1.0)
            pool.memset(va3[:, :, :, 8:9], 1.0)
            pool.memset(sk3[:, :, PARTS3:PARTS3 + 3], 1.0)
            pool.memset(sa3[:, :, PARTS3 + 3:MAXES3], 1.0).then_inc(stack3_ready, 1)
            pool.wait_ge(stack3_ready, 2)

            def context(b, u):
                at_least(pool, qkv3_in_psum, 2 * b - 2)
                pool.tensor_tensor(ctx_b[:, u, :], ctxT[:, bass.ds(b, 1), :].rearrange("p a t -> p (a t)"),
                                   zero[:, 0:1].to_broadcast([128, T]), ALU.add).then_inc(ctx_b_done, 1)

            def part(stack, n, slots):
                first, step, count = slots
                v = stack[:, :, 0:PARTS3].rearrange("p h (s d) -> p h s d", d=8)
                return v[:, :, first:first + step * (count - 1) + 1:step, :]

            def split(b, u, q_free=0):
                Q_AT = ((0, 1, 3), (3, 1, 2), (5, 1, 1))
                K_AT = ((0, 3, 2), (1, 3, 2), (2, 1, 1))
                work = ((qk3[:, 1], sk3, 128, K_AT), (ka3[:, :, :], sa3, T, K_AT), (qk3[:, 0], sq3[:, u], 128, Q_AT))
                pool.wait_ge(proj3_done, 2 * b + 2)
                for n, (x, stack, p, at) in enumerate(work):
                    left = left3[n][0:p, :, :]
                    if n == 2:
                        at_least(pool, t3_in_psum, q_free)

                    def spread(src, slots):
                        return src.unsqueeze(2).to_broadcast([p, H3, slots[2], 8])

                    def nothing(slots):
                        return zero[0:p, :].unsqueeze(2).unsqueeze(3).to_broadcast([p, H3, slots[2], 8])
                    pool.tensor_tensor(part(stack, n, at[0]), spread(x, at[0]), nothing(at[0]), ALU.add).then_inc(split3_step, 1)
                    if n < 2:
                        pool.tensor_copy(part(stack, n, (5, 1, 1))[:, :, 0, :], x)
                    pool.wait_ge(split3_step, 9 * b + 3 * n + 1)
                    pool.tensor_tensor(left, x, stack[:, :, 0:8], ALU.subtract).then_inc(split3_step, 1)
                    pool.wait_ge(split3_step, 9 * b + 3 * n + 2)
                    pool.tensor_tensor(part(stack, n, at[1]), spread(left, at[1]), nothing(at[1]), ALU.add).then_inc(split3_step, 1)
                    pool.wait_ge(split3_step, 9 * b + 3 * n + 3)
                    pool.tensor_tensor(part(stack, n, at[2])[:, :, 0, :], left, part(stack, n, at[1])[:, :, 0, :], ALU.subtract).then_inc(split3_done, 1)

            gpsimd_ln_rstd(pool, NORMS3 + 0, 0)
            gpsimd_ln_rstd(pool, NORMS3 + 1, 1)
            context(0, 0)
            context(1, 1)
            gpsimd_ln_rstd(pool, NORMS3 + 2, 0)
            split(0, 0)
            context(2, 0)
            gpsimd_ln_rstd(pool, NORMS3 + 3, 1)
            split(1, 1)
            context(3, 1)

            def tile(b, u, more):
                if more >= 2:
                    split(b + 2, u, turned3(b, more) + 1)
                if more >= 4:
                    gpsimd_ln_rstd(pool, NORMS3 + b + 4, u)
                    context(b + 4, u)
            over_tiles(pool, tile, 2)

        D_BANK = bank[0:4]
        LOGITS3, PT_BANK = (bank[6], bank[7]), bank[4]
        IN_BANK = bank[4:8]
        F_BANK = [bank[0:4], bank[4:8]]
        ROWS_BANK, COMB_BANK = bank[0:2], bank[2:4]

        def tensor_moe3(pe):
            pe.wait_ge(moe3_loaded, 4 * 16)
            pe.wait_ge(x_updated, 7 * B)

            def logits(g):
                tensor_g_xnT(pe, g + 12, bank[5])
                pe.wait_ge(g_xnT_done, g + 13)
                at_least(pe, perm3_done, g - 1)
                pe.matmul(LOGITS3[g % 2][:, :], ctrl3[:, :], xnT4[:, g % 2, :], start=True, stop=True).then_inc(l3_in_psum, 1)

            logits(0)
            logits(1)
            for g in range(4):
                pe.wait_ge(perm3_done, g + 1)
                at_least(pe, pt3_done, g)
                for j in range(4):
                    tok = (4 * g + j) * 128
                    m = pe.transpose(PT_BANK[:, j * 128:(j + 1) * 128], perm3[:, tok:tok + 128], ident[:, :])
                m.then_inc(pt3_in_psum, 1)
                pe.wait_ge(pt3_done, g + 1)
                at_least(pe, d3_act_done, 2 * g)
                at_least(pe, d3_dve_done, 2 * g)
                for j in range(4):
                    for r in range(4):
                        p = slice(G3 * r, G3 * r + G3)
                        m = pe.matmul(D_BANK[r][:, j * 128:(j + 1) * 128], xn4[p, g % 2, j, :], pt3[p, g % 2, j, :], start=True, stop=True)
                m.then_inc(d3_in_psum, 1)
                if g < 2:
                    logits(g + 2)
            pe.wait_ge(f1_loaded, 16)
            pe.wait_ge(d3_act_done, 8)
            pe.wait_ge(d3_dve_done, 8)
            for e in range(E3):
                for s_ in range(SETS3):
                    m = pe.matmul(IN_BANK[e // 8][F3 * s_:F3 * s_ + F3, (e % 8) * NG3:(e % 8 + 1) * NG3], f1_3[:, SETS3 * e + s_, :],
                                  d3[:, :, SETS3 * e + s_], start=True, stop=True)
                if e % 8 == 7:
                    m.then_inc(in3_in_psum, 1)
            for r in range(4):
                pe.wait_ge(in3_done, 2 * r + 2)
                pe.wait_ge(in3_biased, 2 * r + 6)
                if r >= 2:
                    pe.wait_ge(out3_act_done, 2 * (r - 1))
                    pe.wait_ge(out3_dve_done, 2 * (r - 1))
                for e in range(8 * r, 8 * r + 8):
                    m = pe.matmul(F_BANK[r % 2][e % 8 // 2][:, e % 2 * 256:e % 2 * 256 + 256], f2_3[:, e, :],
                                  bd3[:, e, :, :].rearrange("p s g -> p (s g)"), start=True, stop=True)
                m.then_inc(f3_in_psum, 1)
            pe.wait_ge(out3_act_done, 8)
            pe.wait_ge(out3_dve_done, 8)

            def rows(b):
                at_least(pe, rows3_done, b - 1)
                for r in range(4):
                    m = pe.transpose(ROWS_BANK[b % 2][:, r * 128:(r + 1) * 128], out3[:, 4 * b + r, :], ident[:, :])
                m.then_inc(rows3_in_psum, 1)

            rows(0)
            for b in range(B):
                if b + 1 < B:
                    rows(b + 1)
                pe.wait_ge(rows3_done, b + 1)
                at_least(pe, x_updated, 7 * B + b - 1)
                for r in range(4):
                    tok = 128 * b + G3 * r
                    m = pe.matmul(COMB_BANK[b % 2][G3 * r:G3 * r + G3, 0:D], perm3[:, tok:tok + G3], rows3[:, b % 2, r, :], start=True, stop=True)
                m.then_inc(comb3_in_psum, 1)

        def d3_view(g, r):
            return d3[:, 16 * g + r:16 * g + 13 + r:4, :]

        def out3_view(r, k):
            at = 8 * SETS3 * r + 2 * SETS3 * k
            return out3[:, :, at:at + 2 * SETS3].rearrange("p g e -> p e g")

        def diagonal(r, s_):
            p = slice(F3 * s_, F3 * s_ + F3)
            return bd3[p, 8 * r:8 * r + 8, s_, :], in3[p, 8 * r:8 * r + 8, :]

        def vector_moe3(dve):
            vector_g_stats(dve, 0, 16, 7 * B)
            vector_g_stats(dve, 1, 17, 7 * B)
            vector_g_apply(dve, 0, 12, 16)
            vector_g_apply(dve, 1, 13, 17)
            vector_g_stats(dve, 2, 18, 7 * B)
            vector_g_stats(dve, 3, 19, 7 * B)
            dve.wait_ge(moe3_loaded, 4 * 16)

            def choose(g):
                dve.wait_ge(l3_in_psum, g + 1)
                lt = tmp512[:, g % 2, :].rearrange("p (g t) -> p g t", t=G3)
                linked(dve, dve.tensor_tensor(lt, LOGITS3[g % 2][:, :].rearrange("p (g t) -> p g t", t=G3), tie3[:, :].unsqueeze(1).to_broadcast([128, 16, G3]), ALU.add))
                linked(dve, dve.tensor_reduce(gmax3[:, :], lt, AX.X, ALU.max))
                dve.tensor_tensor(perm3[:, g * 512:(g + 1) * 512].rearrange("p (g t) -> p g t", t=G3), lt,
                                  gmax3[:, :].unsqueeze(2).to_broadcast([128, 16, G3]), ALU.is_equal).then_inc(perm3_done, 1)

            choose(0)
            for g in range(4):
                if g < 3:
                    choose(g + 1)
                if g < 2:
                    vector_g_apply(dve, g + 2, g + 14, g + 18, g + 1)
                dve.wait_ge(d3_in_psum, g + 1)
                for r in (2, 3):
                    dve.tensor_copy(d3_view(g, r), D_BANK[r][:, :].rearrange("p (j e) -> p j e", e=ES3)).then_inc(d3_dve_done, 1)
            for r in range(4):
                dve.wait_ge(in3_in_psum, r + 1)
                dve.tensor_tensor(in3[:, 8 * r:8 * r + 8, :], IN_BANK[r][:, :].rearrange("p (e g) -> p e g", g=NG3),
                                  bias3[:, 8 * r:8 * r + 8].unsqueeze(2).to_broadcast([128, 8, NG3]), ALU.add).then_inc(in3_biased, 1)

            def relu(r):
                dve.wait_ge(in3_biased, r + 1)
                dve.wait_ge(bd3_zeroed, r + 1)
                for s_ in (2, 3):
                    dst, src = diagonal(r, s_)
                    dve.tensor_scalar(dst, src, 0.0, None, ALU.max).then_inc(in3_biased, 1)

            def leave(r):
                dve.wait_ge(f3_in_psum, r + 1)
                for k in (2, 3):
                    dve.tensor_copy(out3_view(r, k), F_BANK[r % 2][k][:, :].rearrange("p (e g) -> p e g", g=NG3)).then_inc(out3_dve_done, 1)

            relu(0)
            for r in range(4):
                if r < 3:
                    relu(r + 1)
                leave(r)
            for b in range(B):
                dve.wait_ge(comb3_in_psum, b + 1)
                dve.scalar_tensor_tensor(X[:, b, :], COMB_BANK[b % 2][:, 0:D], tg[:, 7:8], X[:, b, :], ALU.mult, ALU.add).then_inc(x_updated, 1)

        def scalar_moe3(act):
            scalar_g_xnT(act, 12, bank[5])
            scalar_g_xnT(act, 13, bank[5])
            for g in range(4):
                act.wait_ge(pt3_in_psum, g + 1)
                act.activation(pt3[:, g % 2, :, :].rearrange("p j e -> p (j e)"), PT_BANK[:, :], ACT.Copy).then_inc(pt3_done, 1)
                act.wait_ge(d3_in_psum, g + 1)
                for r in (0, 1):
                    act.activation(d3_view(g, r), D_BANK[r][:, :].rearrange("p (j e) -> p j e", e=ES3), ACT.Copy).then_inc(d3_act_done, 1)
                if g < 2:
                    scalar_g_xnT(act, g + 14, bank[5])

            def relu(r):
                act.wait_ge(in3_biased, r + 1)
                act.wait_ge(bd3_zeroed, r + 1)
                for s_ in (0, 1):
                    dst, src = diagonal(r, s_)
                    act.activation(dst, src, ACT.Relu).then_inc(in3_done, 1)

            def leave(r):
                act.wait_ge(f3_in_psum, r + 1)
                for k in (0, 1):
                    act.activation(out3_view(r, k), F_BANK[r % 2][k][:, :].rearrange("p (e g) -> p e g", g=NG3), ACT.Copy).then_inc(out3_act_done, 1)

            relu(0)
            for r in range(4):
                if r < 3:
                    relu(r + 1)
                leave(r)
            for b in range(B):
                act.wait_ge(rows3_in_psum, b + 1)
                at_least(act, comb3_in_psum, b - 1)
                act.activation(rows3[:, b % 2, :, :].rearrange("p r d -> p (r d)"), ROWS_BANK[b % 2][:, :], ACT.Copy).then_inc(rows3_done, 1)

        def gpsimd_moe3(pool):
            for k in range(16, 20):
                gpsimd_g_rstd(pool, k)
            pool.wait_ge(in3_in_psum, 4)
            for r in range(4):
                pool.memset(bd3[:, 8 * r:8 * r + 8, :, :], 0.0).then_inc(bd3_zeroed, 1)

        @block.sync
        def _(sp):
            sp.dma_start(X[:, :, :], t["x"]).then_inc(x_loaded, 16)
            sp.dma_start(ident[:, :], t["ident"]).then_inc(const_loaded, 16)
            sp.dma_start(ident_b[:, :], t["ident_b"]).then_inc(const_loaded, 16)
            sp.dma_start(gates_in[:, :], t["gates"]).then_inc(const_loaded, 16)
            sp.dma_start(ones[:, :], t["ones"]).then_inc(const_loaded, 16)
            sp.dma_start(ctxT[:, :, :], t["ctxT"]).then_inc(ctx_loaded, 16)
            sp.dma_start(wq0[:, :], t["wq0"]).then_inc(wqkv0_loaded, 16)
            sp.dma_start(bq0[:, :], t["bq0"]).then_inc(wqkv0_loaded, 16)
            sp.dma_start(bk0[:, :], t["bk0"]).then_inc(wqkv0_loaded, 16)
            sp.dma_start(wk0[:, :], t["wk0"]).then_inc(wqkv0_loaded, 16)
            sp.dma_start(wv0[:, :], t["wv0"]).then_inc(wqkv0_loaded, 16)
            sp.dma_start(bv0[:, :, :], t["bv0"]).then_inc(wqkv0_loaded, 16)
            sp.dma_start(wo0[:, :, :], t["wo0"]).then_inc(wo0_loaded, 16)
            sp.dma_start(bo0[:, :], t["bo0"]).then_inc(wo0_loaded, 16)
            for name, dst in (("wg0", wg0), ("rank_w", rank_w), ("slot_base", slot_base), ("spare_slot", spare_slot),
                              ("tri_b", tri_b), ("ones_b", ones_b)):
                sp.dma_start(dst[:, :], t[name]).then_inc(route0_loaded, 16)
            sp.dma_start(b1e[:, :, :], t["b1_0"].rearrange("e p c -> p e c")).then_inc(route0_loaded, 16)
            sp.dma_start(b2e, t["b2_0"].rearrange("e x d -> x e d")).then_inc(route0_loaded, 16)
            sp.wait_ge(pool_ready, 4)
            sp.dma_start(t["x_slots"][0:NT, :].rearrange("(t p) d -> p t d", p=128), XN[:, :, :]).then_inc(slots_zeroed, 16)
            for dst, name in ((w1x, "w1x"), (w2x, "w2x"), (bx, "bx")):
                sp.dma_start(dst[:, :], t[name]).then_inc(mix_loaded, 16)
            for g in range(2):
                sp.dma_start(wgu1[:, g, 0:2, :], t["wgu1"][g, 0:256, :].rearrange("(c p) d -> p c d", p=128)).then_inc(ffn1_loaded, 16)
            sp.dma_start(wgu1[0:I1 - 256, :, 2, :], t["wgu1"][:, 256:I1, :].rearrange("g p d -> p g d")).then_inc(ffn1_loaded, 16)
            sp.dma_start(wd1[:, :], t["wd1"]).then_inc(ffn1_loaded, 16)
            sp.dma_start(clips[:, :], t["clips"]).then_inc(ffn1_loaded, 16)
            for dst, name in ((wqkv2[:, :, :], "wqkv2"), (bqk2[:, 0:1], "bq2"), (bqk2[:, 1:2], "bk2"), (bv2[:, :], "bv2")):
                sp.dma_start(dst, t[name]).then_inc(attn2_loaded, 16)
            for dst, name in ((rw2[:, :], "rw2"), (rb2[:, :], "rb2"), (pair_sel[:, :, :], "pair_sel")):
                sp.dma_start(dst, t[name]).then_inc(moe2_loaded, 16)
            for dst, name in ((wqkv3, "wqkv3"), (wkva3, "wkva3"), (bqkv3, "bqkv3"), (bkva3, "bkva3"), (wo3, "wo3"), (bo3, "bo3"), (g3, "g3")):
                sp.dma_start(dst[:, :], t[name]).then_inc(attn3_loaded, 16)
            for dst, name in ((f2_3[:, :, :], "f2_3"), (ctrl3[:, :], "ctrl3"), (tie3[:, :], "tie3"), (bias3[:, :], "bias3")):
                sp.dma_start(dst, t[name]).then_inc(moe3_loaded, 16)
            for e in range(4):
                load_expert(sp, e)
            sp.wait_ge(x_updated, B)
            for dst, name in ((w13_2[:, :, :, :], "w13_2"), (w2_2[:, :, :], "w2_2")):
                sp.dma_start(dst, t[name]).then_inc(moe2_loaded, 16)
            sync_moe0(sp)
            sp.wait_ge(x_updated, 6 * B)
            sp.dma_start(f1_3, t["f1_3"]).then_inc(f1_loaded, 16)
            sp.wait_ge(x_updated, 8 * B)
            sp.dma_start(t["out"], X[:, :, :]).then_inc(out_stored, 16)
            sp.wait_ge(out_stored, 16)

        @block.gpsimd
        def _(pool):
            pool.memset(minus_half[:, :], -0.5)
            pool.memset(zero[:, :], 0.0)
            pool.memset(minus_magic[:, :], -MAGIC)
            pool.memset(eps[:, :], LN_EPS).then_inc(pool_ready, 1)
            pool.memset(kT[:, :, :], 0.0).then_inc(pool_ready, 1)
            pool.wait_ge(mask_loaded, 16)
            pool.tensor_scalar(mask_bias[:, :, :], mask_u8[:, :, :], -MASKED, MASKED, ALU.mult, ALU.add).then_inc(pool_ready, 1)
            pool.memset(XN[:, :, :], 0.0).then_inc(pool_ready, 1)
            gpsimd_attn0(pool)
            pool.wait_ge(slots_zeroed, 16)
            gpsimd_moe0(pool)
            gpsimd_mix1(pool)
            gpsimd_attn2(pool)
            gpsimd_moe2(pool)
            gpsimd_attn3(pool)
            gpsimd_moe3(pool)

        @block.scalar
        def _(act):
            act.dma_start(mask_u8[:, :, :], t["mask"]).then_inc(mask_loaded, 16)
            act.wait_ge(const_loaded, 4 * 16)
            act.activation(tg[:, :], gates_in[:, :], ACT.Tanh).then_inc(tg_ready, 1)
            scalar_attn0(act)
            act.wait_ge(ffn1_loaded, 5 * 16)
            act.activation(clip_tanh[:, :], clips[:, :], ACT.Tanh, scale=0.5).then_inc(tanh_done, 1)
            act.wait_ge(attn3_loaded, 7 * 16)
            act.activation(g3_tanh[:, :], g3[:, :], ACT.Tanh, scale=0.5).then_inc(tanh_done, 1)
            scalar_moe0(act)
            scalar_mix1(act)
            scalar_ffn1(act)
            scalar_attn2(act)
            scalar_moe2(act)
            scalar_attn3(act)
            scalar_moe3(act)

        @block.vector
        def _(dve):
            vector_attn0(dve)
            vector_moe0(dve)
            vector_mix1(dve)
            vector_ffn1(dve)
            vector_attn2(dve)
            vector_moe2(dve)
            vector_attn3(dve)
            vector_moe3(dve)

        @block.tensor
        def _(pe):
            tensor_attn0(pe)
            tensor_moe0(pe)
            tensor_mix1(pe)
            tensor_ffn1(pe)
            tensor_attn2(pe)
            tensor_moe2(pe)
            tensor_attn3(pe)
            tensor_moe3(pe)


def kernel(**inputs):
    import numpy as np
    from concourse.bass_utils import run_bass_kernel_spmd

    a = {k: np.asarray(v) for k, v in inputs.items()}

    def rows(v, n):
        v = np.asarray(v)
        return np.broadcast_to(v.reshape(1, -1), (n, v.size))

    def pairs(routed, shared):
        both = np.concatenate([routed, shared])
        return both.reshape(5, 2, *both.shape[1:])

    ins = {
        "x": a["x"].transpose(1, 0, 2),
        "ctxT": a["ctx_1024"].transpose(2, 0, 1),
        "mask": a["mask_BxSxS2_bk1"].transpose(1, 0, 2),
        "ident": np.eye(128, dtype=np.float32),
        "ident_b": np.eye(128, dtype=mybir.dt.np(BF16)),
        "ones": np.ones((128, 128), np.float32),
        "gates": rows(np.concatenate([a["g_xattn"], a["g_ffn"]]), 128),
        "wq0": a["L0_xattn_wq"].transpose(1, 0, 2).reshape(128, 1024),
        "wk0": a["L0_xattn_wk"].transpose(1, 0, 2).reshape(128, 1024),
        "wv0": a["L0_xattn_wv"].transpose(1, 0, 2).reshape(128, 1024),
        "wo0": a["L0_xattn_wo"].reshape(8, 128, 128).transpose(1, 0, 2),
        "bq0": a["L0_xattn_bq"].reshape(8, 128).T,
        "bk0": a["L0_xattn_bk"].reshape(8, 128).T,
        "bv0": rows(a["L0_xattn_bv"], T).reshape(T, H0, DK0),
        "bo0": a["L0_xattn_bo"].reshape(1, 128),
        "wg0": a["L0_ffn_wg"],
        "w1x": a["L1_xattn_W"][:, :D].T,
        "w2x": a["L1_xattn_W"][:, D:].T,
        "bx": a["L1_xattn_b"].reshape(1, D),
        "wgu1": np.stack([a["L1_ffn_w_gate"], a["L1_ffn_w_up"]]),
        "wd1": a["L1_ffn_w_down"],
        "wqkv2": np.stack([a["L2_xattn_Wq"], a["L2_xattn_Wk"], a["L2_xattn_Wv"]]).transpose(1, 0, 2),
        "bq2": a["L2_xattn_bq"].reshape(D, 1),
        "bk2": a["L2_xattn_bk"].reshape(D, 1),
        "bv2": rows(a["L2_xattn_bv"], T),
        "rw2": a["L2_ffn_router_w"],
        "rb2": rows(a["L2_ffn_router_b"], 128),
        "w13_2": np.stack([pairs(a[f"L2_ffn_routed_{w}"], a[f"L2_ffn_shared_{w}"]).transpose(2, 0, 1, 3).reshape(D, 5, 128)
                           for w in ("w1", "w3")], axis=1),
        "w2_2": pairs(a["L2_ffn_routed_w2"], a["L2_ffn_shared_w2"]).reshape(5, 128, D).transpose(1, 0, 2),
        "pair_sel": np.tile(0.5 * np.kron(np.eye(E2), np.ones((1, H2))), (3, 1)).reshape(3 * E2, 4, 128).astype(mybir.dt.np(BF16)),
        "wqkv3": a["L3_xattn_Wqkv"],
        "wkva3": a["L3_xattn_Wqkv_aux"][:, D:],
        "bqkv3": rows(a["L3_xattn_bqkv"], 128),
        "bkva3": rows(a["L3_xattn_bqkv_aux"][D:], T),
        "wo3": a["L3_xattn_Wo"],
        "bo3": a["L3_xattn_bo"].reshape(1, D),
        "g3": rows(a["L3_xattn_g"], 128),
        "f1_3": a["L3_ffn_f1"].reshape(D, ES3, F3),
        "f2_3": a["L3_ffn_f2"].transpose(1, 2, 0, 3).reshape(SETS3 * F3, E3, D),
        "ctrl3": a["L3_ffn_controller"].reshape(D, ES3),
        "tie3": rows(np.linspace(0.0, 1e-06, G3, dtype=np.float32), 128),
        "bias3": a["L3_ffn_bias"].transpose(1, 2, 0).reshape(SETS3 * F3, E3),
        "clips": rows(np.concatenate([a["L1_ffn_clip_x"], a["L1_ffn_clip_down"]]), 128),
        "rank_w": rows(np.arange(E0, 0, -1, dtype=np.float32), 128),
        "slot_base": rows(np.arange(E0, dtype=np.float32) * C0 - 1, 128),
        "spare_slot": NT + np.arange(NT, dtype=np.float32).reshape(B, 128).T,
        "tri_b": np.triu(np.ones((128, 128))).astype(mybir.dt.np(BF16)),
        "ones_b": np.ones((128, 128)).astype(mybir.dt.np(BF16)),
        "w1_0": a["L0_ffn_w1"],
        "w2_0": a["L0_ffn_w2"],
        "b1_0": a["L0_ffn_b1"].reshape(E0, FC0, 128).transpose(0, 2, 1),
        "b2_0": a["L0_ffn_b2"].reshape(E0, 1, D),
    }
    ins = {k: np.ascontiguousarray(v) for k, v in ins.items()}
    nc = bacc.Bacc("TRN2", target_bir_lowering=False, num_devices=1)
    t = {k: nc.dram_tensor(f"in_{k}", v.shape, mybir.dt.from_np(v.dtype), kind="ExternalInput").ap() for k, v in ins.items()}
    t["out"] = nc.dram_tensor("out", (S, B, D), F32, kind="ExternalOutput").ap()
    t["x_slots"] = nc.dram_tensor("x_slots", (2 * NT, D), F32, kind="Internal").ap()
    t["y_slots"] = nc.dram_tensor("y_slots", (NT, D), F32, kind="Internal").ap()
    build(nc, t)
    r = run_bass_kernel_spmd(nc, [{f"in_{k}": v for k, v in ins.items()}], core_ids=[0])
    return np.ascontiguousarray(r.results[0]["out"].transpose(1, 0, 2))
```
